# Optimizing a Trainium2 kernel written in Bass

```python
import numpy as np
import jax
import jax.numpy as jnp

def _softmax(x, axis=-1):
    return jax.nn.softmax(x, axis=axis)

def _gelu(x):
    return jax.nn.gelu(x, approximate=True)

def _silu(x):
    return jax.nn.silu(x)

def _sigmoid(x):
    return jax.nn.sigmoid(x)

def _layernorm(x, axis=-1, eps=1e-05):
    m = jnp.mean(x, axis=axis, keepdims=True)
    v = jnp.var(x, axis=axis, keepdims=True)
    return (x - m) / jnp.sqrt(v + eps)

def _scatter_add(tgt, idx, src, axis=0):
    return tgt.at[idx].add(src)

def _segment_sum(src, seg, n):
    return jax.ops.segment_sum(src, seg, n)
kernel_name = 'mk_flamingo_gated_d2_seqx_r8_e6e70f'

def setup_inputs(seed: int=0):
    np.random.seed(seed)
    _w = jnp.asarray

    def _rec_inputs():
        import jax
        import jax.numpy as jnp
        _rk = jax.random.key(seed)
        x = 0.0003765 + 1 * jax.random.normal(jax.random.fold_in(_rk, 1), (8, 128, 256), jnp.float32)
        _lenS = 128 - jax.random.randint(jax.random.fold_in(_rk, 7), (8,), 0, max(1, 128 // 4) + 1, jnp.int32)
        _lenS2 = 128 - jax.random.randint(jax.random.fold_in(_rk, 8), (8,), 0, max(1, 128 // 4) + 1, jnp.int32)
        _ctx_2048P = jax.random.normal(jax.random.fold_in(_rk, 11), (8, 16, 256), jnp.float32)
        _ctx_2048c = jax.random.dirichlet(jax.random.fold_in(_rk, 511), 0.3 * jnp.ones((16,), jnp.float32), (8, 128))
        _ctx_2048t = jnp.einsum('bsk,bkd->bsd', _ctx_2048c, _ctx_2048P)
        _ctx_2048t = _ctx_2048t * jax.lax.rsqrt(jnp.mean(jnp.square(_ctx_2048t)) + 1e-12) * 0.953939
        ctx_2048 = -0.000292821 + 1.00034 * (_ctx_2048t + 0.3 * jax.random.normal(jax.random.fold_in(_rk, 611), (8, 128, 256), jnp.float32))
        _g = jax.random.normal(jax.random.fold_in(_rk, 9001), (2, 2), jnp.float32)
        _g = jnp.sign(_g) * jnp.maximum(jnp.abs(_g), 1.0) + (_g == 0) * 1.0
        g_xattn = _g[0]
        g_ffn = _g[1]
        return (x, ctx_2048, g_xattn, g_ffn)
    x, ctx_2048, g_xattn, g_ffn = _rec_inputs()

    def _L0_xattn_setup():
        import jax, jax.numpy as jnp
        import numpy as np
        key = jax.random.key(seed)
        k1, k2, k3, k4, k5 = jax.random.split(key, 5)
        B, D_MODEL, L = (2, 128, 256)
        HEAD_DIM = 8
        H = D_MODEL // HEAD_DIM
        return {'k': jax.random.normal(k1, (B, D_MODEL, L), dtype=jnp.float32), 'v': jax.random.normal(k2, (B, D_MODEL, L), dtype=jnp.float32), 'q': jax.random.normal(k3, (B, D_MODEL, L), dtype=jnp.float32), 'ssm_kernel': jax.random.normal(k4, (H, L), dtype=jnp.float32), 'D': jax.random.normal(k5, (H,), dtype=jnp.float32), 'head_dim': HEAD_DIM}
    _L0_xattn_all = _L0_xattn_setup()
    _L0_xattn_in = {k: v for k, v in _L0_xattn_all.items() if k in ('ssm_kernel', 'D')}
    del _L0_xattn_all

    def _L0_ffn_setup():
        import jax, jax.numpy as jnp
        import numpy as np
        HID = 256
        N_HEADS = 16
        N_KV = 16
        HEAD_DIM = HID // N_HEADS
        N_EXP = 8
        TOP_K = 2
        MOE_I = 176
        SH_I = 704
        EPS = 1e-06
        ROPE_THETA = 1000000.0

        def _rms(x, w):
            v = jnp.mean(jnp.square(x), axis=-1, keepdims=True)
            return x * jax.lax.rsqrt(v + EPS) * w

        def _rope(q, k):
            S, D = (q.shape[1], q.shape[-1])
            inv = 1.0 / ROPE_THETA ** (jnp.arange(0, D, 2, dtype=jnp.float32) / D)
            freqs = jnp.arange(S, dtype=jnp.float32)[:, None] * inv[None, :]
            emb = jnp.concatenate([freqs, freqs], axis=-1)
            cos = jnp.cos(emb)[None, :, None, :]
            sin = jnp.sin(emb)[None, :, None, :]

            def rot(t):
                t1, t2 = (t[..., :D // 2], t[..., D // 2:])
                return jnp.concatenate([-t2, t1], axis=-1)
            return (q * cos + rot(q) * sin, k * cos + rot(k) * sin)
        key = jax.random.key(seed)
        ks = jax.random.split(key, 20)
        s = 0.02
        d = {'x': jax.random.normal(ks[0], (2, 128, HID), jnp.float32), 'w_ln1': jnp.ones((HID,), jnp.float32), 'wq': jax.random.normal(ks[1], (HID, N_HEADS * HEAD_DIM), jnp.float32) * s, 'bq': jnp.zeros((N_HEADS * HEAD_DIM,), jnp.float32), 'wk': jax.random.normal(ks[2], (HID, N_KV * HEAD_DIM), jnp.float32) * s, 'bk': jnp.zeros((N_KV * HEAD_DIM,), jnp.float32), 'wv': jax.random.normal(ks[3], (HID, N_KV * HEAD_DIM), jnp.float32) * s, 'bv': jnp.zeros((N_KV * HEAD_DIM,), jnp.float32), 'wo': jax.random.normal(ks[4], (N_HEADS * HEAD_DIM, HID), jnp.float32) * s, 'w_ln2': jnp.ones((HID,), jnp.float32), 'w_router': jax.random.normal(ks[5], (HID, N_EXP), jnp.float32) * s, 'w_gate_e': jax.random.normal(ks[6], (N_EXP, HID, MOE_I), jnp.float32) * s, 'w_up_e': jax.random.normal(ks[7], (N_EXP, HID, MOE_I), jnp.float32) * s, 'w_down_e': jax.random.normal(ks[8], (N_EXP, MOE_I, HID), jnp.float32) * s, 'w_sh_gate': jax.random.normal(ks[9], (HID, SH_I), jnp.float32) * s, 'w_sh_up': jax.random.normal(ks[10], (HID, SH_I), jnp.float32) * s, 'w_sh_down': jax.random.normal(ks[11], (SH_I, HID), jnp.float32) * s, 'w_sh_eg': jax.random.normal(ks[12], (HID, 1), jnp.float32) * s}
        return d
    _L0_ffn_all = _L0_ffn_setup()
    _L0_ffn_in = {k: v for k, v in _L0_ffn_all.items() if k in ('w_ln1', 'wq', 'bq', 'wk', 'bk', 'wv', 'bv', 'wo', 'w_ln2', 'w_router', 'w_gate_e', 'w_up_e', 'w_down_e', 'w_sh_gate', 'w_sh_up', 'w_sh_down', 'w_sh_eg')}
    del _L0_ffn_all

    def _L1_xattn_setup():
        import jax, jax.numpy as jnp
        import numpy as np
        D_MODEL = 256
        NUM_HEADS = 16
        HEAD_DIM = D_MODEL // NUM_HEADS

        def _fq_sym(x, axis):
            s = jnp.max(jnp.abs(x), axis=axis, keepdims=True) / 127.0
            s = jnp.maximum(s, 1e-08)
            q = jnp.clip(jnp.round(x / s), -127.0, 127.0) * s
            return x + jax.lax.stop_gradient(q - x)

        def _fq_unsigned(x, axis):
            s = jnp.max(x, axis=axis, keepdims=True) / 255.0
            s = jnp.maximum(s, 1e-08)
            q = jnp.clip(jnp.round(x / s), 0.0, 255.0) * s
            return x + jax.lax.stop_gradient(q - x)
        key = jax.random.key(seed)
        ks = jax.random.split(key, 8)
        B, N, M, C = (2, 256, 64, D_MODEL)
        return {'x': jax.random.normal(ks[0], (B, N, C), jnp.float32), 'cond': jax.random.normal(ks[1], (B, M, C), jnp.float32), 'Wq': jax.random.normal(ks[2], (C, C), jnp.float32) * 0.02, 'bq': jnp.zeros((C,), jnp.float32), 'Wkv': jax.random.normal(ks[3], (C, 2 * C), jnp.float32) * 0.02, 'bkv': jnp.zeros((2 * C,), jnp.float32), 'Wp': jax.random.normal(ks[4], (C, C), jnp.float32) * 0.02, 'bp': jnp.zeros((C,), jnp.float32)}
    _L1_xattn_all = _L1_xattn_setup()
    _L1_xattn_in = {k: v for k, v in _L1_xattn_all.items() if k in ('Wq', 'bq', 'Wkv', 'bkv', 'Wp', 'bp')}
    del _L1_xattn_all

    def _L1_ffn_setup():
        import jax, jax.numpy as jnp
        import numpy as np
        TOPK = 2
        HID, INTER, E, SHARED_INTER = (256, 176, 14, 352)
        key = jax.random.key(seed)
        ks = jax.random.split(key, 11)
        s = 0.02
        return {'x': jax.random.normal(ks[0], (4, 64, HID), jnp.float32), 'gate_w': jax.random.normal(ks[1], (E, HID), jnp.float32) * s, 'cls_w': jax.random.normal(ks[2], (E, HID), jnp.float32) * s, 'extra_scale': jax.random.normal(ks[3], (E,), jnp.float32) * 0.1, 'extra_bias': jax.random.normal(ks[4], (E,), jnp.float32) * 0.01, 'wg': jax.random.normal(ks[5], (E, INTER, HID), jnp.float32) * s, 'wu': jax.random.normal(ks[6], (E, INTER, HID), jnp.float32) * s, 'wd': jax.random.normal(ks[7], (E, HID, INTER), jnp.float32) * s, 'sg': jax.random.normal(ks[8], (SHARED_INTER, HID), jnp.float32) * s, 'su': jax.random.normal(ks[9], (SHARED_INTER, HID), jnp.float32) * s, 'sd': jax.random.normal(ks[10], (HID, SHARED_INTER), jnp.float32) * s}
    _L1_ffn_all = _L1_ffn_setup()
    _L1_ffn_in = {k: v for k, v in _L1_ffn_all.items() if k in ('gate_w', 'cls_w', 'extra_scale', 'extra_bias', 'wg', 'wu', 'wd', 'sg', 'su', 'sd')}
    del _L1_ffn_all
    return {'x': x, 'ctx_2048': ctx_2048, 'g_xattn': g_xattn, 'g_ffn': g_ffn, 'L0_xattn_ssm_kernel': _L0_xattn_in['ssm_kernel'], 'L0_xattn_D': _L0_xattn_in['D'], 'L0_ffn_w_ln1': _L0_ffn_in['w_ln1'], 'L0_ffn_wq': _L0_ffn_in['wq'], 'L0_ffn_bq': _L0_ffn_in['bq'], 'L0_ffn_wk': _L0_ffn_in['wk'], 'L0_ffn_bk': _L0_ffn_in['bk'], 'L0_ffn_wv': _L0_ffn_in['wv'], 'L0_ffn_bv': _L0_ffn_in['bv'], 'L0_ffn_wo': _L0_ffn_in['wo'], 'L0_ffn_w_ln2': _L0_ffn_in['w_ln2'], 'L0_ffn_w_router': _L0_ffn_in['w_router'], 'L0_ffn_w_gate_e': _L0_ffn_in['w_gate_e'], 'L0_ffn_w_up_e': _L0_ffn_in['w_up_e'], 'L0_ffn_w_down_e': _L0_ffn_in['w_down_e'], 'L0_ffn_w_sh_gate': _L0_ffn_in['w_sh_gate'], 'L0_ffn_w_sh_up': _L0_ffn_in['w_sh_up'], 'L0_ffn_w_sh_down': _L0_ffn_in['w_sh_down'], 'L0_ffn_w_sh_eg': _L0_ffn_in['w_sh_eg'], 'L1_xattn_Wq': _L1_xattn_in['Wq'], 'L1_xattn_bq': _L1_xattn_in['bq'], 'L1_xattn_Wkv': _L1_xattn_in['Wkv'], 'L1_xattn_bkv': _L1_xattn_in['bkv'], 'L1_xattn_Wp': _L1_xattn_in['Wp'], 'L1_xattn_bp': _L1_xattn_in['bp'], 'L1_ffn_gate_w': _L1_ffn_in['gate_w'], 'L1_ffn_cls_w': _L1_ffn_in['cls_w'], 'L1_ffn_extra_scale': _L1_ffn_in['extra_scale'], 'L1_ffn_extra_bias': _L1_ffn_in['extra_bias'], 'L1_ffn_wg': _L1_ffn_in['wg'], 'L1_ffn_wu': _L1_ffn_in['wu'], 'L1_ffn_wd': _L1_ffn_in['wd'], 'L1_ffn_sg': _L1_ffn_in['sg'], 'L1_ffn_su': _L1_ffn_in['su'], 'L1_ffn_sd': _L1_ffn_in['sd']}

def reference(x, ctx_2048, g_xattn, g_ffn, L0_xattn_ssm_kernel, L0_xattn_D, L0_ffn_w_ln1, L0_ffn_wq, L0_ffn_bq, L0_ffn_wk, L0_ffn_bk, L0_ffn_wv, L0_ffn_bv, L0_ffn_wo, L0_ffn_w_ln2, L0_ffn_w_router, L0_ffn_w_gate_e, L0_ffn_w_up_e, L0_ffn_w_down_e, L0_ffn_w_sh_gate, L0_ffn_w_sh_up, L0_ffn_w_sh_down, L0_ffn_w_sh_eg, L1_xattn_Wq, L1_xattn_bq, L1_xattn_Wkv, L1_xattn_bkv, L1_xattn_Wp, L1_xattn_bp, L1_ffn_gate_w, L1_ffn_cls_w, L1_ffn_extra_scale, L1_ffn_extra_bias, L1_ffn_wg, L1_ffn_wu, L1_ffn_wd, L1_ffn_sg, L1_ffn_su, L1_ffn_sd):
    import jax
    import jax.numpy as jnp

    def _L0_xattn_ref(k, v, q, ssm_kernel, D, head_dim):
        import jax, jax.numpy as jnp
        import numpy as np
        B, HD, L = k.shape
        H = HD // head_dim
        fft_size = 2 * L
        k_ = k.reshape(B, H, head_dim, L)
        v_ = v.reshape(B, H, head_dim, L)
        q_ = q.reshape(B, H, head_dim, L)
        kv = jnp.einsum('bhil,bhjl->bijhl', k_, v_)
        kv_f = jnp.fft.rfft(kv, n=fft_size)
        kernel_f = jnp.fft.rfft(ssm_kernel, n=fft_size)
        y = jnp.fft.irfft(kv_f * kernel_f, n=fft_size)[..., :L]
        out = y + kv * D[None, None, None, :, None]
        out = jnp.einsum('bijhl,bhil->bjhl', out, q_)
        out = jnp.transpose(out, (0, 2, 1, 3)).reshape(B, H * head_dim, L)
        return out.astype(k.dtype)

    def _L0_ffn_ref(x, w_ln1, wq, bq, wk, bk, wv, bv, wo, w_ln2, w_router, w_gate_e, w_up_e, w_down_e, w_sh_gate, w_sh_up, w_sh_down, w_sh_eg):
        import jax, jax.numpy as jnp
        import numpy as np
        HID = 256
        N_HEADS = 16
        N_KV = 16
        HEAD_DIM = HID // N_HEADS
        N_EXP = 8
        TOP_K = 2
        MOE_I = 176
        SH_I = 704
        EPS = 1e-06
        ROPE_THETA = 1000000.0

        def _rms(x, w):
            v = jnp.mean(jnp.square(x), axis=-1, keepdims=True)
            return x * jax.lax.rsqrt(v + EPS) * w

        def _rope(q, k):
            S, D = (q.shape[1], q.shape[-1])
            inv = 1.0 / ROPE_THETA ** (jnp.arange(0, D, 2, dtype=jnp.float32) / D)
            freqs = jnp.arange(S, dtype=jnp.float32)[:, None] * inv[None, :]
            emb = jnp.concatenate([freqs, freqs], axis=-1)
            cos = jnp.cos(emb)[None, :, None, :]
            sin = jnp.sin(emb)[None, :, None, :]

            def rot(t):
                t1, t2 = (t[..., :D // 2], t[..., D // 2:])
                return jnp.concatenate([-t2, t1], axis=-1)
            return (q * cos + rot(q) * sin, k * cos + rot(k) * sin)
        B, S, H = x.shape
        h = _rms(x, w_ln1)
        q = (h @ wq + bq).reshape(B, S, N_HEADS, HEAD_DIM)
        k = (h @ wk + bk).reshape(B, S, N_KV, HEAD_DIM)
        v = (h @ wv + bv).reshape(B, S, N_KV, HEAD_DIM)
        q, k = _rope(q, k)
        rep = N_HEADS // N_KV
        if rep > 1:
            k = jnp.repeat(k, rep, axis=2)
            v = jnp.repeat(v, rep, axis=2)
        scores = jnp.einsum('bqhd,bkhd->bhqk', q, k) * HEAD_DIM ** (-0.5)
        causal = jnp.tril(jnp.ones((S, S), bool))
        scores = jnp.where(causal[None, None], scores, jnp.finfo(scores.dtype).min)
        attn = jax.nn.softmax(scores, axis=-1)
        ctx = jnp.einsum('bhqk,bkhd->bqhd', attn, v).reshape(B, S, N_HEADS * HEAD_DIM)
        x = x + ctx @ wo
        h = _rms(x, w_ln2).reshape(B * S, H)
        logits = h @ w_router
        probs = jax.nn.softmax(logits, axis=-1)
        top_w, top_i = jax.lax.top_k(probs, TOP_K)
        combine = jnp.sum(jax.nn.one_hot(top_i, N_EXP, dtype=h.dtype) * top_w[..., None], axis=1)
        g = jnp.einsum('th,ehi->eti', h, w_gate_e)
        u = jnp.einsum('th,ehi->eti', h, w_up_e)
        y = jnp.einsum('eti,eih->eth', jax.nn.silu(g) * u, w_down_e)
        routed = jnp.einsum('eth,te->th', y, combine)
        sh = jax.nn.silu(h @ w_sh_gate) * (h @ w_sh_up) @ w_sh_down
        sh = sh * jax.nn.sigmoid(h @ w_sh_eg)
        x = x + (routed + sh).reshape(B, S, H)
        return x

    def _L1_xattn_ref(x, cond, Wq, bq, Wkv, bkv, Wp, bp):
        import jax, jax.numpy as jnp
        import numpy as np
        D_MODEL = 256
        NUM_HEADS = 16
        HEAD_DIM = D_MODEL // NUM_HEADS

        def _fq_sym(x, axis):
            s = jnp.max(jnp.abs(x), axis=axis, keepdims=True) / 127.0
            s = jnp.maximum(s, 1e-08)
            q = jnp.clip(jnp.round(x / s), -127.0, 127.0) * s
            return x + jax.lax.stop_gradient(q - x)

        def _fq_unsigned(x, axis):
            s = jnp.max(x, axis=axis, keepdims=True) / 255.0
            s = jnp.maximum(s, 1e-08)
            q = jnp.clip(jnp.round(x / s), 0.0, 255.0) * s
            return x + jax.lax.stop_gradient(q - x)
        B, N, C = x.shape
        H, hd = (NUM_HEADS, HEAD_DIM)
        q = (x @ Wq + bq).reshape(1, B * N, H, hd)
        kv = (cond @ Wkv + bkv).reshape(1, -1, 2, H, hd)
        k, v = (kv[:, :, 0], kv[:, :, 1])
        scale = 1.0 / np.sqrt(hd).astype(np.float32)
        q = jnp.transpose(q * scale, (0, 2, 1, 3))
        k = jnp.transpose(k, (0, 2, 1, 3))
        v = jnp.transpose(v, (0, 2, 1, 3))
        q = _fq_sym(q, axis=-1)
        k = _fq_sym(k, axis=-1)
        v = _fq_sym(v, axis=2)
        attn = jnp.einsum('bhqd,bhkd->bhqk', q, k)
        attn = jax.nn.softmax(attn.astype(jnp.float32), axis=-1)
        attn = _fq_unsigned(attn, axis=-1)
        out = jnp.einsum('bhqk,bhkd->bhqd', attn, v)
        out = jnp.transpose(out, (0, 2, 1, 3)).reshape(B, N, C)
        return out @ Wp + bp

    def _L1_ffn_ref(x, gate_w, cls_w, extra_scale, extra_bias, wg, wu, wd, sg, su, sd):
        import jax, jax.numpy as jnp
        import numpy as np
        TOPK = 2
        HID, INTER, E, SHARED_INTER = (256, 176, 14, 352)
        shape = x.shape
        d = shape[-1]
        xf = x.reshape(-1, d)
        T = xf.shape[0]
        n_exp = gate_w.shape[0]
        logits = xf @ cls_w.T * jax.nn.silu(xf @ gate_w.T)
        scores = jax.nn.softmax(jnp.abs(logits).astype(jnp.float32), axis=-1)
        biased = scores + extra_bias[None, :]
        _, idx = jax.lax.top_k(biased, TOPK)
        orig = 1.0 + scores * extra_scale[None, :]
        w = jnp.take_along_axis(orig, idx, axis=1).astype(x.dtype)
        combine = jnp.zeros((T, n_exp), x.dtype).at[jnp.arange(T)[:, None], idx].add(w)
        g = jax.nn.silu(jnp.einsum('td,efd->etf', xf, wg))
        u = jnp.einsum('td,efd->etf', xf, wu)
        o = jnp.einsum('etf,edf->etd', g * u, wd)
        y = jnp.einsum('etd,te->td', o, combine)
        z = jax.nn.silu(xf @ sg.T) * (xf @ su.T) @ sd.T
        return (y + z).reshape(shape)
    x = x + jnp.tanh(g_xattn[0]) * _L0_xattn_ref(ctx_2048, ctx_2048, _layernorm(x, axis=-1), L0_xattn_ssm_kernel, L0_xattn_D, 8)
    x = x + jnp.tanh(g_ffn[0]) * _L0_ffn_ref(_layernorm(x, axis=-1), L0_ffn_w_ln1, L0_ffn_wq, L0_ffn_bq, L0_ffn_wk, L0_ffn_bk, L0_ffn_wv, L0_ffn_bv, L0_ffn_wo, L0_ffn_w_ln2, L0_ffn_w_router, L0_ffn_w_gate_e, L0_ffn_w_up_e, L0_ffn_w_down_e, L0_ffn_w_sh_gate, L0_ffn_w_sh_up, L0_ffn_w_sh_down, L0_ffn_w_sh_eg)
    x = x + jnp.tanh(g_xattn[1]) * _L1_xattn_ref(_layernorm(x, axis=-1), ctx_2048, L1_xattn_Wq, L1_xattn_bq, L1_xattn_Wkv, L1_xattn_bkv, L1_xattn_Wp, L1_xattn_bp)
    x = x + jnp.tanh(g_ffn[1]) * _L1_ffn_ref(_layernorm(x, axis=-1), L1_ffn_gate_w, L1_ffn_cls_w, L1_ffn_extra_scale, L1_ffn_extra_bias, L1_ffn_wg, L1_ffn_wu, L1_ffn_wd, L1_ffn_sg, L1_ffn_su, L1_ffn_sd)
    return x

_drawn_inputs = setup_inputs


def setup_inputs(seed=0):
    import zlib

    import numpy as np

    out = dict(_drawn_inputs(seed))
    spreads = {'g_ffn': (-1.0, 0.6),
     'L0_ffn_w_ln1': (1.0, 0.6),
     'L0_ffn_bq': (0.0, 0.8),
     'L0_ffn_bk': (0.0, 0.8),
     'L0_ffn_bv': (0.0, 0.8),
     'L0_ffn_w_ln2': (1.0, 0.6),
     'L1_xattn_bq': (0.0, 0.8),
     'L1_xattn_bkv': (0.0, 0.8),
     'L1_xattn_bp': (0.0, 0.8)}
    factors = {'L0_ffn_wq': 8.0,
     'L0_ffn_wk': 8.0,
     'L0_ffn_wv': 8.0,
     'L0_ffn_wo': 8.0,
     'L0_ffn_w_router': 8.0,
     'L0_ffn_w_gate_e': 8.0,
     'L0_ffn_w_up_e': 8.0,
     'L0_ffn_w_down_e': 8.0,
     'L0_ffn_w_sh_gate': 8.0,
     'L0_ffn_w_sh_up': 8.0,
     'L0_ffn_w_sh_down': 8.0,
     'L0_ffn_w_sh_eg': 8.0,
     'L1_xattn_Wq': 8.0,
     'L1_xattn_Wkv': 8.0,
     'L1_xattn_Wp': 8.0,
     'L1_ffn_gate_w': 8.0,
     'L1_ffn_cls_w': 8.0,
     'L1_ffn_extra_scale': 8.0,
     'L1_ffn_extra_bias': 8.0,
     'L1_ffn_wg': 8.0,
     'L1_ffn_wu': 8.0,
     'L1_ffn_wd': 8.0,
     'L1_ffn_sg': 8.0,
     'L1_ffn_su': 8.0,
     'L1_ffn_sd': 8.0}
    for name, (base, spread) in spreads.items():
        noise = np.random.default_rng([zlib.crc32(name.encode()), seed]).standard_normal(out[name].shape)
        drawn = base * np.exp(spread * noise) if base else spread * noise
        out[name] = jnp.asarray(drawn.astype(out[name].dtype))
    for name, factor in factors.items():
        out[name] = (out[name] * factor).astype(out[name].dtype)
    return out
```

```python
from contextlib import ExitStack

import numpy as np

import concourse.bass as bass
from concourse import mybir

ALU = mybir.AluOpType
ACT = mybir.ActivationFunctionType
AX = mybir.AxisListType
F32 = mybir.dt.float32
BF16 = mybir.dt.bfloat16
I16 = mybir.dt.int16
U32 = mybir.dt.uint32

P = 128
B, S, D = 8, 128, 256
N = B * S
KB = D // P
H = 16
HD = D // H
CH = S // H
LN_EPS, RMS_EPS = 1e-5, 1e-6
SCALE = 1.0 / np.sqrt(HD)
ROUND = 1.5 * 2.0 ** 23
QMAX = 127.0
LN255 = float(np.log(255.0))
PARTS = 3
PAIRS = 6
F = 176
E0, E1 = 8, 14
SH0, SH1 = 704, 352
HALF = 512


def tiles_of(experts, shared):
    return -(-(experts * F + shared) // P)


FT0, FT1 = tiles_of(E0, SH0), tiles_of(E1, SH1)

ROWS = {}
for _name, _n in (("bqk", 2 * D), ("bv", D), ("bq1", D), ("bk1", D), ("bp", D), ("escale", E1),
                  ("ebias", E1), ("conv_d", H), ("gates", 4)):
    ROWS[_name] = (sum(n for _, n in ROWS.values()), _n)
NROWS = sum(n for _, n in ROWS.values())


class Chain:

    def __init__(self, eng, sem):
        self.eng, self.sem, self.count, self.links = eng, sem, 0, 0

    def link(self, ins):
        self.tick(ins)
        self.eng.wait_ge(self.sem, self.count)

    def tick(self, ins):
        ins.then_inc(self.sem, 1)
        self.count = self.count + 1
        self.links += 1

    def rest(self):
        self.eng.wait_ge(self.sem, self.count)

    def enter(self, trip, per):
        self.start, self.per, self.at = self.count, per, self.links
        self.count = self.start + trip * per

    def leave(self, trips):
        assert self.links - self.at == self.per, (self.links - self.at, self.per)
        self.count = self.start + trips * self.per


def build(nc, a, out):
    ctx = ExitStack()
    with ctx:
        def sb(name, shape, dt=F32):
            return ctx.enter_context(nc.sbuf_tensor(name, shape, dt))

        def sem(name):
            return ctx.enter_context(nc.semaphore(name))

        psum = ctx.enter_context(nc.psum_tensor("psum", [P, 8, 512], F32))

        def bank(n):
            return psum[:, n, :]

        def bank16(n):
            return psum[:, n, :].bitcast(BF16)

        consts = sb("consts", [P, 2 * P + 2 * HD + HD + 8])
        identb = sb("identb", [P, P], BF16)
        causal = sb("causal", [P, 4, P], BF16)
        zerob = sb("zerob", [1, 512], BF16)
        sel0 = sb("sel0", [P, FT0 * P], BF16)
        sel1 = sb("sel1", [P, FT1 * P], BF16)
        rows = sb("rows", [P, NROWS])
        cols = sb("cols", [P, 3, KB])
        tgate = sb("tgate", [P, 4])
        ident = consts[:, 0:P]
        cosine = consts[:, P:P + HD]
        sine = consts[:, P + HD:P + 2 * HD]
        iota = consts[:, P + 2 * HD:P + 3 * HD]
        headmask = consts[:, P + 3 * HD:P + 3 * HD + 8]
        antident = consts[:, P + 3 * HD + 8:]

        def row(name):
            o, n = ROWS[name]
            return rows[:, o:o + n]

        X = sb("X", [P, B, D])
        L = sb("L", [P, B, D])
        HT = sb("HT", [P, KB, N])
        CT = sb("CT", [P, KB, N])
        stats = sb("stats", [P, B, 6])
        mv = sb("mv", [P, B, 2])
        var = sb("var", [P, B])
        rvar = sb("rvar", [P, B])
        rstd = sb("rstd", [P, B])
        rms1 = sb("rms1", [P, B])

        wqkv = sb("wqkv", [P, KB, 3 * D])
        wo = sb("wo", [P, KB, D])
        wr0 = sb("wr0", [P, KB, E0 + 1])
        wq1 = sb("wq1", [P, KB, D])
        wk1 = sb("wk1", [P, KB, D])
        wv1 = sb("wv1", [P, KB, D])
        wp1 = sb("wp1", [P, KB, D])
        wr1 = sb("wr1", [P, KB, 2 * E1])
        wm = sb("wm", [P, 2, 3 * D])

        area = sb("area", [P, 16384])

        def part(at, n, dt=F32):
            v = area[:, at:at + n]
            return v if dt == F32 else v.bitcast(dt)

        qf, qr, qd = part(0, 2048), part(2048, 2048), part(4096, 2048)
        vf = part(6144, 2048).rearrange("p (k n) -> p k n", k=KB)
        parts = part(12288, 3072, BF16).rearrange("p (t a c) -> p t a c", t=B, a=PARTS)
        kv = part(0, 2048).rearrange("p (s k n) -> p s k n", s=2, k=KB)
        prod = part(2048, 2048).rearrange("p (s k n) -> p s k n", s=2, k=KB)
        tslot = part(4096, 512).rearrange("p (s l) -> p s l", s=2)
        toep = part(8192, 4096).rearrange("p (h l) -> p h l", h=H)
        diag = part(12288, 2048).rearrange("p (h l) -> p h l", h=H)
        osum = part(14336, 2048).rearrange("p (k b c) -> p k b c", k=KB, b=B)
        Vx = part(0, B * H * (HD + 1)).rearrange("p (t h d) -> p t h d", t=B, h=H)
        kblock = part(2304, 2048).rearrange("p (k j c) -> p k j c", k=KB, j=8)
        sc = part(4352, 1024).rearrange("p (s n) -> p s n", s=2)
        pr = part(5376, 1024).rearrange("p (s n) -> p s n", s=2)
        pT = part(6400, 1024).rearrange("p (s n) -> p s n", s=2)
        QK, rope1, rope2, roped = part(7424, 512), part(7936, 512), part(8448, 512), part(8960, 512)
        U = part(10240, 2048).rearrange("p (t c) -> p t c", t=B)
        sg = part(0, 1024).rearrange("p (s n) -> p s n", s=2)
        su = part(1024, 1024).rearrange("p (s n) -> p s n", s=2)
        hid = part(2048, 1024).rearrange("p (s n) -> p s n", s=2)
        QS = area[0:PAIRS * HD, 0:8192].bitcast(BF16).rearrange("p (u c) -> p u c", c=P)
        e16 = part(8192, 1024, I16).rearrange("p (s n) -> p s n", s=2)
        pb = part(9216, 1024, BF16).rearrange("p (s n) -> p s n", s=2)
        pbT = part(10240, 1024, BF16).rearrange("p (s n) -> p s n", s=2)

        hslot = sb("hslot", [P, KB, P])
        qT = sb("qT", [P, KB, P])
        nmax = sb("nmax", [P, 4, 4])
        rden = sb("rden", [P, H])
        orow = sb("orow", [P, D])
        oT = sb("oT", [P, KB, P])
        sq = sb("sq", [P, D])
        lg = sb("lg", [P, B, 2 * E1])
        ra = sb("ra", [P, B, E1])
        rb = sb("rb", [P, B, E1])
        rc = sb("rc", [P, B, E1])
        key = sb("key", [P, B, E1])
        wgt = sb("wgt", [P, B, E1])
        one = sb("one", [P, B])
        top = sb("top", [P, B, 8])
        topi = sb("topi", [P, B, 8], U32)
        topf = sb("topf", [P, B, 2])
        comb = sb("comb", [P, B, E1 + 1])
        comb2 = sb("comb2", [P, B, E1 + 1])
        cparts = sb("cparts", [P, B, PARTS * (E1 + 1)], BF16)
        combT = sb("combT", [P, N], BF16)
        am = sb("am", [P, P])
        qs = sb("qs", [P, P])
        rqs = sb("rqs", [P, P])
        stack = sb("stack", [P, H, PAIRS * HD], BF16)
        KS = sb("KS", [PAIRS * HD, H, N], BF16)
        vam = sb("vam", [P, KB])
        vs = sb("vs", [P, KB])
        rvs = sb("rvs", [P, KB])
        vq = sb("vq", [P, KB, N], BF16)
        VI = sb("VI", [P, B, D], BF16)
        bq25 = sb("bq25", [P, D])
        bpt = sb("bpt", [P, D])
        peaks = sb("peaks", [P, 4])
        nbias = sb("nbias", [P, 4])
        SUM = sb("SUM", [P, B * H])

        ld_x, ld_ctx, ld_toep, ld_const = sem("ld_x"), sem("ld_ctx"), sem("ld_toep"), sem("ld_const")
        ld_w0, ld_w1 = sem("ld_w0"), sem("ld_w1")
        ld_wm = [sem("ld_wm0"), sem("ld_wm1")]
        tgate_ready, var_ready, rstd_ready = sem("tgate_ready"), sem("var_ready"), sem("rstd_ready")
        rows_ready, turned, cols_ready = sem("rows_ready"), sem("turned"), sem("cols_ready")
        toep_ready = sem("toep_ready")
        t_ready, kv0_ready, kv1_ready = sem("t_ready"), sem("kv0_ready"), sem("kv1_ready")
        conv_done = [sem("conv_done0"), sem("conv_done1")]
        y_used = [sem("y_used0"), sem("y_used1")]
        summed = [sem("summed0"), sem("summed1")]
        zeroed = sem("zeroed")
        oturned, x_updated = sem("oturned"), sem("x_updated")
        hs_ready, qkv_done, qkv_used = sem("hs_ready"), sem("qkv_done"), sem("qkv_used")
        roped_ready, qkT_done, qT_ready, kb_ready = sem("roped_ready"), sem("qkT_done"), sem("qT_ready"), sem("kb_ready")
        s_done, s_used, e_done = sem("s_done"), sem("s_used"), sem("e_done")
        pt_done, pt_ready, pv_done = sem("pt_done"), sem("pt_ready"), sem("pv_done")
        o_ready, oT_done, oT_ready, wo_done, u_updated = (sem("o_ready"), sem("oT_done"), sem("oT_ready"),
                                                         sem("wo_done"), sem("u_updated"))
        ms_ready = sem("ms_ready")
        router_done, router_exp, router_in = sem("router_done"), sem("router_exp"), sem("router_in")
        comb_ready, combT_done, combT_ready = sem("comb_ready"), sem("combT_done"), sem("combT_ready")
        gate_done, up_done, c_done = sem("gate_done"), sem("up_done"), sem("c_done")
        silu_done, su_done, hid_ready, down_done = sem("silu_done"), sem("su_done"), sem("hid_ready"), sem("down_done")
        moe_used = sem("moe_used")
        proj_done, proj_used = sem("proj_done"), sem("proj_used")
        vproj_done, vf_ready, vq_ready, vT_done, vi_ready = (sem("vproj_done"), sem("vf_ready"), sem("vq_ready"),
                                                            sem("vT_done"), sem("vi_ready"))
        hi_in, part_ready, dq_ready = sem("hi_in"), sem("part_ready"), sem("dq_ready")
        stack_dve, stack_act, stack_turned, side_ready = (sem("stack_dve"), sem("stack_act"), sem("stack_turned"),
                                                          sem("side_ready"))
        l_done, nb_ready, x_done, p_ready = sem("l_done"), sem("nb_ready"), sem("x_done"), sem("p_ready")
        xt_done, xt_act, xt_dve, xv_done = sem("xt_done"), sem("xt_act"), sem("xt_dve"), sem("xv_done")
        xo_ready, xoT_done, xoT_ready, xp_done, xx_updated = (sem("xo_ready"), sem("xoT_done"), sem("xoT_ready"),
                                                             sem("xp_done"), sem("xx_updated"))
        peak_found = sem("peak_found")
        dve_step, rope_mid = sem("dve_step"), sem("rope_mid")
        stored = sem("stored")

        block = ctx.enter_context(nc.Block())

        ON_ACT = [h for h in range(H) if h % 8 in (0, 2, 3, 5, 7)]
        ON_DVE = [h for h in range(H) if h not in ON_ACT]
        MAIN0, MAIN1 = (FT0 - 1) // 2, (FT1 - 1) // 2

        def bc(ap, n, at):
            dims = [list(d) for d in ap.ap]
            dims.insert(at + 1, [0, n])
            return bass.AP(ap.tensor, ap.offset, dims)

        def copied_out(eng, t, h):
            if h < 0:
                if isinstance(t, int) and t == 0:
                    return
                t, h = t - 1, h + H
            if h in ON_ACT:
                eng.wait_ge(xt_act, t * len(ON_ACT) + (ON_ACT.index(h) + 1))
            else:
                eng.wait_ge(xt_dve, t * len(ON_DVE) + (ON_DVE.index(h) + 1))

        @block.sync
        def _(sp):
            sp.dma_start(X[:, :, :], a["x"].rearrange("b s d -> s b d")).then_inc(ld_x, 16)
            sp.dma_start(CT[:, :, :], a["ctxT"].rearrange("(k p) n -> p k n", p=P)).then_inc(ld_ctx, 16)
            for h in range(H):
                sp.dma_start(toep[:, h, :],
                             bass.AP(a["conv"].tensor, h * 2 * D + D - (P - 1), [[1, P], [1, D]])).then_inc(ld_toep, 16)
            for w, name in ((wqkv, "wqkv"), (wo, "wo"), (wr0, "wr0")):
                sp.dma_start(w[:, :, :], a[name].rearrange("(k p) n -> p k n", p=P)).then_inc(ld_w0, 16)
            for w, name in ((wq1, "wq1"), (wk1, "wk1"), (wv1, "wv1"), (wp1, "wp1"), (wr1, "wr1")):
                sp.dma_start(w[:, :, :], a[name].rearrange("(k p) n -> p k n", p=P)).then_inc(ld_w1, 16)

            def experts(src, nft, first_step):
                def load(ft, slot):
                    sp.dma_start(wm[:, slot, :], src[ft, :, :]).then_inc(ld_wm[slot], 16)
                for slot in range(2):
                    if first_step:
                        sp.wait_ge(down_done, first_step)
                    load(slot, slot)
                pairs = (nft - 2) // 2
                with sp.Fori(0, pairs) as i:
                    for slot in range(2):
                        sp.wait_ge(down_done, i * 4 + (first_step + 2 * slot + 2))
                        sp.dma_start(wm[:, slot, :], src[bass.ds(i * 2 + (2 + slot), 1), :, :]
                                     .rearrange("a p n -> p (a n)")).then_inc(ld_wm[slot], 16)
                if nft % 2:
                    sp.wait_ge(down_done, first_step + 2 * (nft - 3) + 2)
                    load(nft - 1, 0)

            experts(a["moe0"], FT0, 0)
            experts(a["moe1"], FT1, 2 * FT0)
            for p in range(4):
                sp.wait_ge(moe_used, 4 + p + 1)
                sp.dma_start(out[2 * p:2 * p + 2].rearrange("b s d -> s b d"), X[:, 2 * p:2 * p + 2, :])\
                  .then_inc(stored, 16)
            sp.wait_ge(stored, 64)

        @block.tensor
        def _(pe):
            mm, tr = nc.tensor.matmul, nc.tensor.transpose

            def turn_rows(n, src):
                for p in range(4):
                    pe.wait_ge(rows_ready, 8 * n + 2 * p + 2)
                    if p >= 2:
                        pe.wait_ge(cols_ready, 4 * n + p - 1)
                    for t in range(2):
                        for k in range(KB):
                            last = tr(bank(p % 2)[:, (k * 2 + t) * P:(k * 2 + t + 1) * P],
                                      src[:, 2 * p + t, k * P:(k + 1) * P], ident)
                    last.then_inc(turned, 1)

            def key_value():
                pe.wait_ge(ld_ctx, 16)
                pe.wait_ge(ld_w1, 80)
                project_rows(0, CT, wk1)
                for m in range(KB):
                    for half in range(2):
                        for k in range(KB):
                            last = mm(bank(4 + 2 * m + half), wv1[:, k, m * P:(m + 1) * P],
                                      CT[:, k, half * HALF:(half + 1) * HALF], start=(k == 0), stop=(k == 1))
                last.then_inc(vproj_done, 1)
                pe.wait_ge(proj_used, 4)
                pe.wait_ge(vq_ready, 2)
                for k in range(KB):
                    for t in range(B):
                        last = tr(bank16(k)[:, t * P:(t + 1) * P], vq[:, k, t * P:(t + 1) * P], identb[:, :])
                last.then_inc(vT_done, 1)
                pe.wait_ge(vi_ready, 2)
                turn_side(0)

            def project_rows(n, src, w):
                for p in range(4):
                    for t in range(2):
                        for k in range(KB):
                            last = mm(bank(p)[:, t * D:(t + 1) * D],
                                      src[:, k, (2 * p + t) * P:(2 * p + t + 1) * P], w[:, k, :],
                                      start=(k == 0), stop=(k == 1))
                    last.then_inc(proj_done, 1)

            def turn_side(n):
                with pe.Fori(0, B) as t:
                    pe.wait_ge(stack_dve, t + (n * B + 1))
                    pe.wait_ge(stack_act, t + (n * B + 1))
                    pe.wait_ge(side_ready, t * 2 + 2 * n * B)
                    for h in range(H):
                        last = tr(bank16(h // 8)[0:PAIRS * HD, (h % 8) * P:(h % 8 + 1) * P],
                                  stack[:, h, :], identb[:, :])
                    last.then_inc(stack_turned, 1)

            def convolution():
                pe.wait_ge(cols_ready, 4)
                pe.wait_ge(side_ready, 2 * B)
                with pe.Fori(0, H // 2) as i:
                    for s in range(2):
                        pe.wait_ge(t_ready, i * 2 + (s + 1))
                        pe.wait_ge(kv0_ready, i * 2 + (s + 1))
                        pe.wait_ge(y_used[s], i)
                        mm(bank(2 * s), tslot[:, s, 0:P], kv[:, s, 0, :], start=True, stop=True)
                        mm(bank(2 * s + 1), tslot[:, s, P:D], kv[:, s, 0, :], start=True, stop=False)
                        pe.wait_ge(kv1_ready, i * 2 + (s + 1))
                        mm(bank(2 * s + 1), tslot[:, s, 0:P], kv[:, s, 1, :], start=False, stop=True)\
                            .then_inc(conv_done[s], 1)
                for s in range(2):
                    pe.wait_ge(summed[s], H // 2)
                for p in range(4):
                    for b in range(2):
                        for k in range(KB):
                            last = tr(bank(4 + p)[:, (b * KB + k) * P:(b * KB + k + 1) * P],
                                      osum[:, k, 2 * p + b, :], ident)
                    last.then_inc(oturned, 1)

            def qkv(t):
                pe.wait_ge(hs_ready, t + 1)
                pe.wait_ge(qT_ready, t)
                pe.wait_ge(kb_ready, t)
                for k in range(KB):
                    mm(bank(0), hslot[:, k, :], wqkv[:, k, 0:2 * D], start=(k == 0), stop=(k == 1))
                for k in range(KB):
                    last = mm(bank(1)[:, 0:D], hslot[:, k, :], wqkv[:, k, 2 * D:3 * D], start=(k == 0), stop=(k == 1))
                last.then_inc(qkv_done, 1)

            def turn_qk(t):
                pe.wait_ge(roped_ready, t + 1)
                for c in range(4):
                    last = tr(bank(c // 2)[:, (c % 2) * P:(c % 2 + 1) * P], roped[:, c * P:(c + 1) * P], ident)
                last.then_inc(qkT_done, 1)

            def scores(t, g):
                if g == 0:
                    pe.wait_ge(qT_ready, t + 1)
                    pe.wait_ge(kb_ready, t + 1)
                if g >= 2:
                    pe.wait_ge(s_used, t * 4 + (g - 1))
                mm(bank(2 + g % 2), identb[:, :], causal[:, :, :].rearrange("p j c -> p (j c)"),
                   start=True, stop=False)
                mm(bank(2 + g % 2), qT[:, g // 2, :],
                   kblock[:, g // 2, (g % 2) * 4:(g % 2) * 4 + 4, :].rearrange("p j c -> p (j c)"),
                   start=False, stop=True).then_inc(s_done, 1)

            def turn_probs(t, g):
                pe.wait_ge(e_done, t * 4 + (g + 1))
                if g >= 2:
                    pe.wait_ge(pt_ready, t * 4 + (g - 1))
                for j in range(4):
                    last = tr(bank(4 + g % 2)[:, j * P:(j + 1) * P], pr[:, g % 2, j * P:(j + 1) * P], ident)
                last.then_inc(pt_done, 1)

            def values(t, g):
                pe.wait_ge(pt_ready, t * 4 + (g + 1))
                if g == 0:
                    pe.wait_ge(o_ready, t)
                    pe.wait_ge(qkv_used, t * 2 + 2)
                for j in range(4):
                    h = 4 * g + j
                    last = mm(bank(6)[:, h * (HD + 1):(h + 1) * (HD + 1)], pT[:, g % 2, j * P:(j + 1) * P],
                              Vx[:, bass.ds(t, 1), h, :].rearrange("p a d -> p (a d)"), start=True, stop=True)
                last.then_inc(pv_done, 1)

            def attend(t):
                scores(t, 0)
                scores(t, 1)
                turn_probs(t, 0)
                scores(t, 2)
                turn_probs(t, 1)
                values(t, 0)
                scores(t, 3)
                turn_probs(t, 2)
                values(t, 1)
                turn_probs(t, 3)
                values(t, 2)
                values(t, 3)

            def project_out(t):
                pe.wait_ge(o_ready, t + 1)
                pe.wait_ge(u_updated, t)
                for k in range(KB):
                    last = tr(bank(7)[:, k * P:(k + 1) * P], orow[:, k * P:(k + 1) * P], ident)
                last.then_inc(oT_done, 1)
                pe.wait_ge(oT_ready, t + 1)
                for k in range(KB):
                    last = mm(bank(7)[:, D:2 * D], oT[:, k, :], wo[:, k, :], start=(k == 0), stop=(k == 1))
                last.then_inc(wo_done, 1)

            def causal_attention():
                pe.wait_ge(ld_w0, 48)
                pe.wait_ge(x_updated, 4)
                turn_rows(1, U)
                pe.wait_ge(cols_ready, 8)
                qkv(0)
                turn_qk(0)
                with pe.Fori(1, B) as t:
                    qkv(t)
                    attend(t - 1)
                    turn_qk(t)
                    project_out(t - 1)
                attend(B - 1)
                project_out(B - 1)

            def experts(layer, experts_, nft, main, w_router, n_router, sel):
                steps0 = 2 * FT0 * layer
                parts_ = PARTS * (experts_ + 1)
                turn_rows(2 + 2 * layer, L)
                pe.wait_ge(cols_ready, 4 * (3 + 2 * layer))
                for t in range(B):
                    for k in range(KB):
                        last = mm(bank(2)[:, t * n_router:(t + 1) * n_router], HT[:, k, t * P:(t + 1) * P],
                                  w_router[:, k, :], start=(k == 0), stop=(k == 1))
                last.then_inc(router_done, 1)
                pe.wait_ge(comb_ready, layer + 1)
                for t in range(B):
                    last = tr(bank16(3)[0:parts_, t * P:(t + 1) * P], cparts[:, t, 0:parts_], identb[:, :])
                last.then_inc(combT_done, 1)
                pe.wait_ge(combT_ready, layer + 1)
                for n in range(4):
                    mm(bank(n), zerob[0:1, 0:P], zerob[0:1, :], start=True, stop=False, skip_group_check=True)

                loads0 = [layer * ((FT0 + 1) // 2), layer * (FT0 // 2)]

                def hidden(ft, nth, slot, half):
                    step = ft * 2 + (steps0 + half)
                    tokens = slice(half * HALF, (half + 1) * HALF)
                    if half == 0:
                        pe.wait_ge(ld_wm[slot], (nth + (loads0[slot] + 1)) * 16)
                    pe.wait_ge(silu_done, step)
                    for k in range(KB):
                        last = mm(bank(4), wm[:, slot, k * P:(k + 1) * P], HT[:, k, tokens],
                                  start=(k == 0), stop=(k == 1))
                    last.then_inc(gate_done, 1)
                    pe.wait_ge(su_done, step)
                    for k in range(KB):
                        last = mm(bank(5), wm[:, slot, D + k * P:D + (k + 1) * P], HT[:, k, tokens],
                                  start=(k == 0), stop=(k == 1))
                    last.then_inc(up_done, 1)
                    pe.wait_ge(hid_ready, step)
                    selector = sel[:, ft * P:(ft + 1) * P] if isinstance(ft, int) else sel[:, bass.ds(ft * P, P)]
                    mm(bank(6), selector, combT[:, tokens], start=True, stop=True).then_inc(c_done, 1)

                def down(ft, slot, half):
                    step = ft * 2 + (steps0 + half)
                    pe.wait_ge(hid_ready, step + 1)
                    for t in range(4):
                        last = mm(bank(half * 2 + t // 2)[:, (t % 2) * D:(t % 2 + 1) * D],
                                  hid[:, half, t * P:(t + 1) * P], wm[:, slot, 2 * D:3 * D],
                                  start=False, stop=False, skip_group_check=True)
                    last.then_inc(down_done, 1)

                hidden(0, 0, 0, 0)
                with pe.Fori(0, main) as i:
                    ft = pe.snap(i * 2)
                    hidden(ft, i, 0, 1)
                    down(ft, 0, 0)
                    hidden(ft + 1, i, 1, 0)
                    down(ft, 0, 1)
                    hidden(ft + 1, i, 1, 1)
                    down(ft + 1, 1, 0)
                    hidden(ft + 2, i + 1, 0, 0)
                    down(ft + 1, 1, 1)
                ft = 2 * main
                hidden(ft, main, 0, 1)
                down(ft, 0, 0)
                if ft + 1 < nft:
                    hidden(ft + 1, main, 1, 0)
                down(ft, 0, 1)
                if ft + 1 < nft:
                    hidden(ft + 1, main, 1, 1)
                    down(ft + 1, 1, 0)
                    down(ft + 1, 1, 1)

            def cross_attention():
                pe.wait_ge(moe_used, 4)
                turn_rows(3, L)
                pe.wait_ge(cols_ready, 16)
                project_rows(1, HT, wq1)
                pe.wait_ge(proj_used, 8)
                turn_side(1)
                pe.wait_ge(side_ready, 4 * B)

                def logits(t, h, cond=True):
                    u = t * H + h
                    if not (isinstance(u, int) and u < 2):
                        pe.wait_ge(x_done, u - 1)
                    for c in range(2):
                        last = mm(bank(2 * (h % 2) + c), QS[:, u, :] if isinstance(u, int) else
                                  QS[:, bass.ds(u, 1), :].rearrange("p a c -> p (a c)"),
                                  KS[:, h, c * HALF:(c + 1) * HALF], start=True, stop=True)
                    last.then_inc(l_done, 1)

                def turn(t, h):
                    u = t * H + h
                    pe.wait_ge(p_ready, u + 1)
                    copied_out(pe, t, h - 2)
                    for c in range(B):
                        last = tr(bank16(4 + h % 2)[:, c * P:(c + 1) * P], pb[:, h % 2, c * P:(c + 1) * P], identb[:, :])
                    last.then_inc(xt_done, 1)

                def weigh(t, h):
                    copied_out(pe, t, h)
                    if h == 0:
                        pe.wait_ge(xo_ready, t)
                    for c in range(B):
                        last = mm(bank(6)[:, h * HD:(h + 1) * HD], pbT[:, h % 2, c * P:(c + 1) * P],
                                  VI[:, c, h * HD:(h + 1) * HD], start=(c == 0), stop=(c == B - 1))
                    last.then_inc(xv_done, 1)

                def project(t):
                    pe.wait_ge(xo_ready, t + 1)
                    pe.wait_ge(xx_updated, t)
                    for k in range(KB):
                        last = tr(bank(7)[:, k * P:(k + 1) * P], orow[:, k * P:(k + 1) * P], ident)
                    last.then_inc(xoT_done, 1)
                    pe.wait_ge(xoT_ready, t + 1)
                    for k in range(KB):
                        last = mm(bank(7)[:, D:2 * D], oT[:, k, :], wp1[:, k, :], start=(k == 0), stop=(k == 1))
                    last.then_inc(xp_done, 1)

                def tile(t, first):
                    for h in range(H):
                        logits(t, h)
                        if h >= 2:
                            turn(t, h - 2)
                        elif not first:
                            turn(t - 1, h - 2 + H)
                        if h >= 3:
                            weigh(t, h - 3)
                        elif not first:
                            weigh(t - 1, h - 3 + H)
                        if h == 3 and not first:
                            project(t - 1)

                tile(0, True)
                with pe.Fori(1, B) as t:
                    tile(t, False)
                turn(B - 1, H - 2)
                weigh(B - 1, H - 3)
                turn(B - 1, H - 1)
                weigh(B - 1, H - 2)
                weigh(B - 1, H - 1)
                project(B - 1)

            pe.wait_ge(ld_const, 112)
            key_value()
            turn_rows(0, L)
            convolution()
            causal_attention()
            pe.wait_ge(u_updated, B)
            experts(0, E0, FT0, MAIN0, wr0, E0 + 1, sel0)
            cross_attention()
            pe.wait_ge(xx_updated, B)
            experts(1, E1, FT1, MAIN1, wr1, 2 * E1, sel1)

        @block.scalar
        def _(act):
            f = nc.scalar.activation
            act.dma_start(consts[:, :], a["consts"]).then_inc(ld_const, 16)
            act.dma_start(rows[:, :], bass.AP(a["rows"].tensor, 0, [[0, P], [1, NROWS]])).then_inc(ld_const, 16)
            act.dma_start(cols[:, :, :], a["cols"]).then_inc(ld_const, 16)
            act.dma_start(identb[:, :], a["identb"]).then_inc(ld_const, 16)
            act.dma_start(causal[:, 0, :], a["causal"]).then_inc(ld_const, 16)
            act.dma_start(sel0[:, :], a["sel0"]).then_inc(ld_const, 16)
            act.dma_start(sel1[:, :], a["sel1"]).then_inc(ld_const, 16)

            def root(n, to):
                act.wait_ge(var_ready, n)
                f(to[:, :], rvar[:, :], ACT.Sqrt).then_inc(rstd_ready, 1)

            def columns(n, scale):
                for p in range(4):
                    act.wait_ge(turned, 4 * n + p + 1)
                    for k in range(KB):
                        last = f(HT[:, k, 2 * p * P:(2 * p + 2) * P], bank(p % 2)[:, k * D:(k + 1) * D], ACT.Copy,
                                 scale=1.0 if scale is None else cols[:, scale, k:k + 1])
                    last.then_inc(cols_ready, 1)

            def split_high(n):
                act.wait_ge(hi_in, 2 * n + 1)
                f(parts[:, :, 0, :], qd.rearrange("p (t c) -> p t c", t=B), ACT.Copy).then_inc(part_ready, 1)
                act.wait_ge(hi_in, 2 * n + 2)
                f(parts[:, :, 1, :], qr.rearrange("p (t c) -> p t c", t=B), ACT.Copy).then_inc(part_ready, 1)

            def stack_rows(n):
                act.wait_ge(part_ready, 3 * n + 3)
                with act.Fori(0, B) as t:
                    act.wait_ge(stack_turned, t + n * B)
                    two = stack[:, :, 3 * HD:5 * HD].rearrange("p h (q d) -> p q h d", q=2)
                    one_ = stack[:, :, 5 * HD:6 * HD]
                    for q in range(2):
                        src = (q if n == 0 else 1)
                        f(two[:, q], parts[:, bass.ds(t, 1), src, :].rearrange("p a (h d) -> p (a h) d", h=H), ACT.Copy)
                    src = 0 if n == 0 else 2
                    f(one_, parts[:, bass.ds(t, 1), src, :].rearrange("p a (h d) -> p (a h) d", h=H), ACT.Copy)\
                        .then_inc(stack_act, 1)

            act.wait_ge(vproj_done, 1)
            act.wait_ge(ld_const, 112)
            for m in range(KB):
                for half in range(2):
                    f(vf[:, m, half * HALF:(half + 1) * HALF], bank(4 + 2 * m + half), ACT.Identity,
                      bias=cols[:, 2, m:m + 1]).then_inc(vf_ready, 1)
            split_high(0)
            stack_rows(0)
            f(tgate[:, :], row("gates"), ACT.Tanh).then_inc(tgate_ready, 1)

            root(1, rstd)
            columns(0, None)

            def toeplitz(head, s):
                f(tslot[:, s, :], toep[:, head, :] if isinstance(head, int) else
                  toep[:, bass.ds(head, 1), :].rearrange("p a l -> p (a l)"), ACT.Copy).then_inc(t_ready, 1)

            act.wait_ge(toep_ready, 2)
            toeplitz(0, 0)
            toeplitz(1, 1)
            with act.Fori(0, H // 2 - 1) as i:
                for s in range(2):
                    act.wait_ge(conv_done[s], i + 1)
                    toeplitz(i * 2 + (2 + s), s)

            root(2, rstd)
            root(3, rms1)
            columns(1, 0)

            def hcopy(t):
                act.wait_ge(qkv_done, t)
                f(hslot[:, :, :], HT[:, :, t * P:(t + 1) * P] if isinstance(t, int) else
                  HT[:, :, bass.ds(t * P, P)], ACT.Copy).then_inc(hs_ready, 1)

            def expo(t, g):
                act.wait_ge(s_used, t * 4 + (g + 1))
                if g >= 2:
                    act.wait_ge(pt_done, t * 4 + (g - 1))
                f(pr[:, g % 2, :], sc[:, g % 2, :], ACT.Exp, scale=float(SCALE)).then_inc(e_done, 1)

            def probs_out(t, g):
                act.wait_ge(pt_done, t * 4 + (g + 1))
                if g >= 2:
                    act.wait_ge(pv_done, t * 4 + (g - 1))
                f(pT[:, g % 2, :], bank(4 + g % 2), ACT.Copy).then_inc(pt_ready, 1)

            def attend(t):
                expo(t, 0)
                expo(t, 1)
                probs_out(t, 0)
                expo(t, 2)
                probs_out(t, 1)
                expo(t, 3)
                probs_out(t, 2)
                probs_out(t, 3)

            def q_out(t):
                act.wait_ge(qkT_done, t + 1)
                f(qT[:, :, :], bank(0)[:, 0:2 * P].rearrange("p (k c) -> p k c", k=KB), ACT.Copy).then_inc(qT_ready, 1)

            def o_out(t):
                act.wait_ge(oT_done, t + 1)
                f(oT[:, :, :], bank(7)[:, 0:2 * P].rearrange("p (k c) -> p k c", k=KB), ACT.Copy).then_inc(oT_ready, 1)

            act.wait_ge(cols_ready, 8)
            hcopy(0)
            q_out(0)
            with act.Fori(1, B) as t:
                hcopy(t)
                attend(t - 1)
                q_out(t)
                o_out(t - 1)
            attend(B - 1)
            o_out(B - 1)

            def experts(layer, nft):
                steps0 = 2 * FT0 * layer
                columns(2 + 2 * layer, None if layer else 1)
                for n in range(2):
                    act.wait_ge(router_in, 2 * layer + n + 1)
                    if layer:
                        o, i = (rb[:, :, :], lg[:, :, E1:2 * E1]) if n == 0 else (rb[:, :, :], ra[:, :, :])
                        f(o, i, ACT.Exp, scale=-1.0 if n == 0 else 1.0).then_inc(router_exp, 1)
                    else:
                        o, i = (one[:, :], lg[:, :, E0]) if n == 0 else (rb[:, :, 0:E0], ra[:, :, 0:E0])
                        f(o, i, ACT.Exp, scale=-1.0 if n == 0 else 1.0).then_inc(router_exp, 1)
                act.wait_ge(combT_done, layer + 1)
                np_ = PARTS * ((E1 if layer else E0) + 1)
                act.wait_ge(zeroed, 1)
                f(combT[0:np_, :], bank16(3)[0:np_, :], ACT.Copy).then_inc(combT_ready, 1)
                with act.Fori(0, nft) as i:
                    for half in range(2):
                        act.wait_ge(gate_done, i * 2 + (steps0 + half + 1))
                        f(sg[:, half, :], bank(4), ACT.Silu).then_inc(silu_done, 1)

            act.wait_ge(u_updated, B)
            for t in range(B):
                f(sq[:, :], U[:, t, :], ACT.Square, accum_out=var[:, t:t + 1]).then_inc(ms_ready, 1)
                act.wait_ge(ms_ready, t + 1)
            root(4, rstd)
            experts(0, FT0)

            root(5, rstd)
            columns(3, None)
            split_high(1)
            stack_rows(1)

            def soft(t, h):
                u = t * H + h
                act.wait_ge(nb_ready, u + 1)
                if not (isinstance(u, int) and u < 2):
                    act.wait_ge(p_ready, u - 1)
                f(e16[:, h % 2, :], psum[:, 2 * (h % 2):2 * (h % 2) + 2, :].rearrange("p a n -> p (a n)"), ACT.Exp,
                  bias=nbias[:, h % 4:h % 4 + 1],
                  accum_out=SUM[:, u:u + 1] if isinstance(u, int) else SUM[:, bass.ds(u, 1)]).then_inc(x_done, 1)

            def out_of(t, h):
                if h in ON_ACT:
                    u = t * H + h
                    act.wait_ge(xt_done, u + 1)
                    if not (isinstance(u, int) and u < 2):
                        act.wait_ge(xv_done, u - 1)
                    f(pbT[:, h % 2, :], bank16(4 + h % 2), ACT.Copy).then_inc(xt_act, 1)

            def o_scaled(t):
                act.wait_ge(xoT_done, t + 1)
                for k in range(KB):
                    last = f(oT[:, k, :], bank(7)[:, k * P:(k + 1) * P], ACT.Copy, scale=vs[:, k:k + 1])
                last.then_inc(xoT_ready, 1)

            def tile(t, first):
                for h in range(H):
                    soft(t, h)
                    if h >= 2:
                        out_of(t, h - 2)
                    elif not first:
                        out_of(t - 1, h - 2 + H)
                    if h == 3 and not first:
                        o_scaled(t - 1)

            tile(0, True)
            with act.Fori(1, B) as t:
                tile(t, False)
            out_of(B - 1, H - 2)
            out_of(B - 1, H - 1)
            o_scaled(B - 1)
            root(6, rstd)
            experts(1, FT1)

        @block.vector
        def _(dve):
            chain = Chain(dve, dve_step)
            link, tick = chain.link, chain.tick
            tt, ts, stt = nc.vector.tensor_tensor, nc.vector.tensor_scalar, nc.vector.scalar_tensor_tensor
            red, cp = nc.vector.tensor_reduce, nc.vector.tensor_copy

            def normalise(n, root_use, dst):
                for b in range(B):
                    tick(nc.vector.bn_stats(stats[:, b, :], X[:, b, :]))
                chain.rest()
                for b in range(B):
                    tick(nc.vector.bn_aggr(mv[:, b, :], stats[:, b, :]))
                chain.rest()
                link(ts(var[:, :], mv[:, :, 1], LN_EPS, None, ALU.add))
                nc.vector.reciprocal(rvar[:, :], var[:, :]).then_inc(var_ready, 1)
                dve.wait_ge(rstd_ready, root_use)
                for b in range(B):
                    ts(dst[:, b, :], X[:, b, :], mv[:, b, 0:1], rstd[:, b:b + 1], ALU.subtract, ALU.mult)\
                        .then_inc(rows_ready, 1)

            def quantise(n):
                heads = qf.rearrange("p (g d) -> p g d", d=HD)
                link(red(am[:, :], heads, AX.X, ALU.max, apply_absolute_value=True))
                link(ts(qs[:, :], am[:, :], 1.0 / QMAX, 1e-8, ALU.mult, ALU.max))
                link(nc.vector.reciprocal(rqs[:, :], qs[:, :]))
                link(tt(qr.rearrange("p (g d) -> p g d", d=HD), heads, bc(rqs[:, :], HD, 1), ALU.mult))
                link(ts(qr, qr, ROUND, ROUND, ALU.add, ALU.subtract))
                link(ts(qr, qr, QMAX, -QMAX, ALU.min, ALU.max))
                tt(qd.rearrange("p (g d) -> p g d", d=HD), qr.rearrange("p (g d) -> p g d", d=HD),
                   bc(qs[:, :], HD, 1), ALU.mult).then_inc(hi_in, 1)
                dve.wait_ge(part_ready, 3 * n + 1)
                tt(qr.rearrange("p (t c) -> p t c", t=B), qd.rearrange("p (t c) -> p t c", t=B),
                   parts[:, :, 0, :], ALU.subtract).then_inc(hi_in, 1)
                dve.wait_ge(part_ready, 3 * n + 2)
                tt(parts[:, :, 2, :], qr.rearrange("p (t c) -> p t c", t=B), parts[:, :, 1, :], ALU.subtract)\
                    .then_inc(part_ready, 1)

            def stack_rows(n, place):
                dve.wait_ge(part_ready, 3 * n + 3)
                first = stack[:, :, 0:3 * HD].rearrange("p h (q d) -> p q h d", q=3)
                with dve.Fori(0, B) as t:
                    dve.wait_ge(stack_turned, t + n * B)
                    for q in range(3):
                        src = q if n == 0 else 0
                        last = cp(first[:, q], parts[:, bass.ds(t, 1), src, :].rearrange("p a (h d) -> p (a h) d", h=H))
                    last.then_inc(stack_dve, 1)
                    dve.wait_ge(stack_turned, t + (n * B + 1))
                    for c in range(2):
                        cp(place(t, c), bank16(c)[0:PAIRS * HD, :].rearrange("p (h c) -> p h c", h=8))\
                            .then_inc(side_ready, 1)

            dve.memset(zerob[:, :], 0.0)
            dve.wait_ge(ld_const, 112)
            for j in range(1, 4):
                cp(causal[:, j, :], causal[:, 0, :])
            for p in range(4):
                dve.wait_ge(proj_done, p + 1)
                tt(qf[:, 2 * p * D:(2 * p + 2) * D].rearrange("p (t c) -> p t c", t=2),
                   bank(p).rearrange("p (t c) -> p t c", t=2), bc(row("bk1"), 2, 0), ALU.add).then_inc(proj_used, 1)
            dve.wait_ge(proj_used, 4)
            quantise(0)
            dve.wait_ge(vf_ready, 4)
            link(red(vam[:, :], vf, AX.X, ALU.max, apply_absolute_value=True))
            link(ts(vs[:, :], vam[:, :], 1.0 / QMAX, 1e-8, ALU.mult, ALU.max))
            link(nc.vector.reciprocal(rvs[:, :], vs[:, :]))
            for m in range(KB):
                tick(ts(vf[:, m, :], vf[:, m, :], rvs[:, m:m + 1], ROUND, ALU.mult, ALU.add))
            chain.rest()
            for m in range(KB):
                tick(ts(vf[:, m, :], vf[:, m, :], ROUND, QMAX, ALU.subtract, ALU.min))
            chain.rest()
            for m in range(KB):
                ts(vq[:, m, :], vf[:, m, :], -QMAX, None, ALU.max).then_inc(vq_ready, 1)
            dve.wait_ge(vT_done, 1)
            for k in range(KB):
                cp(VI[:, :, k * P:(k + 1) * P], bank16(k).rearrange("p (t c) -> p t c", t=B)).then_inc(vi_ready, 1)
            stack_rows(0, lambda t, c: KS[:, 8 * c:8 * c + 8, bass.ds(t * P, P)])

            dve.wait_ge(ld_x, 16)
            normalise(0, 1, L)
            dve.wait_ge(cols_ready, 4)

            def ctx_of(k, h8):
                return CT[:, k, :].rearrange("p (b c) -> p b c", b=B)[:, :, bass.ds(h8, CH)]

            def products(h8, s):
                c = ctx_of(0, h8)
                tt(kv[:, s, 0, :].rearrange("p (b i j) -> p b i j", b=B, i=CH), bc(c, CH, 2), bc(c, CH, 1),
                   ALU.mult).then_inc(kv0_ready, 1)

            def query(h8, s, nth):
                dve.wait_ge(summed[s], nth)
                for k in range(KB):
                    q = HT[:, k, :].rearrange("p (b c) -> p b c", b=B)[:, :, bass.ds(h8, CH)]
                    last = tt(prod[:, s, k, :].rearrange("p (b i j) -> p b i j", b=B, i=CH),
                              bank(2 * s + k).rearrange("p (b i j) -> p b i j", b=B, i=CH), bc(q, CH, 2), ALU.mult)
                last.then_inc(y_used[s], 1)
                dve.wait_ge(y_used[s], nth + 1)
                for k in range(KB):
                    last = red(osum[:, k, :, :][:, :, bass.ds(h8, CH)],
                               prod[:, s, k, :].rearrange("p (b i j) -> p b j i", b=B, i=CH), AX.X, ALU.add)
                last.then_inc(summed[s], 1)

            products(0, 0)
            products(CH, 1)
            with dve.Fori(0, H // 2 - 1) as i:
                for s in range(2):
                    h8 = dve.snap(i * (2 * CH) + s * CH)
                    dve.wait_ge(conv_done[s], i + 1)
                    products(h8 + 2 * CH, s)
                    query(h8, s, i)
            for s in range(2):
                dve.wait_ge(conv_done[s], H // 2)
                query(S - 2 * CH + s * CH, s, H // 2 - 1)
            dve.wait_ge(tgate_ready, 1)
            for p in range(4):
                dve.wait_ge(oturned, p + 1)
                stt(X[:, 2 * p:2 * p + 2, :].rearrange("p t c -> p (t c)"), bank(4 + p), tgate[:, 0:1],
                    X[:, 2 * p:2 * p + 2, :].rearrange("p t c -> p (t c)"), ALU.mult, ALU.add).then_inc(x_updated, 1)
            dve.wait_ge(x_updated, 4)

            normalise(1, 2, U)
            link(tt(var[:, :], mv[:, :, 1], rvar[:, :], ALU.mult))
            link(ts(var[:, :], var[:, :], RMS_EPS, None, ALU.add))
            nc.vector.reciprocal(rvar[:, :], var[:, :]).then_inc(var_ready, 1)
            dve.wait_ge(rstd_ready, 3)

            def qkv_in(t):
                dve.wait_ge(qkv_done, t + 1)
                dve.wait_ge(roped_ready, t)
                r = rms1[:, t:t + 1] if isinstance(t, int) else rms1[:, bass.ds(t, 1)]
                stt(QK[:, :], bank(0), r, row("bqk"), ALU.mult, ALU.add).then_inc(qkv_used, 1)
                v = Vx[:, t, :, 0:HD] if isinstance(t, int) else \
                    Vx[:, bass.ds(t, 1), :, 0:HD].rearrange("p a h d -> p (a h) d")
                stt(v, bank(1)[:, 0:D].rearrange("p (h d) -> p h d", h=H), r,
                    row("bv").rearrange("p (h d) -> p h d", h=H), ALU.mult, ALU.add).then_inc(qkv_used, 1)

            def k_blocks(t):
                dve.wait_ge(qkT_done, t + 1)
                for k in range(KB):
                    last = tt(kblock[:, k, :, :], bc(bank(1)[:, k * P:(k + 1) * P], 8, 0), bc(headmask, P, 1), ALU.mult)
                last.then_inc(kb_ready, 1)

            def shift(t, g):
                dve.wait_ge(s_done, t * 4 + (g + 1))
                link(red(nmax[:, g, :], bank(2 + g % 2).rearrange("p (j c) -> p j c", j=4), AX.X, ALU.max, negate=True))
                if g >= 2:
                    dve.wait_ge(e_done, t * 4 + (g - 1))
                tt(sc[:, g % 2, :].rearrange("p (j c) -> p j c", j=4), bank(2 + g % 2).rearrange("p (j c) -> p j c", j=4),
                   bc(nmax[:, g, :], P, 1), ALU.add).then_inc(s_used, 1)

            def divide(t):
                dve.wait_ge(pv_done, t * 4 + 4)
                acc = bank(6)[:, 0:H * (HD + 1)].rearrange("p (h d) -> p h d", h=H)
                link(nc.vector.reciprocal(rden[:, :], acc[:, :, HD]))
                dve.wait_ge(wo_done, t)
                tt(orow[:, :].rearrange("p (h d) -> p h d", h=H), acc[:, :, 0:HD], bc(rden[:, :], HD, 1), ALU.mult)\
                    .then_inc(o_ready, 1)

            def residual(t):
                dve.wait_ge(wo_done, t + 1)
                u = U[:, t, :] if isinstance(t, int) else U[:, bass.ds(t, 1), :].rearrange("p a c -> p (a c)")
                tt(u, bank(7)[:, D:2 * D], u, ALU.add).then_inc(u_updated, 1)

            link(nc.vector.memset(Vx[:, :, :, HD], 1.0))
            qkv_in(0)
            k_blocks(0)
            with dve.Fori(1, B) as t:
                chain.enter(t - 1, 5)
                qkv_in(t)
                for g in range(4):
                    shift(t - 1, g)
                divide(t - 1)
                k_blocks(t)
                residual(t - 1)
            chain.leave(B - 1)
            for g in range(4):
                shift(B - 1, g)
            divide(B - 1)
            residual(B - 1)

            dve.wait_ge(ms_ready, B)
            link(ts(var[:, :], var[:, :], 1.0 / D, RMS_EPS, ALU.mult, ALU.add))
            nc.vector.reciprocal(rvar[:, :], var[:, :]).then_inc(var_ready, 1)
            dve.wait_ge(rstd_ready, 4)
            for b in range(B):
                ts(L[:, b, :], U[:, b, :], rstd[:, b:b + 1], None, ALU.mult).then_inc(rows_ready, 1)

            def softmax(n, e):
                link(red(top[:, :, 0], ra[:, :, 0:e], AX.X, ALU.max, negate=True))
                tt(ra[:, :, 0:e], ra[:, :, 0:e], bc(top[:, :, 0], e, 1), ALU.add).then_inc(router_in, 1)
                dve.wait_ge(router_exp, 2 * n + 2)
                link(red(top[:, :, 1], rb[:, :, 0:e], AX.X, ALU.add))
                link(nc.vector.reciprocal(top[:, :, 2], top[:, :, 1]))
                link(tt(rc[:, :, 0:e], rb[:, :, 0:e], bc(top[:, :, 2], e, 1), ALU.mult))

            def combine(n, e):
                for b in range(B):
                    tick(nc.vector.max(top[:, b, :], key[:, b, 0:e]))
                chain.rest()
                for b in range(B):
                    tick(nc.vector.max_index(topi[:, b, :], top[:, b, :], key[:, b, 0:e]))
                chain.rest()
                link(cp(topf[:, :, :], topi[:, :, 0:2]))
                for s in range(2):
                    tick(tt((ra, rb)[s][:, :, 0:e], bc(iota[:, 0:e], B, 0), bc(topf[:, :, s], e, 1), ALU.is_equal))
                chain.rest()
                link(tt(ra[:, :, 0:e], ra[:, :, 0:e], rb[:, :, 0:e], ALU.add))
                link(tt(comb[:, :, 0:e], ra[:, :, 0:e], wgt[:, :, 0:e], ALU.mult))
                dst = cparts[:, :, :]
                w = e + 1
                link(cp(dst[:, :, 0:w], comb[:, :, 0:w]))
                link(tt(comb2[:, :, 0:w], comb[:, :, 0:w], dst[:, :, 0:w], ALU.subtract))
                link(cp(dst[:, :, w:2 * w], comb2[:, :, 0:w]))
                tt(dst[:, :, 2 * w:3 * w], comb2[:, :, 0:w], dst[:, :, w:2 * w], ALU.subtract).then_inc(comb_ready, 1)

            def experts(layer, nft):
                steps0 = 2 * FT0 * layer
                with dve.Fori(0, nft) as i:
                    for half in range(2):
                        dve.wait_ge(up_done, i * 2 + (steps0 + half + 1))
                        dve.wait_ge(silu_done, i * 2 + (steps0 + half + 1))
                        tt(su[:, half, :], bank(5), sg[:, half, :], ALU.mult).then_inc(su_done, 1)
                        dve.wait_ge(c_done, i * 2 + (steps0 + half + 1))
                        dve.wait_ge(su_done, i * 2 + (steps0 + half + 1))
                        tt(hid[:, half, :], bank(6), su[:, half, :], ALU.mult).then_inc(hid_ready, 1)

            dve.wait_ge(router_done, 1)
            cp(lg[:, :, 0:E0 + 1], bank(2)[:, 0:B * (E0 + 1)].rearrange("p (t e) -> p t e", t=B)).then_inc(router_in, 1)
            dve.wait_ge(router_in, 1)
            link(cp(ra[:, :, 0:E0], lg[:, :, 0:E0]))
            softmax(0, E0)
            link(cp(key[:, :, 0:E0], rc[:, :, 0:E0]))
            link(cp(wgt[:, :, 0:E0], rc[:, :, 0:E0]))
            link(ts(one[:, :], one[:, :], 1.0, None, ALU.add))
            link(nc.vector.reciprocal(comb[:, :, E0], one[:, :]))
            combine(0, E0)
            experts(0, FT0)
            dve.wait_ge(down_done, 2 * FT0)
            for p in range(4):
                pair = slice(2 * p, 2 * p + 2)
                flat = lambda z: z[:, pair, :].rearrange("p t c -> p (t c)")
                link(tt(flat(U), bank(p), flat(U), ALU.add))
                stt(flat(X), flat(U), tgate[:, 1:2], flat(X), ALU.mult, ALU.add).then_inc(moe_used, 1)
            dve.wait_ge(moe_used, 4)

            normalise(2, 5, L)
            link(ts(bq25[:, :], row("bq1"), float(SCALE), None, ALU.mult))
            link(ts(bpt[:, :], row("bp"), tgate[:, 2:3], None, ALU.mult))
            link(tt(X[:, :, :], X[:, :, :], bc(bpt[:, :], B, 0), ALU.add))
            for p in range(4):
                dve.wait_ge(proj_done, 4 + p + 1)
                stt(qf[:, 2 * p * D:(2 * p + 2) * D].rearrange("p (t c) -> p t c", t=2),
                    bank(p).rearrange("p (t c) -> p t c", t=2), float(SCALE), bc(bq25[:, :], 2, 0),
                    ALU.mult, ALU.add).then_inc(proj_used, 1)
            dve.wait_ge(proj_used, 8)
            quantise(1)
            stack_rows(1, lambda t, c: QS[:, bass.ds(t * H + 8 * c, 8), :])

            def peak(t, h):
                u = t * H + h
                dve.wait_ge(l_done, u + 1)
                red(peaks[:, h % 4:h % 4 + 1], psum[:, 2 * (h % 2):2 * (h % 2) + 2, :].rearrange("p a n -> p (a n)"),
                    AX.X, ALU.max, negate=True).then_inc(peak_found, 1)
                dve.wait_ge(peak_found, u + 1)
                ts(nbias[:, h % 4:h % 4 + 1], peaks[:, h % 4:h % 4 + 1], LN255, None, ALU.add).then_inc(nb_ready, 1)

            def integers(t, h):
                u = t * H + h
                dve.wait_ge(x_done, u + 1)
                if not (isinstance(u, int) and u < 2):
                    dve.wait_ge(xt_done, u - 1)
                cp(pb[:, h % 2, :], e16[:, h % 2, :]).then_inc(p_ready, 1)

            def out_of(t, h):
                if h in ON_DVE:
                    u = t * H + h
                    dve.wait_ge(xt_done, u + 1)
                    if not (isinstance(u, int) and u < 2):
                        dve.wait_ge(xv_done, u - 1)
                    cp(pbT[:, h % 2, :], bank16(4 + h % 2)).then_inc(xt_dve, 1)

            def scale_rows(t):
                dve.wait_ge(xv_done, (t + 1) * H)
                s = SUM[:, t * H:(t + 1) * H] if isinstance(t, int) else SUM[:, bass.ds(t * H, H)]
                link(nc.vector.reciprocal(rden[:, :], s))
                dve.wait_ge(xp_done, t)
                tt(orow[:, :].rearrange("p (h d) -> p h d", h=H), bank(6)[:, 0:D].rearrange("p (h d) -> p h d", h=H),
                   bc(rden[:, :], HD, 1), ALU.mult).then_inc(xo_ready, 1)

            def add_out(t):
                dve.wait_ge(xp_done, t + 1)
                x = X[:, t, :] if isinstance(t, int) else X[:, bass.ds(t, 1), :].rearrange("p a c -> p (a c)")
                stt(x, bank(7)[:, D:2 * D], tgate[:, 2:3], x, ALU.mult, ALU.add).then_inc(xx_updated, 1)

            def tile(t, first):
                for h in range(H):
                    peak(t, h)
                    if h >= 1:
                        integers(t, h - 1)
                    elif not first:
                        integers(t - 1, H - 1)
                    if h >= 2:
                        out_of(t, h - 2)
                    elif not first:
                        out_of(t - 1, h - 2 + H)
                    if h == 3 and not first:
                        scale_rows(t - 1)
                    if h == 5 and not first:
                        add_out(t - 1)

            tile(0, True)
            with dve.Fori(1, B) as t:
                chain.enter(t - 1, 1)
                tile(t, False)
            chain.leave(B - 1)
            integers(B - 1, H - 1)
            out_of(B - 1, H - 2)
            out_of(B - 1, H - 1)
            scale_rows(B - 1)
            add_out(B - 1)
            dve.wait_ge(xx_updated, B)

            normalise(3, 6, L)
            dve.wait_ge(router_done, 2)
            cp(lg[:, :, :], bank(2)[:, 0:B * 2 * E1].rearrange("p (t e) -> p t e", t=B)).then_inc(router_in, 1)
            dve.wait_ge(router_in, 3)
            dve.wait_ge(router_exp, 3)
            link(ts(rb[:, :, :], rb[:, :, :], 1.0, None, ALU.add))
            link(nc.vector.reciprocal(rc[:, :, :], rb[:, :, :]))
            link(tt(rc[:, :, :], rc[:, :, :], lg[:, :, E1:2 * E1], ALU.mult))
            link(tt(rc[:, :, :], rc[:, :, :], lg[:, :, 0:E1], ALU.mult))
            link(ts(rb[:, :, :], rc[:, :, :], -1.0, None, ALU.mult))
            link(tt(ra[:, :, :], rb[:, :, :], rc[:, :, :], ALU.max))
            softmax(1, E1)
            link(tt(key[:, :, :], rc[:, :, :], bc(row("ebias"), B, 0), ALU.add))
            link(tt(wgt[:, :, :], rc[:, :, :], bc(row("escale"), B, 0), ALU.mult))
            link(ts(wgt[:, :, :], wgt[:, :, :], 1.0, None, ALU.add))
            link(nc.vector.memset(comb[:, :, E1], 1.0))
            combine(1, E1)
            experts(1, FT1)
            dve.wait_ge(down_done, 2 * (FT0 + FT1))
            for p in range(4):
                flat = X[:, 2 * p:2 * p + 2, :].rearrange("p t c -> p (t c)")
                stt(flat, bank(p), tgate[:, 3:4], flat, ALU.mult, ALU.add).then_inc(moe_used, 1)

        @block.gpsimd
        def _(pool):
            tt = nc.gpsimd.tensor_tensor
            nc.gpsimd.memset(combT[:, :], 0.0).then_inc(zeroed, 1)
            pool.wait_ge(ld_const, 112)
            pool.wait_ge(ld_toep, 16 * H)
            pool.wait_ge(side_ready, 2 * B)
            tt(diag, bc(antident, H, 0), bc(row("conv_d"), P, 1), ALU.mult).then_inc(toep_ready, 1)
            pool.wait_ge(toep_ready, 1)
            tt(toep[:, :, 0:P], toep[:, :, 0:P], diag, ALU.add).then_inc(toep_ready, 1)

            def products(h8, s):
                c = CT[:, 1, :].rearrange("p (b c) -> p b c", b=B)[:, :, bass.ds(h8, CH)]
                tt(kv[:, s, 1, :].rearrange("p (b i j) -> p b i j", b=B, i=CH), bc(c, CH, 2), bc(c, CH, 1),
                   ALU.mult).then_inc(kv1_ready, 1)

            products(0, 0)
            products(CH, 1)
            with pool.Fori(0, H // 2 - 1) as i:
                for s in range(2):
                    pool.wait_ge(conv_done[s], i + 1)
                    products(i * (2 * CH) + (2 + s) * CH, s)

            def rope(t):
                heads = lambda z: z.rearrange("p (g d) -> p g d", d=HD)
                half = HD // 2
                pool.wait_ge(qkv_used, t * 2 + 2)
                tt(heads(rope1), heads(QK), bc(cosine, 2 * H, 0), ALU.mult).then_inc(rope_mid, 1)
                for lo, hi in ((0, half), (half, 0)):
                    tt(heads(rope2)[:, :, lo:lo + half], heads(QK)[:, :, hi:hi + half],
                       bc(sine[:, lo:lo + half], 2 * H, 0), ALU.mult).then_inc(rope_mid, 1)
                pool.wait_ge(qkT_done, t)
                pool.wait_ge(rope_mid, t * 3 + 3)
                tt(roped, rope1, rope2, ALU.add).then_inc(roped_ready, 1)

            rope(0)
            with pool.Fori(1, B) as t:
                rope(t)


def toeplitz_source(kernel):
    return np.concatenate([np.zeros_like(kernel), kernel], axis=1)


def backwards(features):
    return features.reshape(KB, P, -1)[:, ::-1].reshape(D, -1)


def expert_tiles(gate, up, down, nft):
    short = nft * P - gate.shape[1]
    gate, up = (np.pad(w, ((0, 0), (0, short))).reshape(KB, P, nft, P).transpose(2, 1, 0, 3).reshape(nft, P, D)
                for w in (gate, up))
    down = np.pad(down, ((0, short), (0, 0))).reshape(nft, P, D)
    return np.concatenate([gate, up, down], axis=2)


def selector(experts, shared, nft, dtype):
    owner = np.full(nft * P, -1)
    owner[:experts * F + shared] = np.minimum(np.arange(experts * F + shared) // F, experts)
    sel = np.zeros((P, nft * P), dtype)
    for part in range(PARTS):
        for e in range(experts + 1):
            sel[part * (experts + 1) + e] = owner == e
    return sel


def kernel(**z):
    import ml_dtypes
    import concourse.bacc as _bacc
    from concourse import mybir as _mybir
    from concourse.bass_utils import run_bass_kernel_spmd as _run

    z = {k: np.asarray(v) for k, v in z.items()}
    f32, b16 = np.float32, ml_dtypes.bfloat16
    inv = 1.0 / 1000000.0 ** (np.arange(0, HD, 2, dtype=f32) / f32(HD))
    angle = np.arange(S, dtype=f32)[:, None] * inv.astype(f32)[None, :]
    cos, sin = np.cos(angle), np.sin(angle)
    consts = np.concatenate([np.eye(P), cos, cos, -sin, sin, np.tile(np.arange(HD), (P, 1)),
                             np.arange(P)[:, None] // HD == np.arange(8)[None, :], np.eye(P)[::-1]], axis=1).astype(f32)
    flat = lambda w: w.transpose(1, 0, 2).reshape(w.shape[1], -1)
    arrays = {
        "x": z["x"],
        "ctxT": backwards(z["ctx_2048"].reshape(N, D).T),
        "conv": toeplitz_source(z["L0_xattn_ssm_kernel"]),
        "consts": consts,
        "rows": np.concatenate([z["L0_ffn_bq"], z["L0_ffn_bk"], z["L0_ffn_bv"], z["L1_xattn_bq"],
                                z["L1_xattn_bkv"][:D], z["L1_xattn_bp"], z["L1_ffn_extra_scale"],
                                z["L1_ffn_extra_bias"], z["L0_xattn_D"], z["g_xattn"][:1], z["g_ffn"][:1],
                                z["g_xattn"][1:], z["g_ffn"][1:]]),
        "cols": np.stack([z["L0_ffn_w_ln1"], z["L0_ffn_w_ln2"], z["L1_xattn_bkv"][D:]]).reshape(3, KB, P).transpose(2, 0, 1),
        "identb": np.eye(P).astype(b16),
        "causal": np.where(np.tril(np.ones((P, P), bool)), 0.0, -1e30).astype(b16),
        "sel0": selector(E0, SH0, FT0, b16),
        "sel1": selector(E1, SH1, FT1, b16),
        "wqkv": np.concatenate([z["L0_ffn_wq"], z["L0_ffn_wk"], z["L0_ffn_wv"]], axis=1),
        "wo": z["L0_ffn_wo"],
        "wr0": np.concatenate([z["L0_ffn_w_router"], z["L0_ffn_w_sh_eg"]], axis=1),
        "wq1": z["L1_xattn_Wq"],
        "wk1": backwards(z["L1_xattn_Wkv"][:, :D]),
        "wv1": backwards(z["L1_xattn_Wkv"][:, D:]),
        "wp1": z["L1_xattn_Wp"],
        "wr1": np.concatenate([z["L1_ffn_cls_w"].T, z["L1_ffn_gate_w"].T], axis=1),
        "moe0": expert_tiles(np.concatenate([flat(z["L0_ffn_w_gate_e"]), z["L0_ffn_w_sh_gate"]], axis=1),
                             np.concatenate([flat(z["L0_ffn_w_up_e"]), z["L0_ffn_w_sh_up"]], axis=1),
                             np.concatenate([z["L0_ffn_w_down_e"].reshape(-1, D), z["L0_ffn_w_sh_down"]]), FT0),
        "moe1": expert_tiles(np.concatenate([z["L1_ffn_wg"].reshape(-1, D), z["L1_ffn_sg"]]).T,
                             np.concatenate([z["L1_ffn_wu"].reshape(-1, D), z["L1_ffn_su"]]).T,
                             np.concatenate([z["L1_ffn_wd"].transpose(0, 2, 1).reshape(-1, D), z["L1_ffn_sd"].T]),
                             FT1),
    }
    arrays = {k: np.ascontiguousarray(v) for k, v in arrays.items()}
    nc = _bacc.Bacc("TRN2", target_bir_lowering=False, num_devices=1)
    args = {k: nc.dram_tensor(f"in_{k}", v.shape, _mybir.dt.from_np(v.dtype), kind="ExternalInput").ap()
            for k, v in arrays.items()}
    out = nc.dram_tensor("out_0", (B, S, D), _mybir.dt.float32, kind="ExternalOutput").ap()
    build(nc, args, out)
    r = _run(nc, [{f"in_{k}": v for k, v in arrays.items()}], core_ids=[0])
    return r.results[0]["out_0"]
```

```python
from contextlib import ExitStack

import numpy as np

import concourse.bass as bass
from concourse import mybir

ALU = mybir.AluOpType
ACT = mybir.ActivationFunctionType
AX = mybir.AxisListType
F32 = mybir.dt.float32
BF16 = mybir.dt.bfloat16
I16 = mybir.dt.int16
F32R = mybir.dt.float32r
U32 = mybir.dt.uint32

P = 128
B, S, D = 8, 128, 256
N = B * S
KB = D // P
H = 16
HD = D // H
CH = S // H
LN_EPS, RMS_EPS = 1e-5, 1e-6
SCALE = 1.0 / np.sqrt(HD)
ROUND = 1.5 * 2.0 ** 23
QMAX = 127.0
LN255 = float(np.log(255.0))
PARTS = 3
PAIRS = 6
F = 176
E0, E1 = 8, 14
SH0, SH1 = 704, 352
HALF = 512


def tiles_of(experts, shared):
    return -(-(experts * F + shared) // P)


FT0, FT1 = tiles_of(E0, SH0), tiles_of(E1, SH1)

ROWS = {}
for _name, _n in (("bqk", 2 * D), ("bv", D), ("bq1", D), ("bk1", D), ("bp", D), ("escale", E1),
                  ("ebias", E1), ("conv_d", H), ("gates", 4)):
    ROWS[_name] = (sum(n for _, n in ROWS.values()), _n)
NROWS = sum(n for _, n in ROWS.values())


class Chain:

    def __init__(self, eng, sem):
        self.eng, self.sem, self.count, self.links = eng, sem, 0, 0

    def link(self, ins):
        self.tick(ins)
        self.eng.wait_ge(self.sem, self.count)

    def tick(self, ins):
        ins.then_inc(self.sem, 1)
        self.count = self.count + 1
        self.links += 1

    def rest(self):
        self.eng.wait_ge(self.sem, self.count)

    def enter(self, trip, per):
        self.start, self.per, self.at = self.count, per, self.links
        self.count = self.start + trip * per

    def leave(self, trips):
        assert self.links - self.at == self.per, (self.links - self.at, self.per)
        self.count = self.start + trips * self.per


def build(nc, a, out):
    ctx = ExitStack()
    with ctx:
        def sb(name, shape, dt=F32):
            return ctx.enter_context(nc.sbuf_tensor(name, shape, dt))

        def sem(name):
            return ctx.enter_context(nc.semaphore(name))

        psum = ctx.enter_context(nc.psum_tensor("psum", [P, 8, 512], F32))

        def bank(n):
            return psum[:, n, :]

        def bank16(n):
            return psum[:, n, :].bitcast(BF16)

        consts = sb("consts", [P, 2 * P + 2 * HD + HD + 8])
        identb = sb("identb", [P, P], BF16)
        unit = sb("unit", [P, 1])
        causal = sb("causal", [P, 4, P], BF16)
        zerob = sb("zerob", [1, 512], BF16)
        rows = sb("rows", [P, NROWS])
        cols = sb("cols", [P, 3, KB])
        tgate = sb("tgate", [P, 4])
        ident = consts[:, 0:P]
        cosine = consts[:, P:P + HD]
        sine = consts[:, P + HD:P + 2 * HD]
        iota = consts[:, P + 2 * HD:P + 3 * HD]
        headmask = consts[:, P + 3 * HD:P + 3 * HD + 8]
        antident = consts[:, P + 3 * HD + 8:]

        def row(name):
            o, n = ROWS[name]
            return rows[:, o:o + n]

        X = sb("X", [P, B, D])
        L = sb("L", [P, B, D])
        HT = sb("HT", [P, KB, N])
        CT = sb("CT", [P, KB, N])
        stats = sb("stats", [P, B, 6])
        mv = sb("mv", [P, B, 2])
        var = sb("var", [P, B])
        rvar = sb("rvar", [P, B])
        rstd = sb("rstd", [P, B])
        rms1 = sb("rms1", [P, B])

        wqkv = sb("wqkv", [P, KB, 3 * D])
        wo = sb("wo", [P, KB, D])
        wr0 = sb("wr0", [P, KB, E0 + 1])
        wq1 = sb("wq1", [P, KB, D])
        wk1 = sb("wk1", [P, KB, D])
        wv1 = sb("wv1", [P, KB, D])
        wp1 = sb("wp1", [P, KB, D])
        wr1 = sb("wr1", [P, KB, 2 * E1])
        wm = sb("wm", [P, 2, 3 * D])

        hid_hi, hid_lo = sb("hid_hi", [P, 2, HALF], F32R), sb("hid_lo", [P, 2, HALF], F32R)
        HT_hi, HT_lo = sb("HT_hi", [P, KB, N], F32R), sb("HT_lo", [P, KB, N], F32R)
        wm_hi, wm_lo = sb("wm_hi", [P, 2, 3 * D], F32R), sb("wm_lo", [P, 2, 3 * D], F32R)

        area = sb("area", [P, 12288])
        keys = sb("keys", [P, 8192])

        def part(at, n, dt=F32, of=area):
            v = of[:, at:at + n]
            return v if dt == F32 else v.bitcast(dt)

        qf, qr, qd = part(0, 2048), part(2048, 2048), part(4096, 2048)
        vf = part(6144, 2048).rearrange("p (k n) -> p k n", k=KB)
        vq = part(8192, 1024, BF16).rearrange("p (k n) -> p k n", k=KB)
        parts = part(9216, 3072, BF16).rearrange("p (t a c) -> p t a c", t=B, a=PARTS)
        kv = part(0, 2048).rearrange("p (s k n) -> p s k n", s=2, k=KB)
        prod = part(2048, 2048).rearrange("p (s k n) -> p s k n", s=2, k=KB)
        tslot = part(4096, 512).rearrange("p (s l) -> p s l", s=2)
        toep = part(0, 4096, of=keys).rearrange("p (h l) -> p h l", h=H)
        diag = part(4096, 2048, of=keys).rearrange("p (h l) -> p h l", h=H)
        osum = part(6144, 2048, of=keys).rearrange("p (k b c) -> p k b c", k=KB, b=B)
        Vx = part(0, B * H * (HD + 1)).rearrange("p (t h d) -> p t h d", t=B, h=H)
        kblock = part(0, 2048, of=keys).rearrange("p (k j c) -> p k j c", k=KB, j=8)
        pT = part(2048, 1024, of=keys).rearrange("p (s n) -> p s n", s=2)
        QK, rope1, rope2, roped = part(2304, 512), part(2816, 512), part(3328, 512), part(3840, 512)
        sc = part(4352, 1024).rearrange("p (s n) -> p s n", s=2)
        pr = part(5376, 1024).rearrange("p (s n) -> p s n", s=2)
        U = part(7168, 2048).rearrange("p (t c) -> p t c", t=B)
        sg = part(0, 1024).rearrange("p (s n) -> p s n", s=2)
        su = part(1024, 1024).rearrange("p (s n) -> p s n", s=2)
        sel0, sel1 = part(2048, FT0 * P // 2, BF16), part(2048, FT1 * P // 2, BF16)
        QS = area[0:PAIRS * HD, 0:8192].bitcast(BF16).rearrange("p (u c) -> p u c", c=P)
        e16 = part(8192, 1024, I16).rearrange("p (s n) -> p s n", s=2)
        pb = part(9216, 1024, BF16).rearrange("p (s n) -> p s n", s=2)
        pbT = part(10240, 2048, BF16).rearrange("p (s n) -> p s n", s=4)

        hslot = sb("hslot", [P, KB, P])
        qT = sb("qT", [P, KB, P])
        nmax = sb("nmax", [P, 4, 4])
        rden = sb("rden", [P, H])
        orow = sb("orow", [P, D])
        oT = sb("oT", [P, KB, P])
        sq = sb("sq", [P, D])
        lg = sb("lg", [P, B, 2 * E1])
        ra = sb("ra", [P, B, E1])
        rb = sb("rb", [P, B, E1])
        rc = sb("rc", [P, B, E1])
        key = sb("key", [P, B, E1])
        wgt = sb("wgt", [P, B, E1])
        one = sb("one", [P, B])
        top = sb("top", [P, B, 8])
        topi = sb("topi", [P, B, 8], U32)
        topf = sb("topf", [P, B, 2])
        comb = sb("comb", [P, B, E1 + 1])
        comb2 = sb("comb2", [P, B, E1 + 1])
        cparts = sb("cparts", [P, B, PARTS * (E1 + 1)], BF16)
        combT = sb("combT", [P, N], BF16)
        am = sb("am", [P, P])
        qs = sb("qs", [P, P])
        rqs = sb("rqs", [P, P])
        stack = sb("stack", [P, H, PAIRS * HD], BF16)
        KS = keys[0:PAIRS * HD, :].bitcast(BF16).rearrange("p (h n) -> p h n", h=H)
        vam = sb("vam", [P, KB])
        vs = sb("vs", [P, KB])
        rvs = sb("rvs", [P, KB])
        VI = sb("VI", [P, B, D], BF16)
        bq25 = sb("bq25", [P, D])
        bpt = sb("bpt", [P, D])
        peaks = sb("peaks", [P, 4])
        nbias = sb("nbias", [P, 4])
        SUM = sb("SUM", [P, B * H])

        ld_x, ld_ctx, ld_toep, ld_const = sem("ld_x"), sem("ld_ctx"), sem("ld_toep"), sem("ld_const")
        ld_w0, ld_w1, ld_sel = sem("ld_w0"), sem("ld_w1"), sem("ld_sel")
        ld_wm = [sem("ld_wm0"), sem("ld_wm1")]
        tgate_ready, var_ready, rstd_ready = sem("tgate_ready"), sem("var_ready"), sem("rstd_ready")
        rows_ready, turned, cols_ready = sem("rows_ready"), sem("turned"), sem("cols_ready")
        toep_ready = sem("toep_ready")
        t_ready, kv0_ready, kv1_ready = sem("t_ready"), sem("kv0_ready"), sem("kv1_ready")
        conv_done = [sem("conv_done0"), sem("conv_done1")]
        y_used = [sem("y_used0"), sem("y_used1")]
        summed = [sem("summed0"), sem("summed1")]
        zeroed = sem("zeroed")
        oturned, x_updated = sem("oturned"), sem("x_updated")
        hs_ready, qkv_done, qkv_used = sem("hs_ready"), sem("qkv_done"), sem("qkv_used")
        roped_ready, qkT_done, qT_ready, kb_ready = sem("roped_ready"), sem("qkT_done"), sem("qT_ready"), sem("kb_ready")
        s_done, s_used, e_done = sem("s_done"), sem("s_used"), sem("e_done")
        pt_done, pt_ready, pv_done = sem("pt_done"), sem("pt_ready"), sem("pv_done")
        o_ready, oT_done, oT_ready, wo_done, u_updated = (sem("o_ready"), sem("oT_done"), sem("oT_ready"),
                                                         sem("wo_done"), sem("u_updated"))
        ms_ready = sem("ms_ready")
        router_done, router_exp, router_in = sem("router_done"), sem("router_exp"), sem("router_in")
        comb_ready, combT_done, combT_ready = sem("comb_ready"), sem("combT_done"), sem("combT_ready")
        gate_done, up_done, c_done = sem("gate_done"), sem("up_done"), sem("c_done")
        silu_done, su_done, hid_ready, down_done = sem("silu_done"), sem("su_done"), sem("hid_ready"), sem("down_done")
        unit_ready = sem("unit_ready")
        moe_used, ht_split, su_spread = sem("moe_used"), sem("ht_split"), sem("su_spread")
        hid_rounded = sem("hid_rounded")
        w_split = [sem("w_split0"), sem("w_split1")]
        proj_done, proj_used = sem("proj_done"), sem("proj_used")
        keys_turned = sem("keys_turned")
        vproj_done, vf_ready, vq_ready, vT_done, vi_ready = (sem("vproj_done"), sem("vf_ready"), sem("vq_ready"),
                                                            sem("vT_done"), sem("vi_ready"))
        hi_in, part_ready, dq_ready = sem("hi_in"), sem("part_ready"), sem("dq_ready")
        stack_dve, stack_act, stack_turned, side_ready = (sem("stack_dve"), sem("stack_act"), sem("stack_turned"),
                                                          sem("side_ready"))
        l_done, nb_ready, x_done, p_ready = sem("l_done"), sem("nb_ready"), sem("x_done"), sem("p_ready")
        xt_done, xt_act, xt_dve, xv_done = sem("xt_done"), sem("xt_act"), sem("xt_dve"), sem("xv_done")
        xo_ready, xoT_done, xoT_ready, xp_done, xx_updated = (sem("xo_ready"), sem("xoT_done"), sem("xoT_ready"),
                                                             sem("xp_done"), sem("xx_updated"))
        peak_found = sem("peak_found")
        dve_step, rope_mid = sem("dve_step"), sem("rope_mid")
        stored = sem("stored")

        block = ctx.enter_context(nc.Block())

        ON_ACT = [h for h in range(H) if h % 8 in (0, 2, 3, 4, 6, 7)]
        ON_DVE = [h for h in range(H) if h not in ON_ACT]
        HELD = ((0, 0), ((FT0 + 1) // 2, FT0 // 2))
        MAIN0, MAIN1 = (FT0 - 1) // 2, (FT1 - 1) // 2

        def bc(ap, n, at):
            dims = [list(d) for d in ap.ap]
            dims.insert(at + 1, [0, n])
            return bass.AP(ap.tensor, ap.offset, dims)

        def copied_out(eng, t, h):
            if h < 0:
                if isinstance(t, int) and t == 0:
                    return
                t, h = t - 1, h + H
            if h in ON_ACT:
                eng.wait_ge(xt_act, t * len(ON_ACT) + (ON_ACT.index(h) + 1))
            else:
                eng.wait_ge(xt_dve, t * len(ON_DVE) + (ON_DVE.index(h) + 1))

        @block.sync
        def _(sp):
            sp.dma_start(X[:, :, :], a["x"].rearrange("b s d -> s b d")).then_inc(ld_x, 16)
            sp.dma_start(CT[:, :, :], a["ctxT"].rearrange("(k p) n -> p k n", p=P)).then_inc(ld_ctx, 16)
            for h in range(H):
                sp.dma_start(toep[:, h, :],
                             bass.AP(a["conv"].tensor, h * 2 * D + D - (P - 1), [[1, P], [1, D]])).then_inc(ld_toep, 16)
            for w, name in ((wqkv, "wqkv"), (wo, "wo"), (wr0, "wr0")):
                sp.dma_start(w[:, :, :], a[name].rearrange("(k p) n -> p k n", p=P)).then_inc(ld_w0, 16)
            for w, name in ((wq1, "wq1"), (wk1, "wk1"), (wv1, "wv1"), (wp1, "wp1"), (wr1, "wr1")):
                sp.dma_start(w[:, :, :], a[name].rearrange("(k p) n -> p k n", p=P)).then_inc(ld_w1, 16)

            def experts(src, nft, before, selectors, dst, free, count):
                def load(ft, slot):
                    if before[slot] + ft // 2:
                        sp.wait_ge(w_split[slot], 4 * (before[slot] + ft // 2))
                    sp.dma_start(wm[:, slot, :], src[ft, :, :]).then_inc(ld_wm[slot], 16)
                for slot in range(2):
                    load(slot, slot)
                sp.wait_ge(free, count)
                sp.dma_start(dst, a[selectors]).then_inc(ld_sel, 16)
                with sp.Fori(0, (nft - 2) // 2) as i:
                    for slot in range(2):
                        sp.wait_ge(w_split[slot], i * 4 + 4 * (before[slot] + 1))
                        sp.dma_start(wm[:, slot, :], src[bass.ds(i * 2 + (2 + slot), 1), :, :]
                                     .rearrange("a p n -> p (a n)")).then_inc(ld_wm[slot], 16)
                if nft % 2:
                    load(nft - 1, 0)

            experts(a["moe0"], FT0, HELD[0], "sel0", sel0, u_updated, B)
            experts(a["moe1"], FT1, HELD[1], "sel1", sel1, xx_updated, B)
            for p in range(4):
                sp.wait_ge(moe_used, 4 + p + 1)
                sp.dma_start(out[2 * p:2 * p + 2].rearrange("b s d -> s b d"), X[:, 2 * p:2 * p + 2, :])\
                  .then_inc(stored, 16)
            sp.wait_ge(stored, 64)

        @block.tensor
        def _(pe):
            mm, tr = nc.tensor.matmul, nc.tensor.transpose

            def turn_rows(n, src):
                for p in range(4):
                    pe.wait_ge(rows_ready, 8 * n + 2 * p + 2)
                    if p >= 2:
                        pe.wait_ge(cols_ready, 4 * n + p - 1)
                    for t in range(2):
                        for k in range(KB):
                            last = tr(bank(p % 2)[:, (k * 2 + t) * P:(k * 2 + t + 1) * P],
                                      src[:, 2 * p + t, k * P:(k + 1) * P], ident)
                    last.then_inc(turned, 1)

            def key_value():
                pe.wait_ge(ld_ctx, 16)
                pe.wait_ge(ld_w1, 80)
                project_rows(0, CT, wk1)
                for m in range(KB):
                    for half in range(2):
                        for k in range(KB):
                            last = mm(bank(4 + 2 * m + half), wv1[:, k, m * P:(m + 1) * P],
                                      CT[:, k, half * HALF:(half + 1) * HALF], start=(k == 0), stop=(k == 1))
                last.then_inc(vproj_done, 1)
                pe.wait_ge(proj_used, 4)
                pe.wait_ge(vq_ready, 2)
                for k in range(KB):
                    for t in range(B):
                        last = tr(bank16(k)[:, t * P:(t + 1) * P], vq[:, k, t * P:(t + 1) * P], identb[:, :])
                last.then_inc(vT_done, 1)
                pe.wait_ge(vi_ready, 2)

            def project_rows(n, src, w):
                for p in range(4):
                    for t in range(2):
                        for k in range(KB):
                            last = mm(bank(p)[:, t * D:(t + 1) * D],
                                      src[:, k, (2 * p + t) * P:(2 * p + t + 1) * P], w[:, k, :],
                                      start=(k == 0), stop=(k == 1))
                    last.then_inc(proj_done, 1)

            def turn_keys(t, c):
                if c == 0:
                    pe.wait_ge(stack_dve, t + 1)
                    pe.wait_ge(stack_act, t + 1)
                else:
                    pe.wait_ge(side_ready, t * 2 + 1)
                for h in range(8):
                    last = tr(bank16(7)[0:PAIRS * HD, h * P:(h + 1) * P], stack[:, 8 * c + h, :], identb[:, :])
                last.then_inc(keys_turned, 1)

            def turn_queries():
                with pe.Fori(0, B) as t:
                    pe.wait_ge(stack_dve, t + (B + 1))
                    pe.wait_ge(stack_act, t + (B + 1))
                    pe.wait_ge(side_ready, t * 2 + 2 * B)
                    for h in range(H):
                        last = tr(bank16(h // 8)[0:PAIRS * HD, (h % 8) * P:(h % 8 + 1) * P],
                                  stack[:, h, :], identb[:, :])
                    last.then_inc(stack_turned, 1)

            def convolution():
                pe.wait_ge(cols_ready, 4)

                def pair(i):
                    for s in range(2):
                        pe.wait_ge(t_ready, i * 2 + (s + 1))
                        pe.wait_ge(kv0_ready, i * 2 + (s + 1))
                        if not isinstance(i, int):
                            pe.wait_ge(y_used[s], i)
                        mm(bank(2 * s), tslot[:, s, 0:P], kv[:, s, 0, :], start=True, stop=True)
                        mm(bank(2 * s + 1), tslot[:, s, P:D], kv[:, s, 0, :], start=True, stop=False)
                        pe.wait_ge(kv1_ready, i * 2 + (s + 1))
                        mm(bank(2 * s + 1), tslot[:, s, 0:P], kv[:, s, 1, :], start=False, stop=True)\
                            .then_inc(conv_done[s], 1)

                pair(0)
                with pe.Fori(1, H // 2) as i:
                    pair(i)
                for s in range(2):
                    pe.wait_ge(summed[s], H // 2)
                for p in range(4):
                    for b in range(2):
                        for k in range(KB):
                            last = tr(bank(4 + p)[:, (b * KB + k) * P:(b * KB + k + 1) * P],
                                      osum[:, k, 2 * p + b, :], ident)
                    last.then_inc(oturned, 1)

            def qkv(t):
                pe.wait_ge(hs_ready, t + 1)
                pe.wait_ge(qT_ready, t)
                pe.wait_ge(kb_ready, t)
                for k in range(KB):
                    mm(bank(0), hslot[:, k, :], wqkv[:, k, 0:2 * D], start=(k == 0), stop=(k == 1))
                for k in range(KB):
                    last = mm(bank(1)[:, 0:D], hslot[:, k, :], wqkv[:, k, 2 * D:3 * D], start=(k == 0), stop=(k == 1))
                last.then_inc(qkv_done, 1)

            def turn_qk(t):
                pe.wait_ge(roped_ready, t + 1)
                for c in range(4):
                    last = tr(bank(c // 2)[:, (c % 2) * P:(c % 2 + 1) * P], roped[:, c * P:(c + 1) * P], ident)
                last.then_inc(qkT_done, 1)

            def scores(t, g):
                if g == 0:
                    pe.wait_ge(qT_ready, t + 1)
                    pe.wait_ge(kb_ready, t + 1)
                if g >= 2:
                    pe.wait_ge(s_used, t * 4 + (g - 1))
                mm(bank(2 + g % 2), identb[:, :], causal[:, :, :].rearrange("p j c -> p (j c)"),
                   start=True, stop=False)
                mm(bank(2 + g % 2), qT[:, g // 2, :],
                   kblock[:, g // 2, (g % 2) * 4:(g % 2) * 4 + 4, :].rearrange("p j c -> p (j c)"),
                   start=False, stop=True).then_inc(s_done, 1)

            def turn_probs(t, g):
                pe.wait_ge(e_done, t * 4 + (g + 1))
                if g >= 2:
                    pe.wait_ge(pt_ready, t * 4 + (g - 1))
                for j in range(4):
                    last = tr(bank(4 + g % 2)[:, j * P:(j + 1) * P], pr[:, g % 2, j * P:(j + 1) * P], ident)
                last.then_inc(pt_done, 1)

            def values(t, g):
                pe.wait_ge(pt_ready, t * 4 + (g + 1))
                if g == 0:
                    pe.wait_ge(o_ready, t)
                    pe.wait_ge(qkv_used, t * 2 + 2)
                for j in range(4):
                    h = 4 * g + j
                    last = mm(bank(6)[:, h * (HD + 1):(h + 1) * (HD + 1)], pT[:, g % 2, j * P:(j + 1) * P],
                              Vx[:, bass.ds(t, 1), h, :].rearrange("p a d -> p (a d)"), start=True, stop=True)
                last.then_inc(pv_done, 1)

            def attend(t):
                scores(t, 0)
                scores(t, 1)
                turn_probs(t, 0)
                scores(t, 2)
                turn_probs(t, 1)
                values(t, 0)
                scores(t, 3)
                turn_probs(t, 2)
                values(t, 1)
                turn_probs(t, 3)
                values(t, 2)
                values(t, 3)

            def project_out(t):
                pe.wait_ge(o_ready, t + 1)
                pe.wait_ge(u_updated, t)
                for k in range(KB):
                    last = tr(bank(7)[:, k * P:(k + 1) * P], orow[:, k * P:(k + 1) * P], ident)
                last.then_inc(oT_done, 1)
                pe.wait_ge(oT_ready, t + 1)
                for k in range(KB):
                    last = mm(bank(7)[:, D:2 * D], oT[:, k, :], wo[:, k, :], start=(k == 0), stop=(k == 1))
                last.then_inc(wo_done, 1)

            def causal_attention():
                pe.wait_ge(ld_w0, 48)
                pe.wait_ge(x_updated, 4)
                turn_rows(1, U)
                pe.wait_ge(cols_ready, 8)
                qkv(0)
                turn_qk(0)
                with pe.Fori(1, B) as t:
                    qkv(t)
                    attend(t - 1)
                    turn_qk(t)
                    project_out(t - 1)
                attend(B - 1)
                project_out(B - 1)

            def experts(layer, experts_, nft, main, w_router, n_router, sel):
                steps0 = 2 * FT0 * layer
                parts_ = PARTS * (experts_ + 1)
                turn_rows(2 + 2 * layer, L)
                pe.wait_ge(cols_ready, 4 * (3 + 2 * layer))
                for t in range(B):
                    for k in range(KB):
                        last = mm(bank(2)[:, t * n_router:(t + 1) * n_router], HT[:, k, t * P:(t + 1) * P],
                                  w_router[:, k, :], start=(k == 0), stop=(k == 1))
                last.then_inc(router_done, 1)
                pe.wait_ge(comb_ready, layer + 1)
                for t in range(B):
                    last = tr(bank16(3)[0:parts_, t * P:(t + 1) * P], cparts[:, t, 0:parts_], identb[:, :])
                last.then_inc(combT_done, 1)
                pe.wait_ge(combT_ready, layer + 1)
                for n in range(4):
                    last = mm(bank(n), zerob[0:1, 0:P], zerob[0:1, :], start=True, stop=False, skip_group_check=True)
                    if layer == 0 and n < 2:
                        last.then_inc((keys_turned, stack_turned)[n], 1)

                loads0 = HELD[layer]

                def product(to, left, right, n=0, n_of=1):
                    for i, (l, r) in enumerate(((0, 0), (0, 1), (1, 0))):
                        last = mm(to, left[l], right[r], start=(n == 0 and i == 0), stop=(n == n_of - 1 and i == 2))
                    return last

                def wait_used(what, step):
                    if not (isinstance(step, int) and step == 0):
                        pe.wait_ge(what, step)

                def hidden(ft, nth, slot, half):
                    gate_up(ft, nth, slot, half)
                    spread(ft, half)

                def gate_up(ft, nth, slot, half):
                    step = ft * 2 + (steps0 + half)
                    tokens = slice(half * HALF, (half + 1) * HALF)
                    if half == 0:
                        pe.wait_ge(w_split[slot], nth * 4 + (4 * loads0[slot] + 2))
                    wait_used(silu_done, step)
                    columns_ = [[z[:, k, tokens] for z in (HT_hi, HT_lo)] for k in range(KB)]
                    for k in range(KB):
                        last = product(bank(4), [w[:, slot, k * P:(k + 1) * P] for w in (wm_hi, wm_lo)],
                                       columns_[k], k, KB)
                    last.then_inc(gate_done, 1)
                    wait_used(su_done, step)
                    for k in range(KB):
                        last = product(bank(5), [w[:, slot, D + k * P:D + (k + 1) * P] for w in (wm_hi, wm_lo)],
                                       columns_[k], k, KB)
                    last.then_inc(up_done, 1)

                def spread(ft, half):
                    step = ft * 2 + (steps0 + half)
                    tokens = slice(half * HALF, (half + 1) * HALF)
                    wait_used(su_spread, step)
                    selector = sel[:, ft * P:(ft + 1) * P] if isinstance(ft, int) else sel[:, bass.ds(ft * P, P)]
                    mm(bank(6), selector, combT[:, tokens], start=True, stop=True).then_inc(c_done, 1)

                def down(ft, nth, slot, half):
                    step = ft * 2 + (steps0 + half)
                    if half == 0:
                        pe.wait_ge(w_split[slot], nth * 4 + (4 * loads0[slot] + 4))
                    pe.wait_ge(hid_ready, step + 1)
                    for t in range(4):
                        for l, r in ((hid_hi, wm_hi), (hid_hi, wm_lo), (hid_lo, wm_hi)):
                            last = mm(bank(half * 2 + t // 2)[:, (t % 2) * D:(t % 2 + 1) * D],
                                      l[:, half, t * P:(t + 1) * P], r[:, slot, 2 * D:3 * D],
                                      start=False, stop=False, skip_group_check=True)
                    last.then_inc(down_done, 1)

                pe.wait_ge(ht_split, 4 * layer + 2)
                pe.wait_ge(ld_sel, 16 * layer + 16)
                hidden(0, 0, 0, 0)
                pe.wait_ge(ht_split, 4 * layer + 4)
                with pe.Fori(0, main) as i:
                    ft = pe.snap(i * 2)
                    hidden(ft, i, 0, 1)
                    if layer == 0:
                        turn_keys(i, 0)
                    down(ft, i, 0, 0)
                    hidden(ft + 1, i, 1, 0)
                    down(ft, i, 0, 1)
                    if layer == 0:
                        turn_keys(i, 1)
                    hidden(ft + 1, i, 1, 1)
                    down(ft + 1, i, 1, 0)
                    hidden(ft + 2, i + 1, 0, 0)
                    down(ft + 1, i, 1, 1)
                ft = 2 * main
                hidden(ft, main, 0, 1)
                down(ft, main, 0, 0)
                if ft + 1 < nft:
                    hidden(ft + 1, main, 1, 0)
                down(ft, main, 0, 1)
                if ft + 1 < nft:
                    hidden(ft + 1, main, 1, 1)
                    down(ft + 1, main, 1, 0)
                    down(ft + 1, main, 1, 1)

            def cross_attention():
                pe.wait_ge(moe_used, 4)
                turn_rows(3, L)
                pe.wait_ge(cols_ready, 16)
                project_rows(1, HT, wq1)
                pe.wait_ge(proj_used, 8)
                turn_queries()
                pe.wait_ge(side_ready, 4 * B)

                def logits(t, h, cond=True):
                    u = t * H + h
                    if not (isinstance(u, int) and u < 2):
                        pe.wait_ge(x_done, u - 1)
                    for c in range(2):
                        last = mm(bank(2 * (h % 2) + c), QS[:, u, :] if isinstance(u, int) else
                                  QS[:, bass.ds(u, 1), :].rearrange("p a c -> p (a c)"),
                                  KS[:, h, c * HALF:(c + 1) * HALF], start=True, stop=True)
                    last.then_inc(l_done, 1)

                def turn(t, h):
                    u = t * H + h
                    pe.wait_ge(p_ready, u + 1)
                    copied_out(pe, t, h - 2)
                    for c in range(B):
                        last = tr(bank16(4 + h % 2)[:, c * P:(c + 1) * P], pb[:, h % 2, c * P:(c + 1) * P], identb[:, :])
                    last.then_inc(xt_done, 1)

                def weigh(t, h):
                    copied_out(pe, t, h)
                    if h == 0 and not (isinstance(t, int) and t == 0):
                        pe.wait_ge(xoT_ready, t * 2 - 1)
                    if h == 8 and not (isinstance(t, int) and t == 0):
                        pe.wait_ge(xx_updated, t)
                    for c in range(B):
                        last = mm(bank(6 + h // 8)[:, (h % 8) * HD:(h % 8 + 1) * HD], pbT[:, h % 4, c * P:(c + 1) * P],
                                  VI[:, c, h * HD:(h + 1) * HD], start=(c == 0), stop=(c == B - 1))
                    last.then_inc(xv_done, 1)

                def turn_out(t, k):
                    pe.wait_ge(xo_ready, t * 2 + (k + 1))
                    tr(bank(6 + k)[:, P:2 * P], orow[:, k * P:(k + 1) * P], ident).then_inc(xoT_done, 1)

                def project(t):
                    pe.wait_ge(xoT_ready, t * 2 + 2)
                    for k in range(KB):
                        last = mm(bank(7)[:, D:2 * D], oT[:, k, :], wp1[:, k, :], start=(k == 0), stop=(k == 1))
                    last.then_inc(xp_done, 1)

                def step(t, h, first):
                    logits(t, h)
                    if h >= 4:
                        weigh(t, h - 4)
                    elif not first:
                        weigh(t - 1, h - 4 + H)
                    if h == 14:
                        turn_out(t, 0)
                    if h == 6 and not first:
                        turn_out(t - 1, 1)
                    if h == 9 and not first:
                        project(t - 1)
                    if h >= 2:
                        turn(t, h - 2)
                    elif not first:
                        turn(t - 1, h - 2 + H)

                def tile(t, first):
                    for h in range(H):
                        step(t, h, first)

                tile(0, True)
                with pe.Fori(1, B) as t:
                    tile(t, False)
                weigh(B - 1, H - 4)
                turn(B - 1, H - 2)
                weigh(B - 1, H - 3)
                turn(B - 1, H - 1)
                weigh(B - 1, H - 2)
                weigh(B - 1, H - 1)
                turn_out(B - 1, 1)
                project(B - 1)

            pe.wait_ge(ld_const, 80)
            key_value()
            turn_rows(0, L)
            convolution()
            causal_attention()
            pe.wait_ge(u_updated, B)
            experts(0, E0, FT0, MAIN0, wr0, E0 + 1, sel0)
            cross_attention()
            pe.wait_ge(xx_updated, B)
            experts(1, E1, FT1, MAIN1, wr1, 2 * E1, sel1)

        @block.scalar
        def _(act):
            f = nc.scalar.activation
            act.dma_start(consts[:, :], a["consts"]).then_inc(ld_const, 16)
            act.dma_start(rows[:, :], bass.AP(a["rows"].tensor, 0, [[0, P], [1, NROWS]])).then_inc(ld_const, 16)
            act.dma_start(cols[:, :, :], a["cols"]).then_inc(ld_const, 16)
            act.dma_start(identb[:, :], a["identb"]).then_inc(ld_const, 16)
            act.dma_start(causal[:, 0, :], a["causal"]).then_inc(ld_const, 16)

            def root(n, to):
                act.wait_ge(var_ready, n)
                f(to[:, :], rvar[:, :], ACT.Sqrt).then_inc(rstd_ready, 1)

            def columns(n, scale, high=None):
                for p in range(4):
                    act.wait_ge(turned, 4 * n + p + 1)
                    for k in range(KB):
                        last = f(HT[:, k, 2 * p * P:(2 * p + 2) * P], bank(p % 2)[:, k * D:(k + 1) * D], ACT.Copy,
                                 scale=1.0 if scale is None else cols[:, scale, k:k + 1])
                        if high is not None:
                            last = f(high[:, k, 2 * p * P:(2 * p + 2) * P], bank(p % 2)[:, k * D:(k + 1) * D], ACT.Copy,
                                     scale=1.0 if scale is None else cols[:, scale, k:k + 1])
                    last.then_inc(cols_ready, 1)

            def split_high(n):
                act.wait_ge(hi_in, 2 * n + 1)
                f(parts[:, :, 0, :], qd.rearrange("p (t c) -> p t c", t=B), ACT.Copy).then_inc(part_ready, 1)
                act.wait_ge(hi_in, 2 * n + 2)
                f(parts[:, :, 1, :], qr.rearrange("p (t c) -> p t c", t=B), ACT.Copy).then_inc(part_ready, 1)

            def stack_rows(n, t):
                if n == 0:
                    act.wait_ge(keys_turned, t * 2 + 1)
                else:
                    act.wait_ge(stack_turned, t + 1)
                for q, src in zip((3, 4, 5), ((0, 1, 0), (1, 1, 2))[n]):
                    last = f(stack[:, :, q * HD:(q + 1) * HD],
                             parts[:, bass.ds(t, 1), src, :].rearrange("p a (h d) -> p (a h) d", h=H), ACT.Copy)
                last.then_inc(stack_act, 1)

            def keys_out(t, c):
                act.wait_ge(keys_turned, t * 2 + (c + 2))
                f(KS[:, 8 * c:8 * c + 8, bass.ds(t * P, P)],
                  bank16(7)[0:PAIRS * HD, :].rearrange("p (h c) -> p h c", h=8), ACT.Copy).then_inc(side_ready, 1)

            act.wait_ge(vproj_done, 1)
            act.wait_ge(ld_const, 80)
            for m in range(KB):
                for half in range(2):
                    f(vf[:, m, half * HALF:(half + 1) * HALF], bank(4 + 2 * m + half), ACT.Identity,
                      bias=cols[:, 2, m:m + 1]).then_inc(vf_ready, 1)
            split_high(0)
            f(tgate[:, :], row("gates"), ACT.Tanh).then_inc(tgate_ready, 1)

            root(1, rstd)
            columns(0, None)

            def toeplitz(head, s):
                f(tslot[:, s, :], toep[:, head, :] if isinstance(head, int) else
                  toep[:, bass.ds(head, 1), :].rearrange("p a l -> p (a l)"), ACT.Copy).then_inc(t_ready, 1)

            act.wait_ge(toep_ready, 2)
            toeplitz(0, 0)
            toeplitz(1, 1)
            with act.Fori(0, H // 2 - 1) as i:
                for s in range(2):
                    act.wait_ge(conv_done[s], i + 1)
                    toeplitz(i * 2 + (2 + s), s)

            root(2, rstd)
            root(3, rms1)
            columns(1, 0)

            def hcopy(t):
                act.wait_ge(qkv_done, t)
                f(hslot[:, :, :], HT[:, :, t * P:(t + 1) * P] if isinstance(t, int) else
                  HT[:, :, bass.ds(t * P, P)], ACT.Copy).then_inc(hs_ready, 1)

            def expo(t, g):
                act.wait_ge(s_used, t * 4 + (g + 1))
                if g >= 2:
                    act.wait_ge(pt_done, t * 4 + (g - 1))
                f(pr[:, g % 2, :], sc[:, g % 2, :], ACT.Exp, scale=float(SCALE)).then_inc(e_done, 1)

            def probs_out(t, g):
                act.wait_ge(pt_done, t * 4 + (g + 1))
                if g >= 2:
                    act.wait_ge(pv_done, t * 4 + (g - 1))
                f(pT[:, g % 2, :], bank(4 + g % 2), ACT.Copy).then_inc(pt_ready, 1)

            def attend(t):
                expo(t, 0)
                expo(t, 1)
                probs_out(t, 0)
                expo(t, 2)
                probs_out(t, 1)
                expo(t, 3)
                probs_out(t, 2)
                probs_out(t, 3)

            def q_out(t):
                act.wait_ge(qkT_done, t + 1)
                f(qT[:, :, :], bank(0)[:, 0:2 * P].rearrange("p (k c) -> p k c", k=KB), ACT.Copy).then_inc(qT_ready, 1)

            def o_out(t):
                act.wait_ge(oT_done, t + 1)
                f(oT[:, :, :], bank(7)[:, 0:2 * P].rearrange("p (k c) -> p k c", k=KB), ACT.Copy).then_inc(oT_ready, 1)

            act.wait_ge(cols_ready, 8)
            hcopy(0)
            q_out(0)
            with act.Fori(1, B) as t:
                hcopy(t)
                attend(t - 1)
                q_out(t)
                o_out(t - 1)
            attend(B - 1)
            o_out(B - 1)

            def experts(layer, nft, main):
                steps0 = 2 * FT0 * layer
                columns(2 + 2 * layer, None if layer else 1, HT_hi)
                for n in range(2):
                    act.wait_ge(router_in, 2 * layer + n + 1)
                    if layer:
                        o, i = (rb[:, :, :], lg[:, :, E1:2 * E1]) if n == 0 else (rb[:, :, :], ra[:, :, :])
                        f(o, i, ACT.Exp, scale=-1.0 if n == 0 else 1.0).then_inc(router_exp, 1)
                    else:
                        o, i = (one[:, :], lg[:, :, E0]) if n == 0 else (rb[:, :, 0:E0], ra[:, :, 0:E0])
                        f(o, i, ACT.Exp, scale=-1.0 if n == 0 else 1.0).then_inc(router_exp, 1)
                act.wait_ge(combT_done, layer + 1)
                np_ = PARTS * ((E1 if layer else E0) + 1)
                act.wait_ge(zeroed, 1)
                f(combT[0:np_, :], bank16(3)[0:np_, :], ACT.Copy).then_inc(combT_ready, 1)

                with act.Fori(0, main) as i:
                    for s in range(4):
                        act.wait_ge(gate_done, i * 4 + (steps0 + s + 1))
                        f(sg[:, s % 2, :], bank(4), ACT.Silu).then_inc(silu_done, 1)
                        if layer == 0 and s == 0:
                            stack_rows(0, i)
                        if layer == 0 and s >= 2:
                            keys_out(i, s - 2)
                for s in range(4 * main, 2 * nft):
                    act.wait_ge(gate_done, steps0 + s + 1)
                    f(sg[:, s % 2, :], bank(4), ACT.Silu).then_inc(silu_done, 1)

            act.wait_ge(u_updated, B)
            for t in range(B):
                f(sq[:, :], U[:, t, :], ACT.Square, accum_out=var[:, t:t + 1]).then_inc(ms_ready, 1)
                act.wait_ge(ms_ready, t + 1)
            root(4, rstd)
            experts(0, FT0, MAIN0)

            root(5, rstd)
            columns(3, None)
            split_high(1)
            act.wait_ge(part_ready, 6)
            with act.Fori(0, B) as t:
                stack_rows(1, t)

            def soft(t, h):
                u = t * H + h
                act.wait_ge(nb_ready, u + 1)
                if not (isinstance(u, int) and u < 2):
                    act.wait_ge(p_ready, u - 1)
                f(e16[:, h % 2, :], psum[:, 2 * (h % 2):2 * (h % 2) + 2, :].rearrange("p a n -> p (a n)"), ACT.Exp,
                  bias=nbias[:, h % 4:h % 4 + 1],
                  accum_out=SUM[:, u:u + 1] if isinstance(u, int) else SUM[:, bass.ds(u, 1)]).then_inc(x_done, 1)

            def out_of(t, h):
                if h in ON_ACT:
                    u = t * H + h
                    act.wait_ge(xt_done, u + 1)
                    if not (isinstance(u, int) and u < 4):
                        act.wait_ge(xv_done, u - 3)
                    f(pbT[:, h % 4, :], bank16(4 + h % 2), ACT.Copy).then_inc(xt_act, 1)

            def o_scaled(t, k):
                act.wait_ge(xoT_done, t * 2 + (k + 1))
                if k == 0 and not (isinstance(t, int) and t == 0):
                    act.wait_ge(xp_done, t)
                f(oT[:, k, :], bank(6 + k)[:, P:2 * P], ACT.Copy, scale=vs[:, k:k + 1]).then_inc(xoT_ready, 1)

            def tile(t, first):
                for h in range(H):
                    soft(t, h)
                    if h >= 2:
                        out_of(t, h - 2)
                    elif not first:
                        out_of(t - 1, h - 2 + H)
                    if h == 15:
                        o_scaled(t, 0)
                    if h == 7 and not first:
                        o_scaled(t - 1, 1)

            tile(0, True)
            with act.Fori(1, B) as t:
                tile(t, False)
            out_of(B - 1, H - 2)
            out_of(B - 1, H - 1)
            o_scaled(B - 1, 1)
            root(6, rstd)
            experts(1, FT1, MAIN1)

        @block.vector
        def _(dve):
            chain = Chain(dve, dve_step)
            link, tick = chain.link, chain.tick
            tt, ts, stt = nc.vector.tensor_tensor, nc.vector.tensor_scalar, nc.vector.scalar_tensor_tensor
            red, cp = nc.vector.tensor_reduce, nc.vector.tensor_copy

            def normalise(n, root_use, dst):
                for b in range(B):
                    tick(nc.vector.bn_stats(stats[:, b, :], X[:, b, :]))
                chain.rest()
                for b in range(B):
                    tick(nc.vector.bn_aggr(mv[:, b, :], stats[:, b, :]))
                chain.rest()
                link(ts(var[:, :], mv[:, :, 1], LN_EPS, None, ALU.add))
                nc.vector.reciprocal(rvar[:, :], var[:, :]).then_inc(var_ready, 1)
                dve.wait_ge(rstd_ready, root_use)
                for b in range(B):
                    ts(dst[:, b, :], X[:, b, :], mv[:, b, 0:1], rstd[:, b:b + 1], ALU.subtract, ALU.mult)\
                        .then_inc(rows_ready, 1)

            def quantise(n):
                heads = qf.rearrange("p (g d) -> p g d", d=HD)
                link(red(am[:, :], heads, AX.X, ALU.max, apply_absolute_value=True))
                link(ts(qs[:, :], am[:, :], 1.0 / QMAX, 1e-8, ALU.mult, ALU.max))
                link(nc.vector.reciprocal(rqs[:, :], qs[:, :]))
                link(tt(qr.rearrange("p (g d) -> p g d", d=HD), heads, bc(rqs[:, :], HD, 1), ALU.mult))
                link(ts(qr, qr, ROUND, ROUND, ALU.add, ALU.subtract))
                link(ts(qr, qr, QMAX, -QMAX, ALU.min, ALU.max))
                tt(qd.rearrange("p (g d) -> p g d", d=HD), qr.rearrange("p (g d) -> p g d", d=HD),
                   bc(qs[:, :], HD, 1), ALU.mult).then_inc(hi_in, 1)
                dve.wait_ge(part_ready, 3 * n + 1)
                tt(qr.rearrange("p (t c) -> p t c", t=B), qd.rearrange("p (t c) -> p t c", t=B),
                   parts[:, :, 0, :], ALU.subtract).then_inc(hi_in, 1)
                dve.wait_ge(part_ready, 3 * n + 2)
                tt(parts[:, :, 2, :], qr.rearrange("p (t c) -> p t c", t=B), parts[:, :, 1, :], ALU.subtract)\
                    .then_inc(part_ready, 1)

            def stack_rows(n, t):
                if n == 0:
                    dve.wait_ge(keys_turned, t * 2 + 1)
                else:
                    dve.wait_ge(stack_turned, t + 1)
                for q, src in enumerate(((0, 1, 2), (0, 0, 0))[n]):
                    last = cp(stack[:, :, q * HD:(q + 1) * HD],
                              parts[:, bass.ds(t, 1), src, :].rearrange("p a (h d) -> p (a h) d", h=H))
                last.then_inc(stack_dve, 1)

            dve.memset(zerob[:, :], 0.0)
            dve.wait_ge(ld_const, 80)
            for j in range(1, 4):
                cp(causal[:, j, :], causal[:, 0, :])
            for p in range(4):
                dve.wait_ge(proj_done, p + 1)
                tt(qf[:, 2 * p * D:(2 * p + 2) * D].rearrange("p (t c) -> p t c", t=2),
                   bank(p).rearrange("p (t c) -> p t c", t=2), bc(row("bk1"), 2, 0), ALU.add).then_inc(proj_used, 1)
            dve.wait_ge(proj_used, 4)
            quantise(0)
            dve.wait_ge(vf_ready, 4)
            link(red(vam[:, :], vf, AX.X, ALU.max, apply_absolute_value=True))
            link(ts(vs[:, :], vam[:, :], 1.0 / QMAX, 1e-8, ALU.mult, ALU.max))
            link(nc.vector.reciprocal(rvs[:, :], vs[:, :]))
            for m in range(KB):
                tick(ts(vf[:, m, :], vf[:, m, :], rvs[:, m:m + 1], ROUND, ALU.mult, ALU.add))
            chain.rest()
            for m in range(KB):
                tick(ts(vf[:, m, :], vf[:, m, :], ROUND, QMAX, ALU.subtract, ALU.min))
            chain.rest()
            for m in range(KB):
                ts(vq[:, m, :], vf[:, m, :], -QMAX, None, ALU.max).then_inc(vq_ready, 1)
            dve.wait_ge(vT_done, 1)
            for k in range(KB):
                cp(VI[:, :, k * P:(k + 1) * P], bank16(k).rearrange("p (t c) -> p t c", t=B)).then_inc(vi_ready, 1)

            dve.wait_ge(ld_x, 16)
            normalise(0, 1, L)
            dve.wait_ge(cols_ready, 4)

            def ctx_of(k, h8):
                return CT[:, k, :].rearrange("p (b c) -> p b c", b=B)[:, :, bass.ds(h8, CH)]

            def products(h8, s):
                c = ctx_of(0, h8)
                tt(kv[:, s, 0, :].rearrange("p (b i j) -> p b i j", b=B, i=CH), bc(c, CH, 2), bc(c, CH, 1),
                   ALU.mult).then_inc(kv0_ready, 1)

            def query(h8, s, nth):
                if not (isinstance(nth, int) and nth == 0):
                    dve.wait_ge(summed[s], nth)
                for k in range(KB):
                    q = HT[:, k, :].rearrange("p (b c) -> p b c", b=B)[:, :, bass.ds(h8, CH)]
                    last = tt(prod[:, s, k, :].rearrange("p (b i j) -> p b i j", b=B, i=CH),
                              bank(2 * s + k).rearrange("p (b i j) -> p b i j", b=B, i=CH), bc(q, CH, 2), ALU.mult)
                last.then_inc(y_used[s], 1)
                dve.wait_ge(y_used[s], nth + 1)
                for k in range(KB):
                    last = red(osum[:, k, :, :][:, :, bass.ds(h8, CH)],
                               prod[:, s, k, :].rearrange("p (b i j) -> p b j i", b=B, i=CH), AX.X, ALU.add)
                last.then_inc(summed[s], 1)

            products(0, 0)
            products(CH, 1)
            for s in range(2):
                dve.wait_ge(conv_done[s], 1)
                products((2 + s) * CH, s)
                query(s * CH, s, 0)
            with dve.Fori(1, H // 2 - 1) as i:
                for s in range(2):
                    h8 = dve.snap(i * (2 * CH) + s * CH)
                    dve.wait_ge(conv_done[s], i + 1)
                    products(h8 + 2 * CH, s)
                    query(h8, s, i)
            for s in range(2):
                dve.wait_ge(conv_done[s], H // 2)
                query(S - 2 * CH + s * CH, s, H // 2 - 1)
            dve.wait_ge(tgate_ready, 1)
            for p in range(4):
                dve.wait_ge(oturned, p + 1)
                stt(X[:, 2 * p:2 * p + 2, :].rearrange("p t c -> p (t c)"), bank(4 + p), tgate[:, 0:1],
                    X[:, 2 * p:2 * p + 2, :].rearrange("p t c -> p (t c)"), ALU.mult, ALU.add).then_inc(x_updated, 1)
            dve.wait_ge(x_updated, 4)

            normalise(1, 2, U)
            link(tt(var[:, :], mv[:, :, 1], rvar[:, :], ALU.mult))
            link(ts(var[:, :], var[:, :], RMS_EPS, None, ALU.add))
            nc.vector.reciprocal(rvar[:, :], var[:, :]).then_inc(var_ready, 1)
            dve.wait_ge(rstd_ready, 3)

            def qkv_in(t):
                dve.wait_ge(qkv_done, t + 1)
                dve.wait_ge(roped_ready, t)
                r = rms1[:, t:t + 1] if isinstance(t, int) else rms1[:, bass.ds(t, 1)]
                stt(QK[:, :], bank(0), r, row("bqk"), ALU.mult, ALU.add).then_inc(qkv_used, 1)
                v = Vx[:, t, :, 0:HD] if isinstance(t, int) else \
                    Vx[:, bass.ds(t, 1), :, 0:HD].rearrange("p a h d -> p (a h) d")
                stt(v, bank(1)[:, 0:D].rearrange("p (h d) -> p h d", h=H), r,
                    row("bv").rearrange("p (h d) -> p h d", h=H), ALU.mult, ALU.add).then_inc(qkv_used, 1)

            def k_blocks(t):
                dve.wait_ge(qkT_done, t + 1)
                for k in range(KB):
                    last = tt(kblock[:, k, :, :], bc(bank(1)[:, k * P:(k + 1) * P], 8, 0), bc(headmask, P, 1), ALU.mult)
                last.then_inc(kb_ready, 1)

            def shift(t, g):
                dve.wait_ge(s_done, t * 4 + (g + 1))
                link(red(nmax[:, g, :], bank(2 + g % 2).rearrange("p (j c) -> p j c", j=4), AX.X, ALU.max, negate=True))
                if g >= 2:
                    dve.wait_ge(e_done, t * 4 + (g - 1))
                tt(sc[:, g % 2, :].rearrange("p (j c) -> p j c", j=4), bank(2 + g % 2).rearrange("p (j c) -> p j c", j=4),
                   bc(nmax[:, g, :], P, 1), ALU.add).then_inc(s_used, 1)

            def divide(t):
                dve.wait_ge(pv_done, t * 4 + 4)
                acc = bank(6)[:, 0:H * (HD + 1)].rearrange("p (h d) -> p h d", h=H)
                link(nc.vector.reciprocal(rden[:, :], acc[:, :, HD]))
                dve.wait_ge(wo_done, t)
                tt(orow[:, :].rearrange("p (h d) -> p h d", h=H), acc[:, :, 0:HD], bc(rden[:, :], HD, 1), ALU.mult)\
                    .then_inc(o_ready, 1)

            def residual(t):
                dve.wait_ge(wo_done, t + 1)
                u = U[:, t, :] if isinstance(t, int) else U[:, bass.ds(t, 1), :].rearrange("p a c -> p (a c)")
                tt(u, bank(7)[:, D:2 * D], u, ALU.add).then_inc(u_updated, 1)

            link(nc.vector.memset(Vx[:, :, :, HD], 1.0))
            qkv_in(0)
            k_blocks(0)
            with dve.Fori(1, B) as t:
                chain.enter(t - 1, 5)
                qkv_in(t)
                for g in range(4):
                    shift(t - 1, g)
                divide(t - 1)
                k_blocks(t)
                residual(t - 1)
            chain.leave(B - 1)
            for g in range(4):
                shift(B - 1, g)
            divide(B - 1)
            residual(B - 1)

            dve.wait_ge(ms_ready, B)
            link(ts(var[:, :], var[:, :], 1.0 / D, RMS_EPS, ALU.mult, ALU.add))
            nc.vector.reciprocal(rvar[:, :], var[:, :]).then_inc(var_ready, 1)
            dve.wait_ge(rstd_ready, 4)
            for b in range(B):
                ts(L[:, b, :], U[:, b, :], rstd[:, b:b + 1], None, ALU.mult).then_inc(rows_ready, 1)

            def softmax(n, e):
                link(red(top[:, :, 0], ra[:, :, 0:e], AX.X, ALU.max, negate=True))
                tt(ra[:, :, 0:e], ra[:, :, 0:e], bc(top[:, :, 0], e, 1), ALU.add).then_inc(router_in, 1)
                dve.wait_ge(router_exp, 2 * n + 2)
                link(red(top[:, :, 1], rb[:, :, 0:e], AX.X, ALU.add))
                link(nc.vector.reciprocal(top[:, :, 2], top[:, :, 1]))
                link(tt(rc[:, :, 0:e], rb[:, :, 0:e], bc(top[:, :, 2], e, 1), ALU.mult))

            def combine(n, e):
                for b in range(B):
                    tick(nc.vector.max(top[:, b, :], key[:, b, 0:e]))
                chain.rest()
                for b in range(B):
                    tick(nc.vector.max_index(topi[:, b, :], top[:, b, :], key[:, b, 0:e]))
                chain.rest()
                link(cp(topf[:, :, :], topi[:, :, 0:2]))
                for s in range(2):
                    tick(tt((ra, rb)[s][:, :, 0:e], bc(iota[:, 0:e], B, 0), bc(topf[:, :, s], e, 1), ALU.is_equal))
                chain.rest()
                link(tt(ra[:, :, 0:e], ra[:, :, 0:e], rb[:, :, 0:e], ALU.add))
                link(tt(comb[:, :, 0:e], ra[:, :, 0:e], wgt[:, :, 0:e], ALU.mult))
                dst = cparts[:, :, :]
                w = e + 1
                link(cp(dst[:, :, 0:w], comb[:, :, 0:w]))
                link(tt(comb2[:, :, 0:w], comb[:, :, 0:w], dst[:, :, 0:w], ALU.subtract))
                link(cp(dst[:, :, w:2 * w], comb2[:, :, 0:w]))
                tt(dst[:, :, 2 * w:3 * w], comb2[:, :, 0:w], dst[:, :, w:2 * w], ALU.subtract).then_inc(comb_ready, 1)

            def split_columns(layer):
                for p in range(4):
                    dve.wait_ge(cols_ready, 4 * (2 + 2 * layer) + p + 1)
                    two = slice(2 * p * P, (2 * p + 2) * P)
                    tt(HT_lo[:, :, two], HT[:, :, two], HT_hi[:, :, two], ALU.subtract).then_inc(ht_split, 1)

            def experts(layer, nft, main):
                def step(n, half):
                    dve.wait_ge(up_done, n)
                    dve.wait_ge(silu_done, n)
                    tt(su[:, half, :], bank(5), sg[:, half, :], ALU.mult).then_inc(su_done, 1)
                    dve.wait_ge(c_done, n)
                    dve.wait_ge(su_done, n)
                    tt(su[:, half, :], bank(6), su[:, half, :], ALU.mult).then_inc(su_spread, 1)
                    dve.wait_ge(su_spread, n)
                    cp(hid_hi[:, half, :], su[:, half, :]).then_inc(hid_rounded, 1)
                    dve.wait_ge(hid_rounded, n)
                    tt(hid_lo[:, half, :], su[:, half, :], hid_hi[:, half, :], ALU.subtract).then_inc(hid_ready, 1)

                steps0 = 2 * FT0 * layer
                with dve.Fori(0, main) as i:
                    for s in range(4):
                        step(dve.snap(i * 4 + (steps0 + s + 1)), s % 2)
                        if layer == 0 and s == 0:
                            stack_rows(0, i)
                for s in range(4 * main, 2 * nft):
                    step(steps0 + s + 1, s % 2)

            split_columns(0)
            dve.wait_ge(router_done, 1)
            cp(lg[:, :, 0:E0 + 1], bank(2)[:, 0:B * (E0 + 1)].rearrange("p (t e) -> p t e", t=B)).then_inc(router_in, 1)
            dve.wait_ge(router_in, 1)
            link(cp(ra[:, :, 0:E0], lg[:, :, 0:E0]))
            softmax(0, E0)
            link(cp(key[:, :, 0:E0], rc[:, :, 0:E0]))
            link(cp(wgt[:, :, 0:E0], rc[:, :, 0:E0]))
            link(ts(one[:, :], one[:, :], 1.0, None, ALU.add))
            link(nc.vector.reciprocal(comb[:, :, E0], one[:, :]))
            combine(0, E0)
            experts(0, FT0, MAIN0)
            dve.wait_ge(down_done, 2 * FT0)
            for p in range(4):
                pair = slice(2 * p, 2 * p + 2)
                flat = lambda z: z[:, pair, :].rearrange("p t c -> p (t c)")
                link(tt(flat(U), bank(p), flat(U), ALU.add))
                stt(flat(X), flat(U), tgate[:, 1:2], flat(X), ALU.mult, ALU.add).then_inc(moe_used, 1)
            dve.wait_ge(moe_used, 4)

            normalise(2, 5, L)
            link(ts(bq25[:, :], row("bq1"), float(SCALE), None, ALU.mult))
            link(ts(bpt[:, :], row("bp"), tgate[:, 2:3], None, ALU.mult))
            link(tt(X[:, :, :], X[:, :, :], bc(bpt[:, :], B, 0), ALU.add))
            for p in range(4):
                dve.wait_ge(proj_done, 4 + p + 1)
                stt(qf[:, 2 * p * D:(2 * p + 2) * D].rearrange("p (t c) -> p t c", t=2),
                    bank(p).rearrange("p (t c) -> p t c", t=2), float(SCALE), bc(bq25[:, :], 2, 0),
                    ALU.mult, ALU.add).then_inc(proj_used, 1)
            dve.wait_ge(proj_used, 8)
            quantise(1)
            with dve.Fori(0, B) as t:
                stack_rows(1, t)
                dve.wait_ge(stack_turned, t + 2)
                for c in range(2):
                    cp(QS[:, bass.ds(t * H + 8 * c, 8), :],
                       bank16(c)[0:PAIRS * HD, :].rearrange("p (h c) -> p h c", h=8)).then_inc(side_ready, 1)

            def peak(t, h):
                u = t * H + h
                dve.wait_ge(l_done, u + 1)
                red(peaks[:, h % 4:h % 4 + 1], psum[:, 2 * (h % 2):2 * (h % 2) + 2, :].rearrange("p a n -> p (a n)"),
                    AX.X, ALU.max, negate=True).then_inc(peak_found, 1)
                dve.wait_ge(peak_found, u + 1)
                ts(nbias[:, h % 4:h % 4 + 1], peaks[:, h % 4:h % 4 + 1], LN255, None, ALU.add).then_inc(nb_ready, 1)

            def integers(t, h):
                u = t * H + h
                dve.wait_ge(x_done, u + 1)
                if not (isinstance(u, int) and u < 2):
                    dve.wait_ge(xt_done, u - 1)
                cp(pb[:, h % 2, :], e16[:, h % 2, :]).then_inc(p_ready, 1)

            def out_of(t, h):
                if h in ON_DVE:
                    u = t * H + h
                    dve.wait_ge(xt_done, u + 1)
                    if not (isinstance(u, int) and u < 4):
                        dve.wait_ge(xv_done, u - 3)
                    cp(pbT[:, h % 4, :], bank16(4 + h % 2)).then_inc(xt_dve, 1)

            def scale_rows(t, k):
                dve.wait_ge(xv_done, t * H + (8 * k + 8))
                link(nc.vector.reciprocal(rden[:, 8 * k:8 * k + 8], SUM[:, t * H + 8 * k:t * H + 8 * k + 8]
                     if isinstance(t, int) else SUM[:, bass.ds(t * H + 8 * k, 8)]))
                if not (isinstance(t, int) and t == 0):
                    dve.wait_ge(xoT_done, t * 2 + (k - 1))
                tt(orow[:, k * P:(k + 1) * P].rearrange("p (h d) -> p h d", h=8),
                   bank(6 + k)[:, 0:P].rearrange("p (h d) -> p h d", h=8),
                   bc(rden[:, 8 * k:8 * k + 8], HD, 1), ALU.mult).then_inc(xo_ready, 1)

            def add_out(t):
                dve.wait_ge(xp_done, t + 1)
                x = X[:, t, :] if isinstance(t, int) else X[:, bass.ds(t, 1), :].rearrange("p a c -> p (a c)")
                stt(x, bank(7)[:, D:2 * D], tgate[:, 2:3], x, ALU.mult, ALU.add).then_inc(xx_updated, 1)

            def tile(t, first):
                for h in range(H):
                    peak(t, h)
                    if h >= 1:
                        integers(t, h - 1)
                    elif not first:
                        integers(t - 1, H - 1)
                    if h >= 2:
                        out_of(t, h - 2)
                    elif not first:
                        out_of(t - 1, h - 2 + H)
                    if h == 12:
                        scale_rows(t, 0)
                    if h == 4 and not first:
                        scale_rows(t - 1, 1)
                    if h == 10 and not first:
                        add_out(t - 1)

            tile(0, True)
            with dve.Fori(1, B) as t:
                chain.enter(t - 1, 2)
                tile(t, False)
            chain.leave(B - 1)
            integers(B - 1, H - 1)
            out_of(B - 1, H - 2)
            out_of(B - 1, H - 1)
            scale_rows(B - 1, 1)
            add_out(B - 1)
            dve.wait_ge(xx_updated, B)

            normalise(3, 6, L)
            split_columns(1)
            dve.wait_ge(router_done, 2)
            cp(lg[:, :, :], bank(2)[:, 0:B * 2 * E1].rearrange("p (t e) -> p t e", t=B)).then_inc(router_in, 1)
            dve.wait_ge(router_in, 3)
            dve.wait_ge(router_exp, 3)
            link(ts(rb[:, :, :], rb[:, :, :], 1.0, None, ALU.add))
            link(nc.vector.reciprocal(rc[:, :, :], rb[:, :, :]))
            link(tt(rc[:, :, :], rc[:, :, :], lg[:, :, E1:2 * E1], ALU.mult))
            link(tt(rc[:, :, :], rc[:, :, :], lg[:, :, 0:E1], ALU.mult))
            link(ts(rb[:, :, :], rc[:, :, :], -1.0, None, ALU.mult))
            link(tt(ra[:, :, :], rb[:, :, :], rc[:, :, :], ALU.max))
            softmax(1, E1)
            link(tt(key[:, :, :], rc[:, :, :], bc(row("ebias"), B, 0), ALU.add))
            link(tt(wgt[:, :, :], rc[:, :, :], bc(row("escale"), B, 0), ALU.mult))
            link(ts(wgt[:, :, :], wgt[:, :, :], 1.0, None, ALU.add))
            link(nc.vector.memset(comb[:, :, E1], 1.0))
            combine(1, E1)
            experts(1, FT1, MAIN1)
            dve.wait_ge(down_done, 2 * (FT0 + FT1))
            for p in range(4):
                flat = X[:, 2 * p:2 * p + 2, :].rearrange("p t c -> p (t c)")
                stt(flat, bank(p), tgate[:, 3:4], flat, ALU.mult, ALU.add).then_inc(moe_used, 1)

        @block.gpsimd
        def _(pool):
            tt = nc.gpsimd.tensor_tensor
            nc.gpsimd.memset(combT[:, :], 0.0).then_inc(zeroed, 1)
            nc.gpsimd.memset(unit[:, :], 1.0).then_inc(unit_ready, 1)
            pool.wait_ge(ld_const, 80)
            pool.wait_ge(ld_toep, 16 * H)
            tt(diag, bc(antident, H, 0), bc(row("conv_d"), P, 1), ALU.mult).then_inc(toep_ready, 1)
            pool.wait_ge(toep_ready, 1)
            tt(toep[:, :, 0:P], toep[:, :, 0:P], diag, ALU.add).then_inc(toep_ready, 1)
            pool.wait_ge(part_ready, 3)

            def products(h8, s):
                c = CT[:, 1, :].rearrange("p (b c) -> p b c", b=B)[:, :, bass.ds(h8, CH)]
                tt(kv[:, s, 1, :].rearrange("p (b i j) -> p b i j", b=B, i=CH), bc(c, CH, 2), bc(c, CH, 1),
                   ALU.mult).then_inc(kv1_ready, 1)

            products(0, 0)
            products(CH, 1)
            with pool.Fori(0, H // 2 - 1) as i:
                for s in range(2):
                    pool.wait_ge(conv_done[s], i + 1)
                    products(i * (2 * CH) + (2 + s) * CH, s)

            def rope(t):
                heads = lambda z: z.rearrange("p (g d) -> p g d", d=HD)
                half = HD // 2
                pool.wait_ge(qkv_used, t * 2 + 2)
                tt(heads(rope1), heads(QK), bc(cosine, 2 * H, 0), ALU.mult).then_inc(rope_mid, 1)
                for lo, hi in ((0, half), (half, 0)):
                    tt(heads(rope2)[:, :, lo:lo + half], heads(QK)[:, :, hi:hi + half],
                       bc(sine[:, lo:lo + half], 2 * H, 0), ALU.mult).then_inc(rope_mid, 1)
                pool.wait_ge(qkT_done, t)
                pool.wait_ge(rope_mid, t * 3 + 3)
                tt(roped, rope1, rope2, ALU.add).then_inc(roped_ready, 1)

            rope(0)
            with pool.Fori(1, B) as t:
                rope(t)

            def split(nth, slot, first_step, held, step):
                pool.wait_ge(ld_wm[slot], (nth + (held + 1)) * 16)
                for n, columns_, used in ((0, slice(0, 2 * D), up_done), (1, slice(2 * D, 3 * D), down_done)):
                    if not (isinstance(step, int) and step <= first_step):
                        pool.wait_ge(used, step)
                    n_ = columns_.stop - columns_.start
                    tt(wm_hi[:, slot, columns_], wm[:, slot, columns_], bass.AP(unit, 0, [[1, P], [0, n_]]), ALU.mult)\
                        .then_inc(w_split[slot], 1)
                    pool.wait_ge(w_split[slot], nth * 4 + (4 * held + 2 * n + 1))
                    tt(wm_lo[:, slot, columns_], wm[:, slot, columns_], wm_hi[:, slot, columns_], ALU.subtract)\
                        .then_inc(w_split[slot], 1)

            pool.wait_ge(unit_ready, 1)

            def split_experts(layer, nft):
                first = 2 * FT0 * layer
                for slot in range(2):
                    split(0, slot, first, HELD[layer][slot], first)
                with pool.Fori(1, nft // 2) as i:
                    for slot in range(2):
                        split(i, slot, first, HELD[layer][slot], i * 4 + (first + 2 * slot - 2))
                if nft % 2:
                    split(nft // 2, 0, first, HELD[layer][0], first + 2 * (nft - 2))

            split_experts(0, FT0)
            pool.wait_ge(down_done, 2 * FT0)
            split_experts(1, FT1)


def toeplitz_source(kernel):
    return np.concatenate([np.zeros_like(kernel), kernel], axis=1)


def backwards(features):
    return features.reshape(KB, P, -1)[:, ::-1].reshape(D, -1)


def expert_tiles(gate, up, down, nft):
    short = nft * P - gate.shape[1]
    gate, up = (np.pad(w, ((0, 0), (0, short))).reshape(KB, P, nft, P).transpose(2, 1, 0, 3).reshape(nft, P, D)
                for w in (gate, up))
    down = np.pad(down, ((0, short), (0, 0))).reshape(nft, P, D)
    return np.concatenate([gate, up, down], axis=2)


def selector(experts, shared, nft, dtype):
    owner = np.full(nft * P, -1)
    owner[:experts * F + shared] = np.minimum(np.arange(experts * F + shared) // F, experts)
    sel = np.zeros((P, nft * P), dtype)
    for part in range(PARTS):
        for e in range(experts + 1):
            sel[part * (experts + 1) + e] = owner == e
    return sel


def kernel(**z):
    import ml_dtypes
    import concourse.bacc as _bacc
    from concourse import mybir as _mybir
    from concourse.bass_utils import run_bass_kernel_spmd as _run

    z = {k: np.asarray(v) for k, v in z.items()}
    f32, b16 = np.float32, ml_dtypes.bfloat16
    inv = 1.0 / 1000000.0 ** (np.arange(0, HD, 2, dtype=f32) / f32(HD))
    angle = np.arange(S, dtype=f32)[:, None] * inv.astype(f32)[None, :]
    cos, sin = np.cos(angle), np.sin(angle)
    consts = np.concatenate([np.eye(P), cos, cos, -sin, sin, np.tile(np.arange(HD), (P, 1)),
                             np.arange(P)[:, None] // HD == np.arange(8)[None, :], np.eye(P)[::-1]], axis=1).astype(f32)
    flat = lambda w: w.transpose(1, 0, 2).reshape(w.shape[1], -1)
    arrays = {
        "x": z["x"],
        "ctxT": backwards(z["ctx_2048"].reshape(N, D).T),
        "conv": toeplitz_source(z["L0_xattn_ssm_kernel"]),
        "consts": consts,
        "rows": np.concatenate([z["L0_ffn_bq"], z["L0_ffn_bk"], z["L0_ffn_bv"], z["L1_xattn_bq"],
                                z["L1_xattn_bkv"][:D], z["L1_xattn_bp"], z["L1_ffn_extra_scale"],
                                z["L1_ffn_extra_bias"], z["L0_xattn_D"], z["g_xattn"][:1], z["g_ffn"][:1],
                                z["g_xattn"][1:], z["g_ffn"][1:]]),
        "cols": np.stack([z["L0_ffn_w_ln1"], z["L0_ffn_w_ln2"], z["L1_xattn_bkv"][D:]]).reshape(3, KB, P).transpose(2, 0, 1),
        "identb": np.eye(P).astype(b16),
        "causal": np.where(np.tril(np.ones((P, P), bool)), 0.0, -1e30).astype(b16),
        "sel0": selector(E0, SH0, FT0, b16),
        "sel1": selector(E1, SH1, FT1, b16),
        "wqkv": np.concatenate([z["L0_ffn_wq"], z["L0_ffn_wk"], z["L0_ffn_wv"]], axis=1),
        "wo": z["L0_ffn_wo"],
        "wr0": np.concatenate([z["L0_ffn_w_router"], z["L0_ffn_w_sh_eg"]], axis=1),
        "wq1": z["L1_xattn_Wq"],
        "wk1": backwards(z["L1_xattn_Wkv"][:, :D]),
        "wv1": backwards(z["L1_xattn_Wkv"][:, D:]),
        "wp1": z["L1_xattn_Wp"],
        "wr1": np.concatenate([z["L1_ffn_cls_w"].T, z["L1_ffn_gate_w"].T], axis=1),
        "moe0": expert_tiles(np.concatenate([flat(z["L0_ffn_w_gate_e"]), z["L0_ffn_w_sh_gate"]], axis=1),
                             np.concatenate([flat(z["L0_ffn_w_up_e"]), z["L0_ffn_w_sh_up"]], axis=1),
                             np.concatenate([z["L0_ffn_w_down_e"].reshape(-1, D), z["L0_ffn_w_sh_down"]]), FT0),
        "moe1": expert_tiles(np.concatenate([z["L1_ffn_wg"].reshape(-1, D), z["L1_ffn_sg"]]).T,
                             np.concatenate([z["L1_ffn_wu"].reshape(-1, D), z["L1_ffn_su"]]).T,
                             np.concatenate([z["L1_ffn_wd"].transpose(0, 2, 1).reshape(-1, D), z["L1_ffn_sd"].T]),
                             FT1),
    }
    arrays = {k: np.ascontiguousarray(v) for k, v in arrays.items()}
    nc = _bacc.Bacc("TRN2", target_bir_lowering=False, num_devices=1)
    args = {k: nc.dram_tensor(f"in_{k}", v.shape, _mybir.dt.from_np(v.dtype), kind="ExternalInput").ap()
            for k, v in arrays.items()}
    out = nc.dram_tensor("out_0", (B, S, D), _mybir.dt.float32, kind="ExternalOutput").ap()
    build(nc, args, out)
    r = _run(nc, [{f"in_{k}": v for k, v in arrays.items()}], core_ids=[0])
    return r.results[0]["out_0"]
```

```python
from contextlib import ExitStack

import numpy as np

import concourse.bass as bass
from concourse import mybir

ALU = mybir.AluOpType
ACT = mybir.ActivationFunctionType
AX = mybir.AxisListType
F32 = mybir.dt.float32
BF16 = mybir.dt.bfloat16
I16 = mybir.dt.int16
F32R = mybir.dt.float32r
U32 = mybir.dt.uint32

P = 128
B, S, D = 8, 128, 256
N = B * S
KB = D // P
H = 16
HD = D // H
CH = S // H
LN_EPS, RMS_EPS = 1e-5, 1e-6
SCALE = 1.0 / np.sqrt(HD)
ROUND = 1.5 * 2.0 ** 23
QMAX = 127.0
LN255 = float(np.log(255.0))
PARTS = 3
STACK = 96
F = 176
E0, E1 = 8, 14
SH0, SH1 = 704, 352
HALF = 512


def tiles_of(experts, shared):
    return -(-(experts * F + shared) // P)


FT0, FT1 = tiles_of(E0, SH0), tiles_of(E1, SH1)

ROWS = {}
for _name, _n in (("bqk", 2 * D), ("bv", D), ("bq1", D), ("bk1", D), ("bp", D), ("escale", E1),
                  ("ebias", E1), ("conv_d", H), ("gates", 4)):
    ROWS[_name] = (sum(n for _, n in ROWS.values()), _n)
NROWS = sum(n for _, n in ROWS.values())


class Chain:

    def __init__(self, eng, sem):
        self.eng, self.sem, self.count, self.links = eng, sem, 0, 0

    def link(self, ins):
        self.tick(ins)
        self.eng.wait_ge(self.sem, self.count)

    def tick(self, ins):
        ins.then_inc(self.sem, 1)
        self.count = self.count + 1
        self.links += 1

    def rest(self):
        self.eng.wait_ge(self.sem, self.count)

    def enter(self, trip, per):
        self.start, self.per, self.at = self.count, per, self.links
        self.count = self.start + trip * per

    def leave(self, trips):
        assert self.links - self.at == self.per, (self.links - self.at, self.per)
        self.count = self.start + trips * self.per


class Uses:

    def __init__(self):
        self.count = 0

    def next(self):
        self.count += 1
        return self.count


def build(nc, a, out):
    ctx = ExitStack()
    with ctx:
        def sb(name, shape, dt=F32):
            return ctx.enter_context(nc.sbuf_tensor(name, shape, dt))

        def sem(name):
            return ctx.enter_context(nc.semaphore(name))

        psum = ctx.enter_context(nc.psum_tensor("psum", [P, 8, 512], F32))

        def bank(n):
            return psum[:, n, :]

        def bank16(n):
            return psum[:, n, :].bitcast(BF16)

        consts = sb("consts", [P, 2 * P + 2 * HD + HD + 8])
        identb = sb("identb", [P, P], BF16)
        unit = sb("unit", [P, 1])
        causal = sb("causal", [P, 4, P], BF16)
        zerob = sb("zerob", [1, 512], BF16)
        rows = sb("rows", [P, NROWS])
        cols = sb("cols", [P, 3, KB])
        tgate = sb("tgate", [P, 4])
        ident = consts[:, 0:P]
        cosine = consts[:, P:P + HD]
        sine = consts[:, P + HD:P + 2 * HD]
        iota = consts[:, P + 2 * HD:P + 3 * HD]
        headmask = consts[:, P + 3 * HD:P + 3 * HD + 8]
        antident = consts[:, P + 3 * HD + 8:]

        def row(name):
            o, n = ROWS[name]
            return rows[:, o:o + n]

        X = sb("X", [P, B, D])
        L = sb("L", [P, B, D])
        HT = sb("HT", [P, KB, N])
        CT = sb("CT", [P, KB, N])
        stats = sb("stats", [P, B, 6])
        mv = sb("mv", [P, B, 2])
        var = sb("var", [P, B])
        rvar = sb("rvar", [P, B])
        rstd = sb("rstd", [P, B])
        rms1 = sb("rms1", [P, B])

        wqkv = sb("wqkv", [P, KB, 3 * D])
        wo = sb("wo", [P, KB, D])
        wr0 = sb("wr0", [P, KB, E0 + 1])
        wq1 = sb("wq1", [P, KB, D])
        wk1 = sb("wk1", [P, KB, D])
        wv1 = sb("wv1", [P, KB, D])
        wp1 = sb("wp1", [P, KB, D])
        wr1 = sb("wr1", [P, KB, 2 * E1])
        wm = sb("wm", [P, 2, 3 * D])

        hid_hi, hid_lo = sb("hid_hi", [P, 2, HALF], F32R), sb("hid_lo", [P, 2, HALF], F32R)
        HT_hi, HT_lo = sb("HT_hi", [P, KB, N], F32R), sb("HT_lo", [P, KB, N], F32R)
        wm_hi, wm_lo = sb("wm_hi", [P, 2, 3 * D], F32R), sb("wm_lo", [P, 2, 3 * D], F32R)

        area = sb("area", [P, 12288])
        keys = sb("keys", [P, 8192])

        def part(at, n, dt=F32, of=area):
            v = of[:, at:at + n]
            return v if dt == F32 else v.bitcast(dt)

        kf = part(9472, 2048)
        vf = part(7424, 2048).rearrange("p (k n) -> p k n", k=KB)
        vq = part(3712, 1024, BF16).rearrange("p (k n) -> p k n", k=KB)
        kv = part(0, 2048).rearrange("p (s k n) -> p s k n", s=2, k=KB)
        prod = part(2048, 2048).rearrange("p (s k n) -> p s k n", s=2, k=KB)
        tslot = part(4096, 512).rearrange("p (s l) -> p s l", s=2)
        toep = part(0, 4096, of=keys).rearrange("p (h l) -> p h l", h=H)
        osum = part(6144, 2048, of=keys).rearrange("p (k b c) -> p k b c", k=KB, b=B)
        Vx = part(0, B * H * (HD + 1)).rearrange("p (t h d) -> p t h d", t=B, h=H)
        kblock = part(0, 4096, of=keys).rearrange("p (s k j c) -> p s k j c", s=2, k=KB, j=8)
        pT = part(4096, 1024, of=keys).rearrange("p (s n) -> p s n", s=2)
        QK, rope1, rope2, roped = part(2304, 512), part(2816, 512), part(3328, 512), part(3840, 512)
        sc = part(4352, 1024).rearrange("p (s n) -> p s n", s=2)
        pr = part(5120, 1024, of=keys).rearrange("p (s n) -> p s n", s=2)
        U = part(5376, 2048).rearrange("p (t c) -> p t c", t=B)
        sg = part(0, 1024).rearrange("p (s n) -> p s n", s=2)
        su = part(1024, 1024).rearrange("p (s n) -> p s n", s=2)
        sel0, sel1 = part(2048, FT0 * P // 2, BF16), part(2048, FT1 * P // 2, BF16)
        kr, kd = part(3200, D), part(3456, D)
        qi = part(9216, 1024, BF16).rearrange("p (t c) -> p t c", t=B)
        qf, qr = part(4096, 2048), part(6144, 2048)
        qslot = part(10240, H * STACK, BF16).rearrange("p (s h c) -> p s h c", s=2, h=H)
        QS = area[0:STACK, 0:8192].bitcast(BF16).rearrange("p (u c) -> p u c", c=P)
        e16 = part(8192, 1024, I16).rearrange("p (s n) -> p s n", s=2)
        pb = part(9216, 1024, BF16).rearrange("p (s n) -> p s n", s=2)
        pbT = part(10240, 2048, BF16).rearrange("p (s n) -> p s n", s=4)

        hslot = sb("hslot", [P, KB, P])
        qT = sb("qT", [P, 2, KB, P])
        nmax = sb("nmax", [P, 4, 4])
        rden = sb("rden", [P, H])
        orow = sb("orow", [P, D])
        oT = sb("oT", [P, KB, P])
        sq = sb("sq", [P, D])
        lg = sb("lg", [P, B, 2 * E1])
        ra = sb("ra", [P, B, E1])
        rb = sb("rb", [P, B, E1])
        rc = sb("rc", [P, B, E1])
        key = sb("key", [P, B, E1])
        wgt = sb("wgt", [P, B, E1])
        one = sb("one", [P, B])
        top = sb("top", [P, B, 8])
        topi = sb("topi", [P, B, 8], U32)
        topf = sb("topf", [P, B, 2])
        comb = sb("comb", [P, B, E1 + 1])
        comb2 = sb("comb2", [P, B, E1 + 1])
        cparts = sb("cparts", [P, B, PARTS * (E1 + 1)], BF16)
        combT = sb("combT", [P, N], BF16)
        am = sb("am", [P, P])
        qs = sb("qs", [P, P])
        rqs = sb("rqs", [P, P])
        kam, kscale, krscale = sb("kam", [P, H]), sb("kscale", [P, H]), sb("krscale", [P, H])
        stack = sb("stack", [P, H, STACK], BF16)
        KS = keys[0:STACK, :].bitcast(BF16).rearrange("p (h n) -> p h n", h=H)
        vam = sb("vam", [P, KB])
        vs = sb("vs", [P, KB])
        rvs = sb("rvs", [P, KB])
        VI = sb("VI", [P, B, D], BF16)
        bq25 = sb("bq25", [P, D])
        bpt = sb("bpt", [P, D])
        peaks = sb("peaks", [P, 4])
        nbias = sb("nbias", [P, 4])
        SUM = sb("SUM", [P, B * H])

        ld_x, ld_ctx, ld_toep, ld_const = sem("ld_x"), sem("ld_ctx"), sem("ld_toep"), sem("ld_const")
        ld_small = sem("ld_small")
        ld_w0, ld_w1, ld_sel = sem("ld_w0"), sem("ld_w1"), sem("ld_sel")
        ld_wm = [sem("ld_wm0"), sem("ld_wm1")]
        tgate_ready, var_ready, rstd_ready = sem("tgate_ready"), sem("var_ready"), sem("rstd_ready")
        rows_ready, turned, cols_ready = sem("rows_ready"), sem("turned"), sem("cols_ready")
        toep_ready = sem("toep_ready")
        t_ready, kv0_ready, kv1_ready = sem("t_ready"), sem("kv0_ready"), sem("kv1_ready")
        conv_done = [sem("conv_done0"), sem("conv_done1")]
        y_used = [sem("y_used0"), sem("y_used1")]
        summed = [sem("summed0"), sem("summed1")]
        zeroed = sem("zeroed")
        oturned, x_updated = sem("oturned"), sem("x_updated")
        hs_ready, qkv_done, qkv_used = sem("hs_ready"), sem("qkv_done"), sem("qkv_used")
        roped_ready, qkT_done, qT_ready, kb_ready = sem("roped_ready"), sem("qkT_done"), sem("qT_ready"), sem("kb_ready")
        s_done, s_used, e_done = sem("s_done"), sem("s_used"), sem("e_done")
        pt_done, pt_ready, pv_done = sem("pt_done"), sem("pt_ready"), sem("pv_done")
        o_ready, oT_done, oT_ready, wo_done, u_updated = (sem("o_ready"), sem("oT_done"), sem("oT_ready"),
                                                         sem("wo_done"), sem("u_updated"))
        ms_ready = sem("ms_ready")
        router_done, router_exp, router_in = sem("router_done"), sem("router_exp"), sem("router_in")
        comb_ready, combT_done, combT_ready = sem("comb_ready"), sem("combT_done"), sem("combT_ready")
        gate_done, up_done, c_done = sem("gate_done"), sem("up_done"), sem("c_done")
        silu_done, su_done, hid_ready, down_done = sem("silu_done"), sem("su_done"), sem("hid_ready"), sem("down_done")
        unit_ready = sem("unit_ready")
        moe_used, ht_split, su_spread = sem("moe_used"), sem("ht_split"), sem("su_spread")
        hid_rounded = sem("hid_rounded")
        w_split = [sem("w_split0"), sem("w_split1")]
        proj_done, proj_used = sem("proj_done"), sem("proj_used")
        keys_turned = sem("keys_turned")
        vproj_done, vf_ready, vq_ready, vT_done, vi_ready = (sem("vproj_done"), sem("vf_ready"), sem("vq_ready"),
                                                            sem("vT_done"), sem("vi_ready"))
        key_rest, key_rounded = sem("key_rest"), sem("key_rounded")
        keys_stacked, side_ready = sem("keys_stacked"), sem("side_ready")
        qslot_ready, q_turned, q_out, qslot_clear = (sem("qslot_ready"), sem("q_turned"), sem("q_out"),
                                                    sem("qslot_clear"))
        biases_ready, bias_added = sem("biases_ready"), sem("bias_added")
        l_done, nb_ready, x_done, p_ready = sem("l_done"), sem("nb_ready"), sem("x_done"), sem("p_ready")
        xt_done, xt_act, xt_dve, xv_done = sem("xt_done"), sem("xt_act"), sem("xt_dve"), sem("xv_done")
        xo_ready, xoT_done, xoT_ready, xp_done, xx_updated = (sem("xo_ready"), sem("xoT_done"), sem("xoT_ready"),
                                                             sem("xp_done"), sem("xx_updated"))
        peak_found = sem("peak_found")
        dve_step, rope_mid = sem("dve_step"), sem("rope_mid")
        stored = sem("stored")

        block = ctx.enter_context(nc.Block())

        ON_ACT = [h for h in range(H) if h % 8 in (0, 2, 3, 4, 6, 7)]
        ON_DVE = [h for h in range(H) if h not in ON_ACT]
        HELD = ((0, 0), ((FT0 + 1) // 2, FT0 // 2))
        HALVES = (slice(0, B // 2), slice(B // 2, B))
        MAIN0, MAIN1 = (FT0 - 1) // 2, (FT1 - 1) // 2

        def since(t, n):
            return not isinstance(t, int) or t >= n

        def before_end(t):
            return not isinstance(t, int) or t < B

        def bc(ap, n, at):
            dims = [list(d) for d in ap.ap]
            dims.insert(at + 1, [0, n])
            return bass.AP(ap.tensor, ap.offset, dims)

        def copied_out(eng, t, h):
            if h < 0:
                if isinstance(t, int) and t == 0:
                    return
                t, h = t - 1, h + H
            if h in ON_ACT:
                eng.wait_ge(xt_act, t * len(ON_ACT) + (ON_ACT.index(h) + 1))
            else:
                eng.wait_ge(xt_dve, t * len(ON_DVE) + (ON_DVE.index(h) + 1))

        def rope_products(eng, done):
            heads = lambda z: z.rearrange("p (g d) -> p g d", d=HD)
            half = HD // 2
            done(eng.tensor_tensor(heads(rope1), heads(QK), bc(cosine, 2 * H, 0), ALU.mult))
            for lo, hi in ((0, half), (half, 0)):
                done(eng.tensor_tensor(heads(rope2)[:, :, lo:lo + half], heads(QK)[:, :, hi:hi + half],
                                       bc(sine[:, lo:lo + half], 2 * H, 0), ALU.mult))

        @block.sync
        def _(sp):
            sp.dma_start(X[:, :, :], a["x"].rearrange("b s d -> s b d")).then_inc(ld_x, 16)
            sp.dma_start(CT[:, :, :], a["ctxT"].rearrange("(k p) n -> p k n", p=P)).then_inc(ld_ctx, 16)
            sp.dma_start(wk1[:, :, :], a["wk1"].rearrange("(k p) n -> p k n", p=P)).then_inc(ld_ctx, 16)
            for h in range(H):
                sp.dma_start(toep[:, h, :],
                             bass.AP(a["conv"].tensor, h * 2 * D + D - (P - 1), [[1, P], [1, D]])).then_inc(ld_toep, 16)
            for w, name in ((wqkv, "wqkv"), (wo, "wo"), (wr0, "wr0")):
                sp.dma_start(w[:, :, :], a[name].rearrange("(k p) n -> p k n", p=P)).then_inc(ld_w0, 16)
            for w, name in ((wv1, "wv1"), (wq1, "wq1"), (wp1, "wp1"), (wr1, "wr1")):
                sp.dma_start(w[:, :, :], a[name].rearrange("(k p) n -> p k n", p=P)).then_inc(ld_w1, 16)

            def experts(src, nft, before, selectors, dst, free, count):
                def load(ft, slot):
                    if before[slot] + ft // 2:
                        sp.wait_ge(w_split[slot], 4 * (before[slot] + ft // 2))
                    sp.dma_start(wm[:, slot, :], src[ft, :, :]).then_inc(ld_wm[slot], 16)
                for slot in range(2):
                    load(slot, slot)
                sp.wait_ge(free, count)
                sp.dma_start(dst, a[selectors]).then_inc(ld_sel, 16)
                with sp.Fori(0, (nft - 2) // 2) as i:
                    for slot in range(2):
                        sp.wait_ge(w_split[slot], i * 4 + 4 * (before[slot] + 1))
                        sp.dma_start(wm[:, slot, :], src[bass.ds(i * 2 + (2 + slot), 1), :, :]
                                     .rearrange("a p n -> p (a n)")).then_inc(ld_wm[slot], 16)
                if nft % 2:
                    load(nft - 1, 0)

            experts(a["moe0"], FT0, HELD[0], "sel0", sel0, u_updated, B)
            experts(a["moe1"], FT1, HELD[1], "sel1", sel1, xx_updated, B)
            for p in range(4):
                sp.wait_ge(moe_used, 4 + p + 1)
                sp.dma_start(out[2 * p:2 * p + 2].rearrange("b s d -> s b d"), X[:, 2 * p:2 * p + 2, :])\
                  .then_inc(stored, 16)
            sp.wait_ge(stored, 64)

        @block.tensor
        def _(pe):
            mm, tr = nc.tensor.matmul, nc.tensor.transpose

            def turn_rows(n, src, pairs=range(4), after=lambda p: None):
                for p in pairs:
                    pe.wait_ge(rows_ready, 8 * n + 2 * p + 2)
                    if p >= 2:
                        pe.wait_ge(cols_ready, 4 * n + p - 1)
                    for t in range(2):
                        for k in range(KB):
                            last = tr(bank(p % 2)[:, (k * 2 + t) * P:(k * 2 + t + 1) * P],
                                      src[:, 2 * p + t, k * P:(k + 1) * P], ident)
                    last.then_inc(turned, 1)
                    after(p)

            def context():
                pe.wait_ge(ld_ctx, 32)
                for p in range(2):
                    project_rows(p, 2 + p, CT, wk1)
                pe.wait_ge(ld_const, 16)
                turn_rows(0, L)
                for p in range(2, 4):
                    project_rows(p, 4 + p, CT, wk1)
                pe.wait_ge(proj_used, 4)
                pe.wait_ge(cols_ready, 4)

            def values_in(m):
                for half in range(2):
                    for k in range(KB):
                        last = mm(bank(6 - 4 * m + half), wv1[:, k, m * P:(m + 1) * P],
                                  CT[:, k, half * HALF:(half + 1) * HALF], start=(k == 0), stop=(k == 1))
                last.then_inc(vproj_done, 1)

            def turn_values():
                pe.wait_ge(vq_ready, 2)
                for k in range(KB):
                    for t in range(B):
                        last = tr(bank16(k)[:, t * P:(t + 1) * P], vq[:, k, t * P:(t + 1) * P], identb[:, :])
                last.then_inc(vT_done, 1)

            def project_rows(p, to, src, w):
                for t in range(2):
                    for k in range(KB):
                        last = mm(bank(to)[:, t * D:(t + 1) * D],
                                  src[:, k, (2 * p + t) * P:(2 * p + t + 1) * P], w[:, k, :],
                                  start=(k == 0), stop=(k == 1))
                last.then_inc(proj_done, 1)

            def turn_keys(t, c):
                if c == 0:
                    pe.wait_ge(keys_stacked, t + 1)
                else:
                    pe.wait_ge(side_ready, t * 2 + 1)
                for h in range(8):
                    last = tr(bank16(7)[0:STACK, h * P:(h + 1) * P], stack[:, 8 * c + h, :], identb[:, :])
                last.then_inc(keys_turned, 1)

            def turn_queries():
                def pair(i):
                    for s in range(2):
                        pe.wait_ge(qslot_ready, i * 2 + (s + 1))
                        if not isinstance(i, int):
                            pe.wait_ge(q_out, i * 2 + (s - 1))
                        for h in range(H):
                            last = tr(bank16(4 + 2 * s + h // 8)[0:STACK, (h % 8) * P:(h % 8 + 1) * P],
                                      qslot[:, s, h, :], identb[:, :])
                        last.then_inc(q_turned, 1)

                pair(0)
                with pe.Fori(1, B // 2) as i:
                    pair(i)

            def convolution():
                def pair(i):
                    for s in range(2):
                        pe.wait_ge(t_ready, i * 2 + (s + 1))
                        pe.wait_ge(kv0_ready, i * 2 + (s + 1))
                        if not isinstance(i, int):
                            pe.wait_ge(y_used[s], i)
                        mm(bank(2 * s), tslot[:, s, 0:P], kv[:, s, 0, :], start=True, stop=True)
                        mm(bank(2 * s + 1), tslot[:, s, P:D], kv[:, s, 0, :], start=True, stop=False)
                        pe.wait_ge(kv1_ready, i * 2 + (s + 1))
                        mm(bank(2 * s + 1), tslot[:, s, 0:P], kv[:, s, 1, :], start=False, stop=True)\
                            .then_inc(conv_done[s], 1)

                pair(0)
                with pe.Fori(1, H // 2) as i:
                    pair(i)
                pe.wait_ge(ld_w1, 64)
                values_in(0)
                for s in range(2):
                    pe.wait_ge(summed[s], H // 2)
                for p in range(4):
                    if p == 2:
                        pe.wait_ge(vf_ready, 2)
                    for b in range(2):
                        for k in range(KB):
                            last = tr(bank(4 + p)[:, (b * KB + k) * P:(b * KB + k + 1) * P],
                                      osum[:, k, 2 * p + b, :], ident)
                    last.then_inc(oturned, 1)

            def qkv(t):
                pe.wait_ge(hs_ready, t + 1)
                if since(t, 1):
                    pe.wait_ge(qT_ready, t)
                    pe.wait_ge(kb_ready, t)
                for k in range(KB):
                    mm(bank(0), hslot[:, k, :], wqkv[:, k, 0:2 * D], start=(k == 0), stop=(k == 1))
                for k in range(KB):
                    last = mm(bank(1)[:, 0:D], hslot[:, k, :], wqkv[:, k, 2 * D:3 * D], start=(k == 0), stop=(k == 1))
                last.then_inc(qkv_done, 1)

            def turn_qk(t):
                pe.wait_ge(roped_ready, t + 1)
                for c in range(4):
                    last = tr(bank(c // 2)[:, (c % 2) * P:(c % 2 + 1) * P], roped[:, c * P:(c + 1) * P], ident)
                last.then_inc(qkT_done, 1)

            def scores(t, s, g):
                if g == 0:
                    pe.wait_ge(qT_ready, t + 1)
                    pe.wait_ge(kb_ready, t + 1)
                if since(t, 1) or g >= 2:
                    pe.wait_ge(s_used, t * 4 + (g - 1))
                mm(bank(2 + g % 2), identb[:, :], causal[:, :, :].rearrange("p j c -> p (j c)"),
                   start=True, stop=False)
                mm(bank(2 + g % 2), qT[:, s, g // 2, :],
                   kblock[:, s, g // 2, (g % 2) * 4:(g % 2) * 4 + 4, :].rearrange("p j c -> p (j c)"),
                   start=False, stop=True).then_inc(s_done, 1)

            def turn_probs(t, g):
                pe.wait_ge(e_done, t * 4 + (g + 1))
                if since(t, 1) or g >= 2:
                    pe.wait_ge(pt_ready, t * 4 + (g - 1))
                for j in range(4):
                    last = tr(bank(4 + g % 2)[:, j * P:(j + 1) * P], pr[:, g % 2, j * P:(j + 1) * P], ident)
                last.then_inc(pt_done, 1)

            def values(t, g):
                pe.wait_ge(pt_ready, t * 4 + (g + 1))
                if g == 0:
                    pe.wait_ge(qkv_used, t * 2 + 2)
                if g % 2 == 0 and since(t, 1):
                    pe.wait_ge(oT_ready, t * 2 + (g // 2 - 1))
                if g == 3 and since(t, 1):
                    pe.wait_ge(u_updated, t)
                for j in range(4):
                    h = 4 * g + j
                    v = Vx[:, t, h, :] if isinstance(t, int) else \
                        Vx[:, bass.ds(t, 1), h, :].rearrange("p a d -> p (a d)")
                    last = mm(bank(6 + h // 8)[:, (h % 8) * (HD + 1):(h % 8 + 1) * (HD + 1)],
                              pT[:, g % 2, j * P:(j + 1) * P], v, start=True, stop=True)
                last.then_inc(pv_done, 1)

            def turn_out(t, k):
                pe.wait_ge(o_ready, t * 2 + (k + 1))
                tr(bank(6 + k)[:, 0:P], orow[:, k * P:(k + 1) * P], ident).then_inc(oT_done, 1)

            def project_out(t):
                pe.wait_ge(oT_ready, t * 2 + 2)
                if since(t, 1):
                    pe.wait_ge(u_updated, t)
                for k in range(KB):
                    last = mm(bank(7)[:, D:2 * D], oT[:, k, :], wo[:, k, :], start=(k == 0), stop=(k == 1))
                last.then_inc(wo_done, 1)

            def attend(t, s, enters=True):
                for g in range(4):
                    if enters:
                        scores(t, s, g)
                    if g < 2 and since(t, 1):
                        values(t - 1, g + 2)
                    if g >= 2 and enters:
                        values(t, g - 2)
                    if g == 0 and since(t, 2):
                        project_out(t - 2)
                    if g == 1 and since(t, 1):
                        turn_out(t - 1, 0)
                    if g == 1 and before_end(t + 1):
                        turn_qk(t + 1)
                    if g == 2 and before_end(t + 2):
                        qkv(t + 2)
                    if g == 3 and since(t, 1):
                        turn_out(t - 1, 1)
                    if g == 0 and since(t, 1):
                        turn_probs(t - 1, 3)
                    if g >= 1 and enters:
                        turn_probs(t, g - 1)

            def causal_attention():
                pe.wait_ge(ld_small, 64)
                pe.wait_ge(ld_w0, 48)
                values_in(1)
                pe.wait_ge(x_updated, 4)
                turn_rows(1, U)
                pe.wait_ge(cols_ready, 8)
                qkv(0)
                turn_qk(0)
                qkv(1)
                pe.wait_ge(vf_ready, 4)
                for s in range(2):
                    attend(s, s)
                with pe.Fori(1, B // 2 - 1) as i:
                    for s in range(2):
                        attend(pe.snap(i * 2 + s), s)
                for s in range(2):
                    attend(B - 2 + s, s)
                attend(B, 0, enters=False)
                project_out(B - 1)

            def experts(layer, experts_, nft, main, w_router, n_router, sel):
                steps0 = 2 * FT0 * layer
                parts_ = PARTS * (experts_ + 1)

                loads0 = HELD[layer]

                def product(to, left, right, n=0, n_of=1):
                    for i, (l, r) in enumerate(((0, 0), (0, 1), (1, 0))):
                        last = mm(to, left[l], right[r], start=(n == 0 and i == 0), stop=(n == n_of - 1 and i == 2))
                    return last

                def wait_used(what, step):
                    if not (isinstance(step, int) and step == 0):
                        pe.wait_ge(what, step)

                def hidden(ft, nth, slot, half):
                    gate_up(ft, nth, slot, half)
                    spread(ft, half)

                def gate_up(ft, nth, slot, half):
                    step = ft * 2 + (steps0 + half)
                    tokens = slice(half * HALF, (half + 1) * HALF)
                    if half == 0:
                        pe.wait_ge(w_split[slot], nth * 4 + (4 * loads0[slot] + 2))
                    wait_used(silu_done, step)
                    columns_ = [[z[:, k, tokens] for z in (HT_hi, HT_lo)] for k in range(KB)]
                    for k in range(KB):
                        last = product(bank(4), [w[:, slot, k * P:(k + 1) * P] for w in (wm_hi, wm_lo)],
                                       columns_[k], k, KB)
                    last.then_inc(gate_done, 1)
                    wait_used(su_done, step)
                    for k in range(KB):
                        last = product(bank(5), [w[:, slot, D + k * P:D + (k + 1) * P] for w in (wm_hi, wm_lo)],
                                       columns_[k], k, KB)
                    last.then_inc(up_done, 1)

                def spread(ft, half):
                    step = ft * 2 + (steps0 + half)
                    tokens = slice(half * HALF, (half + 1) * HALF)
                    wait_used(su_spread, step)
                    selector = sel[:, ft * P:(ft + 1) * P] if isinstance(ft, int) else sel[:, bass.ds(ft * P, P)]
                    mm(bank(6), selector, combT[:, tokens], start=True, stop=True).then_inc(c_done, 1)

                def down(ft, nth, slot, half):
                    step = ft * 2 + (steps0 + half)
                    if half == 0:
                        pe.wait_ge(w_split[slot], nth * 4 + (4 * loads0[slot] + 4))
                    pe.wait_ge(hid_ready, step + 1)
                    for t in range(4):
                        for l, r in ((hid_hi, wm_hi), (hid_hi, wm_lo), (hid_lo, wm_hi)):
                            last = mm(bank(half * 2 + t // 2)[:, (t % 2) * D:(t % 2 + 1) * D],
                                      l[:, half, t * P:(t + 1) * P], r[:, slot, 2 * D:3 * D],
                                      start=False, stop=False, skip_group_check=True)
                    last.then_inc(down_done, 1)

                def route(p):
                    pe.wait_ge(cols_ready, 4 * (2 + 2 * layer) + p + 1)
                    for t in (2 * p, 2 * p + 1):
                        for k in range(KB):
                            last = mm(bank(2)[:, t * n_router:(t + 1) * n_router], HT[:, k, t * P:(t + 1) * P],
                                      w_router[:, k, :], start=(k == 0), stop=(k == 1))
                    return last

                turn_rows(2 + 2 * layer, L, after=lambda p: route(p - 1) if p else None)
                route(3).then_inc(router_done, 1)
                pe.wait_ge(ht_split, 4 * layer + 2)
                gate_up(0, 0, 0, 0)
                if layer == 0:
                    turn_values()
                    pe.wait_ge(vi_ready, 2)
                pe.wait_ge(comb_ready, layer + 1)
                for t in range(B):
                    last = tr(bank16(3)[0:parts_, t * P:(t + 1) * P], cparts[:, t, 0:parts_], identb[:, :])
                last.then_inc(combT_done, 1)
                pe.wait_ge(combT_ready, layer + 1)
                for n in range(4):
                    last = mm(bank(n), zerob[0:1, 0:P], zerob[0:1, :], start=True, stop=False, skip_group_check=True)
                if layer == 0:
                    last.then_inc(keys_turned, 1)

                pe.wait_ge(ld_sel, 16 * layer + 16)
                spread(0, 0)
                pe.wait_ge(ht_split, 4 * layer + 4)
                def two_tiles(ft, i):
                    keys = layer == 0 and since(i, 1)
                    if keys:
                        turn_keys(i - 1, 0)
                    hidden(ft, i, 0, 1)
                    if keys:
                        turn_keys(i - 1, 1)
                    down(ft, i, 0, 0)
                    hidden(ft + 1, i, 1, 0)
                    down(ft, i, 0, 1)
                    hidden(ft + 1, i, 1, 1)
                    down(ft + 1, i, 1, 0)
                    hidden(ft + 2, i + 1, 0, 0)
                    down(ft + 1, i, 1, 1)

                if layer == 0:
                    two_tiles(0, 0)
                with pe.Fori(1 - layer, main) as i:
                    two_tiles(pe.snap(i * 2), i)
                ft = 2 * main
                if layer == 0:
                    turn_keys(B - 1, 0)
                hidden(ft, main, 0, 1)
                if layer == 0:
                    turn_keys(B - 1, 1)
                down(ft, main, 0, 0)
                if ft + 1 < nft:
                    hidden(ft + 1, main, 1, 0)
                down(ft, main, 0, 1)
                if ft + 1 < nft:
                    hidden(ft + 1, main, 1, 1)
                    down(ft + 1, main, 1, 0)
                    down(ft + 1, main, 1, 1)

            def cross_attention():
                pe.wait_ge(moe_used, 4)
                for half in range(2):
                    two = (2 * half, 2 * half + 1)
                    turn_rows(3, L, two)
                    for p in two:
                        pe.wait_ge(cols_ready, 12 + p + 1)
                        if p >= 2:
                            pe.wait_ge(proj_used, 4 + p - 1)
                        project_rows(p, 2 + p % 2, HT, wq1)
                turn_queries()
                pe.wait_ge(q_out, B)
                pe.wait_ge(side_ready, 2 * B)

                def logits(t, h, cond=True):
                    u = t * H + h
                    if not (isinstance(u, int) and u < 2):
                        pe.wait_ge(x_done, u - 1)
                    for c in range(2):
                        last = mm(bank(2 * (h % 2) + c), QS[:, u, :] if isinstance(u, int) else
                                  QS[:, bass.ds(u, 1), :].rearrange("p a c -> p (a c)"),
                                  KS[:, h, c * HALF:(c + 1) * HALF], start=True, stop=True)
                    last.then_inc(l_done, 1)

                def turn(t, h):
                    u = t * H + h
                    pe.wait_ge(p_ready, u + 1)
                    copied_out(pe, t, h - 2)
                    for c in range(B):
                        last = tr(bank16(4 + h % 2)[:, c * P:(c + 1) * P], pb[:, h % 2, c * P:(c + 1) * P], identb[:, :])
                    last.then_inc(xt_done, 1)

                def weigh(t, h):
                    copied_out(pe, t, h)
                    if h == 0 and not (isinstance(t, int) and t == 0):
                        pe.wait_ge(xoT_ready, t * 2 - 1)
                    if h == 8 and not (isinstance(t, int) and t == 0):
                        pe.wait_ge(xx_updated, t)
                    for c in range(B):
                        last = mm(bank(6 + h // 8)[:, (h % 8) * HD:(h % 8 + 1) * HD], pbT[:, h % 4, c * P:(c + 1) * P],
                                  VI[:, c, h * HD:(h + 1) * HD], start=(c == 0), stop=(c == B - 1))
                    last.then_inc(xv_done, 1)

                def turn_out(t, k):
                    pe.wait_ge(xo_ready, t * 2 + (k + 1))
                    tr(bank(6 + k)[:, P:2 * P], orow[:, k * P:(k + 1) * P], ident).then_inc(xoT_done, 1)

                def project(t):
                    pe.wait_ge(xoT_ready, t * 2 + 2)
                    for k in range(KB):
                        last = mm(bank(7)[:, D:2 * D], oT[:, k, :], wp1[:, k, :], start=(k == 0), stop=(k == 1))
                    last.then_inc(xp_done, 1)

                def step(t, h, first):
                    logits(t, h)
                    if h >= 4:
                        weigh(t, h - 4)
                    elif not first:
                        weigh(t - 1, h - 4 + H)
                    if h == 14:
                        turn_out(t, 0)
                    if h == 6 and not first:
                        turn_out(t - 1, 1)
                    if h == 9 and not first:
                        project(t - 1)
                    if h >= 2:
                        turn(t, h - 2)
                    elif not first:
                        turn(t - 1, h - 2 + H)

                def tile(t, first):
                    for h in range(H):
                        step(t, h, first)

                tile(0, True)
                with pe.Fori(1, B) as t:
                    tile(t, False)
                weigh(B - 1, H - 4)
                turn(B - 1, H - 2)
                weigh(B - 1, H - 3)
                turn(B - 1, H - 1)
                weigh(B - 1, H - 2)
                weigh(B - 1, H - 1)
                turn_out(B - 1, 1)
                project(B - 1)

            context()
            convolution()
            causal_attention()
            pe.wait_ge(u_updated, B)
            experts(0, E0, FT0, MAIN0, wr0, E0 + 1, sel0)
            cross_attention()
            experts(1, E1, FT1, MAIN1, wr1, 2 * E1, sel1)

        @block.scalar
        def _(act):
            f = nc.scalar.activation
            act.dma_start(consts[:, :], a["consts"]).then_inc(ld_const, 16)
            act.dma_start(cols[:, :, :], a["cols"]).then_inc(ld_small, 16)
            act.dma_start(identb[:, :], a["identb"]).then_inc(ld_small, 16)
            act.dma_start(causal[:, 0, :], a["causal"]).then_inc(ld_small, 16)
            act.dma_start(rows[:, :], bass.AP(a["rows"].tensor, 0, [[0, P], [1, NROWS]])).then_inc(ld_small, 16)

            roots = Uses()

            def root(to, tiles=slice(0, B)):
                act.wait_ge(var_ready, roots.next())
                f(to[:, tiles], rvar[:, tiles], ACT.Sqrt).then_inc(rstd_ready, 1)

            def columns(n, scale, high=None, pairs=range(4)):
                for p in pairs:
                    act.wait_ge(turned, 4 * n + p + 1)
                    for k in range(KB):
                        last = f(HT[:, k, 2 * p * P:(2 * p + 2) * P], bank(p % 2)[:, k * D:(k + 1) * D], ACT.Copy,
                                 scale=1.0 if scale is None else cols[:, scale, k:k + 1])
                        if high is not None:
                            last = f(high[:, k, 2 * p * P:(2 * p + 2) * P], bank(p % 2)[:, k * D:(k + 1) * D], ACT.Copy,
                                     scale=1.0 if scale is None else cols[:, scale, k:k + 1])
                    last.then_inc(cols_ready, 1)

            def roots_and_columns(n, scale):
                for half in range(2):
                    root(rstd, HALVES[half])
                    columns(n, scale, None, (2 * half, 2 * half + 1))

            def round_keys(t, n):
                act.wait_ge(key_rest, t * 2 + (n + 1))
                if n == 0:
                    act.wait_ge(keys_turned, t * 2 + 1)
                f(stack[:, :, n * HD:(n + 1) * HD], (kd, kr)[n].rearrange("p (h d) -> p h d", h=H), ACT.Copy)\
                    .then_inc(key_rounded, 1)

            def keys_out(t, c):
                act.wait_ge(keys_turned, t * 2 + (c + 2))
                f(KS[:, 8 * c:8 * c + 8, t * P:(t + 1) * P] if isinstance(t, int) else
                  KS[:, 8 * c:8 * c + 8, bass.ds(t * P, P)],
                  bank16(7)[0:STACK, :].rearrange("p (h c) -> p h c", h=8), ACT.Copy).then_inc(side_ready, 1)

            for half in range(2):
                root(rstd, HALVES[half])
            columns(0, None)
            act.wait_ge(ld_small, 64)
            f(tgate[:, :], row("gates"), ACT.Tanh).then_inc(tgate_ready, 1)

            def toeplitz(head, s):
                f(tslot[:, s, :], toep[:, head, :] if isinstance(head, int) else
                  toep[:, bass.ds(head, 1), :].rearrange("p a l -> p (a l)"), ACT.Copy).then_inc(t_ready, 1)

            act.wait_ge(toep_ready, 2)
            toeplitz(0, 0)
            toeplitz(1, 1)
            act.wait_ge(toep_ready, H)
            with act.Fori(0, H // 2 - 1) as i:
                for s in range(2):
                    act.wait_ge(conv_done[s], i + 1)
                    toeplitz(i * 2 + (2 + s), s)

            def values_out(m):
                act.wait_ge(vproj_done, m + 1)
                for half in range(2):
                    f(vf[:, m, half * HALF:(half + 1) * HALF], bank(6 - 4 * m + half), ACT.Identity,
                      bias=cols[:, 2, m:m + 1]).then_inc(vf_ready, 1)

            values_out(0)
            for half in range(2):
                root(rstd, HALVES[half])
                columns(1, 0, None, (2 * half, 2 * half + 1))
                if half == 0:
                    values_out(1)
            root(rms1)

            def hcopy(t):
                if since(t, 1):
                    act.wait_ge(qkv_done, t)
                f(hslot[:, :, :], HT[:, :, t * P:(t + 1) * P] if isinstance(t, int) else
                  HT[:, :, bass.ds(t * P, P)], ACT.Copy).then_inc(hs_ready, 1)

            def expo(t, g):
                act.wait_ge(s_used, t * 4 + (g + 1))
                if since(t, 1) or g >= 2:
                    act.wait_ge(pt_done, t * 4 + (g - 1))
                f(pr[:, g % 2, :], sc[:, g % 2, :], ACT.Exp, scale=float(SCALE)).then_inc(e_done, 1)

            def probs_out(t, g):
                act.wait_ge(pt_done, t * 4 + (g + 1))
                if since(t, 1) or g >= 2:
                    act.wait_ge(pv_done, t * 4 + (g - 1))
                f(pT[:, g % 2, :], bank(4 + g % 2), ACT.Copy).then_inc(pt_ready, 1)

            def qT_out(t, s):
                act.wait_ge(qkT_done, t + 1)
                if since(t, 2):
                    act.wait_ge(s_done, t * 4 - 4)
                f(qT[:, s, :, :], bank(0)[:, 0:2 * P].rearrange("p (k c) -> p k c", k=KB), ACT.Copy)\
                    .then_inc(qT_ready, 1)

            def o_out(t, k):
                act.wait_ge(oT_done, t * 2 + (k + 1))
                if k == 0 and since(t, 1):
                    act.wait_ge(wo_done, t)
                f(oT[:, k, :], bank(6 + k)[:, 0:P], ACT.Copy).then_inc(oT_ready, 1)

            def squares(t):
                act.wait_ge(u_updated, t + 1)
                if since(t, 1):
                    act.wait_ge(ms_ready, t)
                f(sq[:, :], U[:, t, :] if isinstance(t, int) else U[:, bass.ds(t, 1), :].rearrange("p a c -> p (a c)"),
                  ACT.Square, accum_out=var[:, t:t + 1] if isinstance(t, int) else var[:, bass.ds(t, 1)])\
                    .then_inc(ms_ready, 1)

            def attend(t, s, enters=True):
                for g in range(4):
                    if g == 0 and before_end(t + 2):
                        hcopy(t + 2)
                    if enters:
                        expo(t, g)
                    if g == 1 and since(t, 1):
                        o_out(t - 1, 0)
                    if g == 1 and before_end(t + 1):
                        qT_out(t + 1, 1 - s)
                    if g == 2 and since(t, 2):
                        squares(t - 2)
                    if g == 3 and since(t, 1):
                        o_out(t - 1, 1)
                    if g == 0 and since(t, 1):
                        probs_out(t - 1, 3)
                    if g >= 1 and enters:
                        probs_out(t, g - 1)

            act.wait_ge(cols_ready, 8)
            hcopy(0)
            qT_out(0, 0)
            hcopy(1)
            for s in range(2):
                attend(s, s)
            with act.Fori(1, B // 2 - 1) as i:
                for s in range(2):
                    attend(act.snap(i * 2 + s), s)
            for s in range(2):
                attend(B - 2 + s, s)
            attend(B, 0, enters=False)

            def experts(layer, nft, main):
                steps0 = 2 * FT0 * layer
                if layer == 0:
                    columns(2, 1, HT_hi)
                else:
                    columns(4, None, HT_hi, (0, 1))
                    root(rstd, HALVES[1])
                    columns(4, None, HT_hi, (2, 3))
                for n in range(2):
                    act.wait_ge(router_in, 2 * layer + n + 1)
                    if layer:
                        o, i = (rb[:, :, :], lg[:, :, E1:2 * E1]) if n == 0 else (rb[:, :, :], ra[:, :, :])
                        f(o, i, ACT.Exp, scale=-1.0 if n == 0 else 1.0).then_inc(router_exp, 1)
                    else:
                        o, i = (one[:, :], lg[:, :, E0]) if n == 0 else (rb[:, :, 0:E0], ra[:, :, 0:E0])
                        f(o, i, ACT.Exp, scale=-1.0 if n == 0 else 1.0).then_inc(router_exp, 1)
                if layer == 0:
                    act.wait_ge(vT_done, 1)
                    for k in range(KB):
                        f(VI[:, :, k * P:(k + 1) * P], bank16(k).rearrange("p (t c) -> p t c", t=B), ACT.Copy)\
                            .then_inc(vi_ready, 1)
                act.wait_ge(combT_done, layer + 1)
                np_ = PARTS * ((E1 if layer else E0) + 1)
                act.wait_ge(zeroed, 1)
                f(combT[0:np_, :], bank16(3)[0:np_, :], ACT.Copy).then_inc(combT_ready, 1)


                def silu(done, slot):
                    act.wait_ge(gate_done, done)
                    f(sg[:, slot, :], bank(4), ACT.Silu).then_inc(silu_done, 1)

                def two_tiles(i):
                    for s in range(4):
                        silu(i * 4 + (steps0 + s + 1), s % 2)
                        if layer == 0:
                            if s < 2 and since(i, 1):
                                keys_out(i - 1, s)
                            if s in (1, 2):
                                round_keys(i, s - 1)

                if layer == 0:
                    two_tiles(0)
                with act.Fori(1 - layer, main) as i:
                    two_tiles(i)
                for s in range(4 * main, 2 * nft):
                    silu(steps0 + s + 1, s % 2)
                    if layer == 0:
                        keys_out(B - 1, s - 4 * main)

            squares(B - 1)
            for half in range(2):
                root(rstd, HALVES[half])
            experts(0, FT0, MAIN0)

            roots_and_columns(3, None)
            with act.Fori(0, B // 2) as i:
                for s in range(2):
                    t = i * 2 + s
                    act.wait_ge(q_turned, t + 1)
                    for c in range(2):
                        last = f(QS[:, bass.ds(t * H + 8 * c, 8), :],
                                 bank16(4 + 2 * s + c)[0:STACK, :].rearrange("p (h c) -> p h c", h=8), ACT.Copy)
                    last.then_inc(q_out, 1)

            def soft(t, h):
                u = t * H + h
                act.wait_ge(nb_ready, u + 1)
                if not (isinstance(u, int) and u < 2):
                    act.wait_ge(p_ready, u - 1)
                f(e16[:, h % 2, :], psum[:, 2 * (h % 2):2 * (h % 2) + 2, :].rearrange("p a n -> p (a n)"), ACT.Exp,
                  bias=nbias[:, h % 4:h % 4 + 1], scale=qs[:, u:u + 1] if isinstance(u, int) else qs[:, bass.ds(u, 1)],
                  accum_out=SUM[:, u:u + 1] if isinstance(u, int) else SUM[:, bass.ds(u, 1)]).then_inc(x_done, 1)

            def out_of(t, h):
                if h in ON_ACT:
                    u = t * H + h
                    act.wait_ge(xt_done, u + 1)
                    if not (isinstance(u, int) and u < 4):
                        act.wait_ge(xv_done, u - 3)
                    f(pbT[:, h % 4, :], bank16(4 + h % 2), ACT.Copy).then_inc(xt_act, 1)

            def o_scaled(t, k):
                act.wait_ge(xoT_done, t * 2 + (k + 1))
                if k == 0 and not (isinstance(t, int) and t == 0):
                    act.wait_ge(xp_done, t)
                f(oT[:, k, :], bank(6 + k)[:, P:2 * P], ACT.Copy, scale=vs[:, k:k + 1]).then_inc(xoT_ready, 1)

            def tile(t, first):
                for h in range(H):
                    soft(t, h)
                    if h >= 2:
                        out_of(t, h - 2)
                    elif not first:
                        out_of(t - 1, h - 2 + H)
                    if h == 15:
                        o_scaled(t, 0)
                    if h == 7 and not first:
                        o_scaled(t - 1, 1)

            tile(0, True)
            with act.Fori(1, B) as t:
                tile(t, False)
            out_of(B - 1, H - 2)
            out_of(B - 1, H - 1)
            root(rstd, HALVES[0])
            o_scaled(B - 1, 1)
            experts(1, FT1, MAIN1)

        @block.vector
        def _(dve):
            chain = Chain(dve, dve_step)
            link, tick = chain.link, chain.tick
            tt, ts, stt = nc.vector.tensor_tensor, nc.vector.tensor_scalar, nc.vector.scalar_tensor_tensor
            red, cp = nc.vector.tensor_reduce, nc.vector.tensor_copy

            roots = Uses()

            def statistics(half):
                tiles = HALVES[half]
                for b in range(tiles.start, tiles.stop):
                    tick(nc.vector.bn_stats(stats[:, b, :], X[:, b, :]))
                chain.rest()
                for b in range(tiles.start, tiles.stop):
                    tick(nc.vector.bn_aggr(mv[:, b, :], stats[:, b, :]))
                chain.rest()
                link(ts(var[:, tiles], mv[:, tiles, 1], LN_EPS, None, ALU.add))
                nc.vector.reciprocal(rvar[:, tiles], var[:, tiles]).then_inc(var_ready, 1)

            def normal_rows(half, dst):
                dve.wait_ge(rstd_ready, roots.next())
                for b in range(HALVES[half].start, HALVES[half].stop):
                    ts(dst[:, b, :], X[:, b, :], mv[:, b, 0:1], rstd[:, b:b + 1], ALU.subtract, ALU.mult)\
                        .then_inc(rows_ready, 1)

            def normalise(dst):
                statistics(0)
                statistics(1)
                for half in range(2):
                    normal_rows(half, dst)

            def quantise(g, to, between=()):
                between = iter(between)
                f_ = slice(g.start * HD, g.stop * HD)
                n_ = g.stop - g.start
                heads = qf[:, f_].rearrange("p (g d) -> p g d", d=HD)
                link(red(am[:, g], heads, AX.X, ALU.max, apply_absolute_value=True))
                link(ts(qs[:, g], am[:, g], 1.0 / QMAX, 1e-8, ALU.mult, ALU.max))
                link(nc.vector.reciprocal(rqs[:, g], qs[:, g]))
                next(between, int)()
                link(tt(qr[:, f_].rearrange("p (g d) -> p g d", d=HD), heads, bc(rqs[:, g], HD, 1), ALU.mult))
                next(between, int)()
                link(ts(qr[:, f_], qr[:, f_], ROUND, ROUND, ALU.add, ALU.subtract))
                link(ts(to, qr[:, f_], QMAX, -QMAX, ALU.min, ALU.max))

            def key_step(t, s):
                heads = lambda z: z.rearrange("p (h d) -> p h d", h=H)
                low = lambda n: stack[:, :, n * HD:(n + 1) * HD]
                if s == 0:
                    src = kf[:, bass.ds(t * D, D)]
                    link(red(kam[:, :], heads(src), AX.X, ALU.max, apply_absolute_value=True))
                    link(ts(kscale[:, :], kam[:, :], 1.0 / QMAX, 1e-8, ALU.mult, ALU.max))
                    link(nc.vector.reciprocal(krscale[:, :], kscale[:, :]))
                    link(tt(heads(kr), heads(src), bc(krscale[:, :], HD, 1), ALU.mult))
                elif s == 1:
                    link(ts(kr, kr, ROUND, ROUND, ALU.add, ALU.subtract))
                    link(ts(kr, kr, QMAX, -QMAX, ALU.min, ALU.max))
                    tt(heads(kd), heads(kr), bc(kscale[:, :], HD, 1), ALU.mult).then_inc(key_rest, 1)
                elif s == 2:
                    dve.wait_ge(key_rounded, t * 2 + 1)
                    tt(heads(kr), heads(kd), low(0), ALU.subtract).then_inc(key_rest, 1)
                else:
                    dve.wait_ge(key_rounded, t * 2 + 2)
                    tt(low(2), heads(kr), low(1), ALU.subtract).then_inc(keys_stacked, 1)

            dve.memset(zerob[:, :], 0.0)
            dve.memset(stack[:, :, PARTS * HD:STACK], 0.0)
            dve.wait_ge(ld_x, 16)
            normalise(L)
            dve.wait_ge(ld_small, 64)
            for j in range(1, 4):
                cp(causal[:, j, :], causal[:, 0, :])
            dve.wait_ge(ld_const, 16)
            dve.wait_ge(ld_toep, 16 * H)
            for h in range(H):
                stt(toep[:, h, 0:P], antident, row("conv_d")[:, h:h + 1], toep[:, h, 0:P], ALU.mult, ALU.add)\
                    .then_inc(toep_ready, 1)
            for p in range(4):
                dve.wait_ge(proj_done, p + 1)
                tt(kf[:, 2 * p * D:(2 * p + 2) * D].rearrange("p (t c) -> p t c", t=2),
                   bank((2, 3, 6, 7)[p]).rearrange("p (t c) -> p t c", t=2), bc(row("bk1"), 2, 0), ALU.add)\
                    .then_inc(proj_used, 1)
            dve.wait_ge(cols_ready, 4)

            def query(h8, s, nth):
                if not (isinstance(nth, int) and nth == 0):
                    dve.wait_ge(summed[s], nth)
                for k in range(KB):
                    q = HT[:, k, :].rearrange("p (b c) -> p b c", b=B)[:, :, bass.ds(h8, CH)]
                    last = tt(prod[:, s, k, :].rearrange("p (b i j) -> p b i j", b=B, i=CH),
                              bank(2 * s + k).rearrange("p (b i j) -> p b i j", b=B, i=CH), bc(q, CH, 2), ALU.mult)
                last.then_inc(y_used[s], 1)
                dve.wait_ge(y_used[s], nth + 1)
                for k in range(KB):
                    last = red(osum[:, k, :, :][:, :, bass.ds(h8, CH)],
                               prod[:, s, k, :].rearrange("p (b i j) -> p b j i", b=B, i=CH), AX.X, ALU.add)
                last.then_inc(summed[s], 1)

            for s in range(2):
                dve.wait_ge(conv_done[s], 1)
                query(s * CH, s, 0)
            with dve.Fori(1, H // 2 - 1) as i:
                for s in range(2):
                    h8 = dve.snap(i * (2 * CH) + s * CH)
                    dve.wait_ge(conv_done[s], i + 1)
                    query(h8, s, i)
            for s in range(2):
                dve.wait_ge(conv_done[s], H // 2)
                query(S - 2 * CH + s * CH, s, H // 2 - 1)
            dve.wait_ge(tgate_ready, 1)
            for p in range(4):
                dve.wait_ge(oturned, p + 1)
                stt(X[:, 2 * p:2 * p + 2, :].rearrange("p t c -> p (t c)"), bank(4 + p), tgate[:, 0:1],
                    X[:, 2 * p:2 * p + 2, :].rearrange("p t c -> p (t c)"), ALU.mult, ALU.add).then_inc(x_updated, 1)
            dve.wait_ge(x_updated, 4)

            normalise(U)
            link(tt(var[:, :], mv[:, :, 1], rvar[:, :], ALU.mult))
            link(ts(var[:, :], var[:, :], RMS_EPS, None, ALU.add))
            nc.vector.reciprocal(rvar[:, :], var[:, :]).then_inc(var_ready, 1)
            dve.wait_ge(rstd_ready, roots.next())

            def qkv_in(t):
                dve.wait_ge(qkv_done, t + 1)
                if since(t, 1):
                    dve.wait_ge(roped_ready, t)
                r = rms1[:, t:t + 1] if isinstance(t, int) else rms1[:, bass.ds(t, 1)]
                stt(QK[:, :], bank(0), r, row("bqk"), ALU.mult, ALU.add).then_inc(qkv_used, 1)
                v = Vx[:, t, :, 0:HD] if isinstance(t, int) else \
                    Vx[:, bass.ds(t, 1), :, 0:HD].rearrange("p a h d -> p (a h) d")
                stt(v, bank(1)[:, 0:D].rearrange("p (h d) -> p h d", h=H), r,
                    row("bv").rearrange("p (h d) -> p h d", h=H), ALU.mult, ALU.add).then_inc(qkv_used, 1)

            def rope(t):
                dve.wait_ge(qkv_used, t * 2 + 2)
                if t:
                    dve.wait_ge(qkT_done, t)
                rope_products(nc.vector, tick)
                chain.rest()
                tt(roped, rope1, rope2, ALU.add).then_inc(roped_ready, 1)

            def k_blocks(t, s):
                dve.wait_ge(qkT_done, t + 1)
                if since(t, 2):
                    dve.wait_ge(s_done, t * 4 - 4)
                for k in range(KB):
                    last = tt(kblock[:, s, k, :, :], bc(bank(1)[:, k * P:(k + 1) * P], 8, 0), bc(headmask, P, 1),
                              ALU.mult)
                last.then_inc(kb_ready, 1)

            def shift(t, g):
                dve.wait_ge(s_done, t * 4 + (g + 1))
                link(red(nmax[:, g, :], bank(2 + g % 2).rearrange("p (j c) -> p j c", j=4), AX.X, ALU.max, negate=True))
                if since(t, 1) or g >= 2:
                    dve.wait_ge(e_done, t * 4 + (g - 1))
                tt(sc[:, g % 2, :].rearrange("p (j c) -> p j c", j=4), bank(2 + g % 2).rearrange("p (j c) -> p j c", j=4),
                   bc(nmax[:, g, :], P, 1), ALU.add).then_inc(s_used, 1)

            def divide(t, k):
                dve.wait_ge(pv_done, t * 4 + (2 * k + 2))
                acc = bank(6 + k)[:, 0:8 * (HD + 1)].rearrange("p (h d) -> p h d", h=8)
                link(nc.vector.reciprocal(rden[:, 8 * k:8 * k + 8], acc[:, :, HD]))
                if since(t, 1):
                    dve.wait_ge(oT_done, t * 2 + (k - 1))
                tt(orow[:, k * P:(k + 1) * P].rearrange("p (h d) -> p h d", h=8), acc[:, :, 0:HD],
                   bc(rden[:, 8 * k:8 * k + 8], HD, 1), ALU.mult).then_inc(o_ready, 1)

            def residual(t):
                dve.wait_ge(wo_done, t + 1)
                u = U[:, t, :] if isinstance(t, int) else U[:, bass.ds(t, 1), :].rearrange("p a c -> p (a c)")
                tt(u, bank(7)[:, D:2 * D], u, ALU.add).then_inc(u_updated, 1)

            def value_scales():
                link(red(vam[:, :], vf, AX.X, ALU.max, apply_absolute_value=True))
                link(ts(vs[:, :], vam[:, :], 1.0 / QMAX, 1e-8, ALU.mult, ALU.max))
                link(nc.vector.reciprocal(rvs[:, :], vs[:, :]))
                for m in range(KB):
                    tick(ts(vf[:, m, :], vf[:, m, :], rvs[:, m:m + 1], ROUND, ALU.mult, ALU.add))

            def value_numbers():
                chain.rest()
                for m in range(KB):
                    tick(ts(vf[:, m, :], vf[:, m, :], ROUND, QMAX, ALU.subtract, ALU.min))
                chain.rest()
                for m in range(KB):
                    ts(vq[:, m, :], vf[:, m, :], -QMAX, None, ALU.max).then_inc(vq_ready, 1)

            def attend(t, s, enters=True, between=None):
                for g in range(4):
                    if enters:
                        shift(t, g)
                    if g == 1 and between:
                        between()
                    if g == 0 and since(t, 1):
                        divide(t - 1, 0)
                    if g == 0 and since(t, 2):
                        residual(t - 2)
                    if g == 1 and before_end(t + 1):
                        k_blocks(t + 1, 1 - s)
                    if g == 2 and since(t, 1):
                        divide(t - 1, 1)
                    if g == 3 and before_end(t + 2):
                        qkv_in(t + 2)

            def mean_square(half):
                tiles = HALVES[half]
                dve.wait_ge(ms_ready, tiles.stop)
                link(ts(var[:, tiles], var[:, tiles], 1.0 / D, RMS_EPS, ALU.mult, ALU.add))
                nc.vector.reciprocal(rvar[:, tiles], var[:, tiles]).then_inc(var_ready, 1)

            link(nc.vector.memset(Vx[:, :, :, HD], 1.0))
            qkv_in(0)
            rope(0)
            k_blocks(0, 0)
            qkv_in(1)
            rope(1)
            for s in range(2):
                attend(s, s)
            with dve.Fori(1, B // 2 - 1) as i:
                chain.enter(i - 1, 12)
                for s in range(2):
                    attend(dve.snap(i * 2 + s), s)
            chain.leave(B // 2 - 2)
            for s in range(2):
                attend(B - 2 + s, s)
            mean_square(0)
            dve.wait_ge(vf_ready, 4)
            attend(B, 0, enters=False, between=value_scales)
            value_numbers()
            residual(B - 1)

            mean_square(1)
            for half in range(2):
                dve.wait_ge(rstd_ready, roots.next())
                for b in range(HALVES[half].start, HALVES[half].stop):
                    ts(L[:, b, :], U[:, b, :], rstd[:, b:b + 1], None, ALU.mult).then_inc(rows_ready, 1)

            def softmax(n, e):
                link(red(top[:, :, 0], ra[:, :, 0:e], AX.X, ALU.max, negate=True))
                tt(ra[:, :, 0:e], ra[:, :, 0:e], bc(top[:, :, 0], e, 1), ALU.add).then_inc(router_in, 1)
                dve.wait_ge(router_exp, 2 * n + 2)
                link(red(top[:, :, 1], rb[:, :, 0:e], AX.X, ALU.add))
                link(nc.vector.reciprocal(top[:, :, 2], top[:, :, 1]))
                link(tt(rc[:, :, 0:e], rb[:, :, 0:e], bc(top[:, :, 2], e, 1), ALU.mult))

            def combine(n, e):
                for b in range(B):
                    tick(nc.vector.max(top[:, b, :], key[:, b, 0:e]))
                chain.rest()
                for b in range(B):
                    tick(nc.vector.max_index(topi[:, b, :], top[:, b, :], key[:, b, 0:e]))
                chain.rest()
                link(cp(topf[:, :, :], topi[:, :, 0:2]))
                for s in range(2):
                    tick(tt((ra, rb)[s][:, :, 0:e], bc(iota[:, 0:e], B, 0), bc(topf[:, :, s], e, 1), ALU.is_equal))
                chain.rest()
                link(tt(ra[:, :, 0:e], ra[:, :, 0:e], rb[:, :, 0:e], ALU.add))
                link(tt(comb[:, :, 0:e], ra[:, :, 0:e], wgt[:, :, 0:e], ALU.mult))
                dst = cparts[:, :, :]
                w = e + 1
                link(cp(dst[:, :, 0:w], comb[:, :, 0:w]))
                link(tt(comb2[:, :, 0:w], comb[:, :, 0:w], dst[:, :, 0:w], ALU.subtract))
                link(cp(dst[:, :, w:2 * w], comb2[:, :, 0:w]))
                tt(dst[:, :, 2 * w:3 * w], comb2[:, :, 0:w], dst[:, :, w:2 * w], ALU.subtract).then_inc(comb_ready, 1)

            def split_columns(layer):
                for p in range(4):
                    dve.wait_ge(cols_ready, 4 * (2 + 2 * layer) + p + 1)
                    two = slice(2 * p * P, (2 * p + 2) * P)
                    tt(HT_lo[:, :, two], HT[:, :, two], HT_hi[:, :, two], ALU.subtract).then_inc(ht_split, 1)

            def experts(layer, nft, main):
                def step(n, half):
                    dve.wait_ge(up_done, n)
                    dve.wait_ge(silu_done, n)
                    tt(su[:, half, :], bank(5), sg[:, half, :], ALU.mult).then_inc(su_done, 1)
                    dve.wait_ge(c_done, n)
                    dve.wait_ge(su_done, n)
                    tt(su[:, half, :], bank(6), su[:, half, :], ALU.mult).then_inc(su_spread, 1)
                    dve.wait_ge(su_spread, n)
                    cp(hid_hi[:, half, :], su[:, half, :]).then_inc(hid_rounded, 1)
                    dve.wait_ge(hid_rounded, n)
                    tt(hid_lo[:, half, :], su[:, half, :], hid_hi[:, half, :], ALU.subtract).then_inc(hid_ready, 1)

                steps0 = 2 * FT0 * layer
                with dve.Fori(0, main) as i:
                    if layer == 0:
                        chain.enter(i, 6)
                    for s in range(4):
                        step(dve.snap(i * 4 + (steps0 + s + 1)), s % 2)
                        if layer == 0:
                            key_step(i, s)
                if layer == 0:
                    chain.leave(main)
                for s in range(4 * main, 2 * nft):
                    step(steps0 + s + 1, s % 2)

            split_columns(0)
            dve.wait_ge(router_done, 1)
            cp(lg[:, :, 0:E0 + 1], bank(2)[:, 0:B * (E0 + 1)].rearrange("p (t e) -> p t e", t=B)).then_inc(router_in, 1)
            dve.wait_ge(router_in, 1)
            link(cp(ra[:, :, 0:E0], lg[:, :, 0:E0]))
            softmax(0, E0)
            link(cp(key[:, :, 0:E0], rc[:, :, 0:E0]))
            link(cp(wgt[:, :, 0:E0], rc[:, :, 0:E0]))
            link(ts(one[:, :], one[:, :], 1.0, None, ALU.add))
            link(nc.vector.reciprocal(comb[:, :, E0], one[:, :]))
            combine(0, E0)
            stt(X[:, :, :], U[:, :, :], tgate[:, 1:2], X[:, :, :], ALU.mult, ALU.add).then_inc(x_updated, 1)
            tick(ts(bq25[:, :], row("bq1"), float(SCALE), None, ALU.mult))
            ts(bpt[:, :], row("bp"), tgate[:, 2:3], None, ALU.mult).then_inc(biases_ready, 1)
            experts(0, FT0, MAIN0)

            def add_experts(half, gate, steps):
                dve.wait_ge(down_done, steps - 1 + half)
                for p in (2 * half, 2 * half + 1):
                    flat = X[:, 2 * p:2 * p + 2, :].rearrange("p t c -> p (t c)")
                    stt(flat, bank(p), tgate[:, gate:gate + 1], flat, ALU.mult, ALU.add).then_inc(moe_used, 1)

            dve.wait_ge(x_updated, 5)
            add_experts(0, 1, 2 * FT0)
            dve.wait_ge(moe_used, 2)
            statistics(0)
            add_experts(1, 1, 2 * FT0)
            dve.wait_ge(moe_used, 4)
            normal_rows(0, L)
            statistics(1)
            normal_rows(1, L)
            chain.rest()

            def queries_in(half):
                for p in (2 * half, 2 * half + 1):
                    dve.wait_ge(proj_done, 4 + p + 1)
                    stt(qf[:, 2 * p * D:(2 * p + 2) * D].rearrange("p (t c) -> p t c", t=2),
                        bank(2 + p % 2).rearrange("p (t c) -> p t c", t=2), float(SCALE), bc(bq25[:, :], 2, 0),
                        ALU.mult, ALU.add).then_inc(proj_used, 1)
                dve.wait_ge(proj_used, 4 + 2 * half + 2)

            def quantise_queries(half, between=()):
                quantise(slice(half * B * H // 2, (half + 1) * B * H // 2),
                         qi[:, 4 * half:4 * half + 4, :].rearrange("p t c -> p (t c)"), between)

            def query_in(t, s):
                if since(t, 2):
                    dve.wait_ge(q_turned, t - 1)
                src = qi[:, t, :] if isinstance(t, int) else qi[:, bass.ds(t, 1), :].rearrange("p a c -> p (a c)")
                cp(qslot[:, s, :, 0:PARTS * HD].rearrange("p h (q d) -> p h q d", q=PARTS),
                   bc(src.rearrange("p (h d) -> p h d", h=H), PARTS, 1)).then_inc(qslot_ready, 1)

            queries_in(0)
            quantise_queries(0)
            dve.wait_ge(qslot_clear, 1)
            query_in(0, 0)
            query_in(1, 1)
            queries_in(1)
            quantise_queries(1, (lambda: query_in(2, 0), lambda: query_in(3, 1)))
            for t in range(4, B):
                query_in(t, t % 2)

            def peak(t, h):
                u = t * H + h
                dve.wait_ge(l_done, u + 1)
                red(peaks[:, h % 4:h % 4 + 1], psum[:, 2 * (h % 2):2 * (h % 2) + 2, :].rearrange("p a n -> p (a n)"),
                    AX.X, ALU.max, negate=True).then_inc(peak_found, 1)

            def bias(t, h):
                u = t * H + h
                dve.wait_ge(peak_found, u + 1)
                ts(nbias[:, h % 4:h % 4 + 1], peaks[:, h % 4:h % 4 + 1],
                   qs[:, u:u + 1] if isinstance(u, int) else qs[:, bass.ds(u, 1)], LN255, ALU.mult, ALU.add)\
                    .then_inc(nb_ready, 1)

            def integers(t, h):
                u = t * H + h
                dve.wait_ge(x_done, u + 1)
                if not (isinstance(u, int) and u < 2):
                    dve.wait_ge(xt_done, u - 1)
                cp(pb[:, h % 2, :], e16[:, h % 2, :]).then_inc(p_ready, 1)

            def out_of(t, h):
                if h in ON_DVE:
                    u = t * H + h
                    dve.wait_ge(xt_done, u + 1)
                    if not (isinstance(u, int) and u < 4):
                        dve.wait_ge(xv_done, u - 3)
                    cp(pbT[:, h % 4, :], bank16(4 + h % 2)).then_inc(xt_dve, 1)

            def scale_rows(t, k):
                dve.wait_ge(xv_done, t * H + (8 * k + 8))
                link(nc.vector.reciprocal(rden[:, 8 * k:8 * k + 8], SUM[:, t * H + 8 * k:t * H + 8 * k + 8]
                     if isinstance(t, int) else SUM[:, bass.ds(t * H + 8 * k, 8)]))
                if not (isinstance(t, int) and t == 0):
                    dve.wait_ge(xoT_done, t * 2 + (k - 1))
                tt(orow[:, k * P:(k + 1) * P].rearrange("p (h d) -> p h d", h=8),
                   bank(6 + k)[:, 0:P].rearrange("p (h d) -> p h d", h=8),
                   bc(rden[:, 8 * k:8 * k + 8], HD, 1), ALU.mult).then_inc(xo_ready, 1)

            def add_out(t):
                dve.wait_ge(xp_done, t + 1)
                x = X[:, t, :] if isinstance(t, int) else X[:, bass.ds(t, 1), :].rearrange("p a c -> p (a c)")
                stt(x, bank(7)[:, D:2 * D], tgate[:, 2:3], x, ALU.mult, ALU.add).then_inc(xx_updated, 1)

            def tile(t, first):
                for h in range(H):
                    peak(t, h)
                    if h >= 1:
                        integers(t, h - 1)
                    elif not first:
                        integers(t - 1, H - 1)
                    bias(t, h)
                    if h >= 2:
                        out_of(t, h - 2)
                    elif not first:
                        out_of(t - 1, h - 2 + H)
                    if h == 12:
                        scale_rows(t, 0)
                    if h == 4 and not first:
                        scale_rows(t - 1, 1)
                    if h == 10 and not first:
                        add_out(t - 1)

            tile(0, True)
            dve.wait_ge(bias_added, 1)
            with dve.Fori(1, B) as t:
                chain.enter(t - 1, 2)
                tile(t, False)
            chain.leave(B - 1)
            integers(B - 1, H - 1)
            out_of(B - 1, H - 2)
            out_of(B - 1, H - 1)
            statistics(0)
            scale_rows(B - 1, 1)
            normal_rows(0, L)
            add_out(B - 1)
            dve.wait_ge(xx_updated, B)
            statistics(1)
            normal_rows(1, L)

            split_columns(1)
            dve.wait_ge(router_done, 2)
            cp(lg[:, :, :], bank(2)[:, 0:B * 2 * E1].rearrange("p (t e) -> p t e", t=B)).then_inc(router_in, 1)
            dve.wait_ge(router_in, 3)
            dve.wait_ge(router_exp, 3)
            link(ts(rb[:, :, :], rb[:, :, :], 1.0, None, ALU.add))
            link(nc.vector.reciprocal(rc[:, :, :], rb[:, :, :]))
            link(tt(rc[:, :, :], rc[:, :, :], lg[:, :, E1:2 * E1], ALU.mult))
            link(tt(rc[:, :, :], rc[:, :, :], lg[:, :, 0:E1], ALU.mult))
            link(ts(rb[:, :, :], rc[:, :, :], -1.0, None, ALU.mult))
            link(tt(ra[:, :, :], rb[:, :, :], rc[:, :, :], ALU.max))
            softmax(1, E1)
            link(tt(key[:, :, :], rc[:, :, :], bc(row("ebias"), B, 0), ALU.add))
            link(tt(wgt[:, :, :], rc[:, :, :], bc(row("escale"), B, 0), ALU.mult))
            link(ts(wgt[:, :, :], wgt[:, :, :], 1.0, None, ALU.add))
            link(nc.vector.memset(comb[:, :, E1], 1.0))
            combine(1, E1)
            experts(1, FT1, MAIN1)
            for half in range(2):
                add_experts(half, 3, 2 * (FT0 + FT1))

        @block.gpsimd
        def _(pool):
            tt = nc.gpsimd.tensor_tensor
            nc.gpsimd.memset(combT[:, :], 0.0).then_inc(zeroed, 1)
            nc.gpsimd.memset(unit[:, :], 1.0).then_inc(unit_ready, 1)
            def products(h8, s):
                for k, ready in enumerate((kv0_ready, kv1_ready)):
                    c = CT[:, k, :].rearrange("p (b c) -> p b c", b=B)[:, :, bass.ds(h8, CH)]
                    tt(kv[:, s, k, :].rearrange("p (b i j) -> p b i j", b=B, i=CH), bc(c, CH, 2), bc(c, CH, 1),
                       ALU.mult).then_inc(ready, 1)

            pool.wait_ge(ld_ctx, 32)
            products(0, 0)
            products(CH, 1)
            with pool.Fori(0, H // 2 - 1) as i:
                for s in range(2):
                    pool.wait_ge(conv_done[s], i + 1)
                    products(i * (2 * CH) + (2 + s) * CH, s)

            def rope(t):
                pool.wait_ge(qkv_used, t * 2 + 2)
                pool.wait_ge(qkT_done, t)
                rope_products(nc.gpsimd, lambda ins: ins.then_inc(rope_mid, 1))
                pool.wait_ge(rope_mid, t * 3 - 3)
                tt(roped, rope1, rope2, ALU.add).then_inc(roped_ready, 1)

            with pool.Fori(2, B) as t:
                rope(t)

            def split(nth, slot, first_step, held, step):
                pool.wait_ge(ld_wm[slot], (nth + (held + 1)) * 16)
                for n, columns_, used in ((0, slice(0, 2 * D), up_done), (1, slice(2 * D, 3 * D), down_done)):
                    if not (isinstance(step, int) and step <= first_step):
                        pool.wait_ge(used, step)
                    n_ = columns_.stop - columns_.start
                    tt(wm_hi[:, slot, columns_], wm[:, slot, columns_], bass.AP(unit, 0, [[1, P], [0, n_]]), ALU.mult)\
                        .then_inc(w_split[slot], 1)
                    pool.wait_ge(w_split[slot], nth * 4 + (4 * held + 2 * n + 1))
                    tt(wm_lo[:, slot, columns_], wm[:, slot, columns_], wm_hi[:, slot, columns_], ALU.subtract)\
                        .then_inc(w_split[slot], 1)

            pool.wait_ge(unit_ready, 1)

            def split_experts(layer, nft):
                first = 2 * FT0 * layer
                for slot in range(2):
                    split(0, slot, first, HELD[layer][slot], first)
                with pool.Fori(1, nft // 2) as i:
                    for slot in range(2):
                        split(i, slot, first, HELD[layer][slot], i * 4 + (first + 2 * slot - 2))
                if nft % 2:
                    split(nft // 2, 0, first, HELD[layer][0], first + 2 * (nft - 2))

            split_experts(0, FT0)
            pool.wait_ge(keys_stacked, B)
            nc.gpsimd.memset(qslot[:, :, :, PARTS * HD:STACK], 0.0).then_inc(qslot_clear, 1)
            pool.wait_ge(biases_ready, 1)
            pool.wait_ge(rows_ready, 32)
            tt(X[:, :, :], X[:, :, :], bc(bpt[:, :], B, 0), ALU.add).then_inc(bias_added, 1)
            pool.wait_ge(down_done, 2 * FT0)
            split_experts(1, FT1)


def toeplitz_source(kernel):
    return np.concatenate([np.zeros_like(kernel), kernel], axis=1)


def backwards(features):
    return features.reshape(KB, P, -1)[:, ::-1].reshape(D, -1)


def expert_tiles(gate, up, down, nft):
    short = nft * P - gate.shape[1]
    gate, up = (np.pad(w, ((0, 0), (0, short))).reshape(KB, P, nft, P).transpose(2, 1, 0, 3).reshape(nft, P, D)
                for w in (gate, up))
    down = np.pad(down, ((0, short), (0, 0))).reshape(nft, P, D)
    return np.concatenate([gate, up, down], axis=2)


def selector(experts, shared, nft, dtype):
    owner = np.full(nft * P, -1)
    owner[:experts * F + shared] = np.minimum(np.arange(experts * F + shared) // F, experts)
    sel = np.zeros((P, nft * P), dtype)
    for part in range(PARTS):
        for e in range(experts + 1):
            sel[part * (experts + 1) + e] = owner == e
    return sel


def kernel(**z):
    import ml_dtypes
    import concourse.bacc as _bacc
    from concourse import mybir as _mybir
    from concourse.bass_utils import run_bass_kernel_spmd as _run

    z = {k: np.asarray(v) for k, v in z.items()}
    f32, b16 = np.float32, ml_dtypes.bfloat16
    inv = 1.0 / 1000000.0 ** (np.arange(0, HD, 2, dtype=f32) / f32(HD))
    angle = np.arange(S, dtype=f32)[:, None] * inv.astype(f32)[None, :]
    cos, sin = np.cos(angle), np.sin(angle)
    consts = np.concatenate([np.eye(P), cos, cos, -sin, sin, np.tile(np.arange(HD), (P, 1)),
                             np.arange(P)[:, None] // HD == np.arange(8)[None, :], np.eye(P)[::-1]], axis=1).astype(f32)
    flat = lambda w: w.transpose(1, 0, 2).reshape(w.shape[1], -1)
    arrays = {
        "x": z["x"],
        "ctxT": backwards(z["ctx_2048"].reshape(N, D).T),
        "conv": toeplitz_source(z["L0_xattn_ssm_kernel"]),
        "consts": consts,
        "rows": np.concatenate([z["L0_ffn_bq"], z["L0_ffn_bk"], z["L0_ffn_bv"], z["L1_xattn_bq"],
                                z["L1_xattn_bkv"][:D], z["L1_xattn_bp"], z["L1_ffn_extra_scale"],
                                z["L1_ffn_extra_bias"], z["L0_xattn_D"], z["g_xattn"][:1], z["g_ffn"][:1],
                                z["g_xattn"][1:], z["g_ffn"][1:]]),
        "cols": np.stack([z["L0_ffn_w_ln1"], z["L0_ffn_w_ln2"], z["L1_xattn_bkv"][D:]]).reshape(3, KB, P).transpose(2, 0, 1),
        "identb": np.eye(P).astype(b16),
        "causal": np.where(np.tril(np.ones((P, P), bool)), 0.0, -1e30).astype(b16),
        "sel0": selector(E0, SH0, FT0, b16),
        "sel1": selector(E1, SH1, FT1, b16),
        "wqkv": np.concatenate([z["L0_ffn_wq"], z["L0_ffn_wk"], z["L0_ffn_wv"]], axis=1),
        "wo": z["L0_ffn_wo"],
        "wr0": np.concatenate([z["L0_ffn_w_router"], z["L0_ffn_w_sh_eg"]], axis=1),
        "wq1": z["L1_xattn_Wq"],
        "wk1": backwards(z["L1_xattn_Wkv"][:, :D]),
        "wv1": backwards(z["L1_xattn_Wkv"][:, D:]),
        "wp1": z["L1_xattn_Wp"],
        "wr1": np.concatenate([z["L1_ffn_cls_w"].T, z["L1_ffn_gate_w"].T], axis=1),
        "moe0": expert_tiles(np.concatenate([flat(z["L0_ffn_w_gate_e"]), z["L0_ffn_w_sh_gate"]], axis=1),
                             np.concatenate([flat(z["L0_ffn_w_up_e"]), z["L0_ffn_w_sh_up"]], axis=1),
                             np.concatenate([z["L0_ffn_w_down_e"].reshape(-1, D), z["L0_ffn_w_sh_down"]]), FT0),
        "moe1": expert_tiles(np.concatenate([z["L1_ffn_wg"].reshape(-1, D), z["L1_ffn_sg"]]).T,
                             np.concatenate([z["L1_ffn_wu"].reshape(-1, D), z["L1_ffn_su"]]).T,
                             np.concatenate([z["L1_ffn_wd"].transpose(0, 2, 1).reshape(-1, D), z["L1_ffn_sd"].T]),
                             FT1),
    }
    arrays = {k: np.ascontiguousarray(v) for k, v in arrays.items()}
    nc = _bacc.Bacc("TRN2", target_bir_lowering=False, num_devices=1)
    args = {k: nc.dram_tensor(f"in_{k}", v.shape, _mybir.dt.from_np(v.dtype), kind="ExternalInput").ap()
            for k, v in arrays.items()}
    out = nc.dram_tensor("out_0", (B, S, D), _mybir.dt.float32, kind="ExternalOutput").ap()
    build(nc, args, out)
    r = _run(nc, [{f"in_{k}": v for k, v in arrays.items()}], core_ids=[0])
    return r.results[0]["out_0"]
```
